# Optimizing a Trainium2 kernel written in Bass

```python
import numpy as np
import jax
import jax.numpy as jnp

def _softmax(x, axis=-1):
    return jax.nn.softmax(x, axis=axis)

def _gelu(x):
    return jax.nn.gelu(x, approximate=True)

def _silu(x):
    return jax.nn.silu(x)

def _sigmoid(x):
    return jax.nn.sigmoid(x)

def _layernorm(x, axis=-1, eps=1e-05):
    m = jnp.mean(x, axis=axis, keepdims=True)
    v = jnp.var(x, axis=axis, keepdims=True)
    return (x - m) / jnp.sqrt(v + eps)

def _scatter_add(tgt, idx, src, axis=0):
    return tgt.at[idx].add(src)

def _segment_sum(src, seg, n):
    return jax.ops.segment_sum(src, seg, n)
kernel_name = 'mk_flamingo_gated_d1_seqx_r4_d0d2cd'

def setup_inputs(seed: int=0):
    np.random.seed(seed)
    _w = jnp.asarray

    def _rec_inputs():
        import jax
        import jax.numpy as jnp
        _rk = jax.random.key(seed)
        x = 0.5 + 0.2887 * jax.random.normal(jax.random.fold_in(_rk, 1), (4, 512, 512), jnp.float32)
        _lenS = 512 - jax.random.randint(jax.random.fold_in(_rk, 7), (4,), 0, max(1, 512 // 4) + 1, jnp.int32)
        _lenS2 = 512 - jax.random.randint(jax.random.fold_in(_rk, 8), (4,), 0, max(1, 512 // 4) + 1, jnp.int32)
        _ctx_512P = jax.random.normal(jax.random.fold_in(_rk, 11), (4, 16, 128), jnp.float32)
        _ctx_512c = jax.random.dirichlet(jax.random.fold_in(_rk, 511), 0.3 * jnp.ones((16,), jnp.float32), (4, 512))
        _ctx_512t = jnp.einsum('bsk,bkd->bsd', _ctx_512c, _ctx_512P)
        _ctx_512t = _ctx_512t * jax.lax.rsqrt(jnp.mean(jnp.square(_ctx_512t)) + 1e-12) * 0.953939
        ctx_512 = 7.22013e-05 + 1.00017 * (_ctx_512t + 0.3 * jax.random.normal(jax.random.fold_in(_rk, 611), (4, 512, 128), jnp.float32))
        _g = jax.random.normal(jax.random.fold_in(_rk, 9001), (2, 1), jnp.float32)
        _g = jnp.sign(_g) * jnp.maximum(jnp.abs(_g), 1.0) + (_g == 0) * 1.0
        g_xattn = _g[0]
        g_ffn = _g[1]
        return (x, ctx_512, g_xattn, g_ffn)
    x, ctx_512, g_xattn, g_ffn = _rec_inputs()

    def _L0_xattn_setup():
        import jax, jax.numpy as jnp
        import numpy as np
        P_ASEM = 0.6
        key = jax.random.key(seed)
        k1, k2, k3 = jax.random.split(key, 3)
        B, N, D = (8, 512, 128)
        x = jax.random.normal(k1, (B, N, D), dtype=jnp.float32)
        adj = jax.random.uniform(k2, (B, N, N), dtype=jnp.float32)
        bound = 1.0 / np.sqrt(2 * D)
        W = jax.random.uniform(k3, (1, 2 * D), dtype=jnp.float32, minval=-bound, maxval=bound)
        b = jnp.zeros((1,), dtype=jnp.float32)
        return {'x': x, 'adj': adj, 'W': W, 'b': b}
    _L0_xattn_all = _L0_xattn_setup()
    _L0_xattn_in = {k: v for k, v in _L0_xattn_all.items() if k in ('W', 'b')}
    del _L0_xattn_all

    def _L0_ffn_setup():
        import jax, jax.numpy as jnp
        import numpy as np
        E, K, H, I, GS = (16, 4, 512, 384, 128)
        B, S = (1, 256)
        FP4_LUT = jnp.array([0.0, 0.5, 1.0, 1.5, 2.0, 3.0, 4.0, 6.0, -0.0, -0.5, -1.0, -1.5, -2.0, -3.0, -4.0, -6.0], jnp.float32)

        def dequant_fp4(packed, scales, gs=GS):
            shifts = jnp.arange(8, dtype=jnp.int32) * 4
            codes = packed[..., :, None, :] >> shifts[:, None] & 15
            w = FP4_LUT[codes]
            new_shape = codes.shape[:-3] + (codes.shape[-3] * 8, codes.shape[-1])
            w = w.reshape(new_shape)
            return w * jnp.repeat(scales, gs, axis=-2)

        def swiglu(h):
            g, u = jnp.split(h, 2, axis=-1)
            return jax.nn.silu(g) * u
        key = jax.random.key(seed)
        ks = jax.random.split(key, 10)

        def packed(k, shape):
            return jax.random.randint(k, shape, 0, 2147483647, dtype=jnp.int32)

        def scale(k, shape):
            return 0.01 + 0.04 * jax.random.uniform(k, shape, dtype=jnp.float32)
        return {'hidden': jax.random.normal(ks[0], (B, S, H), jnp.float32), 'gate_w': jax.random.normal(ks[1], (E, H), jnp.float32) * H ** (-0.5), 'gate_up_packed': packed(ks[2], (E, H // 8, 2 * I)), 'gate_up_scales': scale(ks[3], (E, H // GS, 2 * I)), 'down_packed': packed(ks[4], (E, I // 8, H)), 'down_scales': scale(ks[5], (E, I // GS, H)), 'shared_gate_up_packed': packed(ks[6], (H // 8, 2 * I)), 'shared_gate_up_scales': scale(ks[7], (H // GS, 2 * I)), 'shared_down_packed': packed(ks[8], (I // 8, H)), 'shared_down_scales': scale(ks[9], (I // GS, H))}
    _L0_ffn_all = _L0_ffn_setup()
    _L0_ffn_in = {k: v for k, v in _L0_ffn_all.items() if k in ('gate_w', 'gate_up_packed', 'gate_up_scales', 'down_packed', 'down_scales', 'shared_gate_up_packed', 'shared_gate_up_scales', 'shared_down_packed', 'shared_down_scales')}
    del _L0_ffn_all
    return {'x': x, 'ctx_512': ctx_512, 'g_xattn': g_xattn, 'g_ffn': g_ffn, 'L0_xattn_W': _L0_xattn_in['W'], 'L0_xattn_b': _L0_xattn_in['b'], 'L0_ffn_gate_w': _L0_ffn_in['gate_w'], 'L0_ffn_gate_up_packed': _L0_ffn_in['gate_up_packed'], 'L0_ffn_gate_up_scales': _L0_ffn_in['gate_up_scales'], 'L0_ffn_down_packed': _L0_ffn_in['down_packed'], 'L0_ffn_down_scales': _L0_ffn_in['down_scales'], 'L0_ffn_shared_gate_up_packed': _L0_ffn_in['shared_gate_up_packed'], 'L0_ffn_shared_gate_up_scales': _L0_ffn_in['shared_gate_up_scales'], 'L0_ffn_shared_down_packed': _L0_ffn_in['shared_down_packed'], 'L0_ffn_shared_down_scales': _L0_ffn_in['shared_down_scales']}

def reference(x, ctx_512, g_xattn, g_ffn, L0_xattn_W, L0_xattn_b, L0_ffn_gate_w, L0_ffn_gate_up_packed, L0_ffn_gate_up_scales, L0_ffn_down_packed, L0_ffn_down_scales, L0_ffn_shared_gate_up_packed, L0_ffn_shared_gate_up_scales, L0_ffn_shared_down_packed, L0_ffn_shared_down_scales):
    import jax
    import jax.numpy as jnp

    def _L0_xattn_ref(x, adj, W, b):
        import jax, jax.numpy as jnp
        import numpy as np
        P_ASEM = 0.6
        D = x.shape[-1]
        Wi = W[:, :D]
        Wj = W[:, D:]
        si = jnp.einsum('bnd,d->bn', x, Wi[0])
        sj = jnp.einsum('bnd,d->bn', x, Wj[0])
        xij = jax.nn.sigmoid(si[:, :, None] + sj[:, None, :] + b[0])
        return P_ASEM * xij + (1.0 - P_ASEM) * adj

    def _L0_ffn_ref(hidden, gate_w, gate_up_packed, gate_up_scales, down_packed, down_scales, shared_gate_up_packed, shared_gate_up_scales, shared_down_packed, shared_down_scales):
        import jax, jax.numpy as jnp
        import numpy as np
        E, K, H, I, GS = (16, 4, 512, 384, 128)
        B, S = (1, 256)
        FP4_LUT = jnp.array([0.0, 0.5, 1.0, 1.5, 2.0, 3.0, 4.0, 6.0, -0.0, -0.5, -1.0, -1.5, -2.0, -3.0, -4.0, -6.0], jnp.float32)

        def dequant_fp4(packed, scales, gs=GS):
            shifts = jnp.arange(8, dtype=jnp.int32) * 4
            codes = packed[..., :, None, :] >> shifts[:, None] & 15
            w = FP4_LUT[codes]
            new_shape = codes.shape[:-3] + (codes.shape[-3] * 8, codes.shape[-1])
            w = w.reshape(new_shape)
            return w * jnp.repeat(scales, gs, axis=-2)

        def swiglu(h):
            g, u = jnp.split(h, 2, axis=-1)
            return jax.nn.silu(g) * u
        b, s, h = hidden.shape
        x = hidden.reshape(-1, h)
        probs = jax.nn.softmax(x @ gate_w.T, axis=-1)
        vals, idx = jax.lax.top_k(probs, K)
        w = vals / jnp.sum(vals, axis=-1, keepdims=True)
        combine = jnp.einsum('tke,tk->te', jax.nn.one_hot(idx, E, dtype=x.dtype), w)
        w_gu = dequant_fp4(gate_up_packed, gate_up_scales)
        act = swiglu(jnp.einsum('th,ehi->eti', x, w_gu))
        w_d = dequant_fp4(down_packed, down_scales)
        y_e = jnp.einsum('eti,eih->eth', act, w_d)
        out = jnp.einsum('te,eth->th', combine, y_e)
        act_s = swiglu(x @ dequant_fp4(shared_gate_up_packed, shared_gate_up_scales))
        out = out + act_s @ dequant_fp4(shared_down_packed, shared_down_scales)
        return out.reshape(b, s, h)
    x = x + jnp.tanh(g_xattn[0]) * _L0_xattn_ref(ctx_512, _layernorm(x, axis=-1), L0_xattn_W, L0_xattn_b)
    x = x + jnp.tanh(g_ffn[0]) * _L0_ffn_ref(_layernorm(x, axis=-1), L0_ffn_gate_w, L0_ffn_gate_up_packed, L0_ffn_gate_up_scales, L0_ffn_down_packed, L0_ffn_down_scales, L0_ffn_shared_gate_up_packed, L0_ffn_shared_gate_up_scales, L0_ffn_shared_down_packed, L0_ffn_shared_down_scales)
    return x

_drawn_inputs = setup_inputs


def setup_inputs(seed=0):
    import zlib

    import numpy as np

    out = dict(_drawn_inputs(seed))
    spreads = {}
    factors = {}
    for name, (base, spread) in spreads.items():
        noise = np.random.default_rng([zlib.crc32(name.encode()), seed]).standard_normal(out[name].shape)
        drawn = base * np.exp(spread * noise) if base else spread * noise
        out[name] = jnp.asarray(drawn.astype(out[name].dtype))
    for name, factor in factors.items():
        out[name] = (out[name] * factor).astype(out[name].dtype)
    return out
```

```python
import math
from contextlib import ExitStack

import concourse.bass as bass
from concourse import mybir

F32, F16 = mybir.dt.float32, mybir.dt.float16
I32, U16 = mybir.dt.int32, mybir.dt.uint16
ALU = mybir.AluOpType
ACT = mybir.ActivationFunctionType
AX = mybir.AxisListType.X

P = 128
LN_EPS = 1e-5
P_ASEM = 0.6
TOP_K = 4
NIB = 8
NIB_HALF = NIB // 2

X_SCALE = 2.0 ** 4
W_SCALE = 2.0 ** 8
R_SCALE = 2.0 ** 6
CODE_SCALE = 2.0 ** 14
SPLITTER = 2.0 ** 15 + 1


def gated_xattn_moe(nc, x, ctx_512, g_xattn, g_ffn, xattn_w, xattn_b, gate_w, gu_packed, gu_scales,
                    dn_packed, dn_scales, sh_gu_packed, sh_gu_scales, sh_dn_packed, sh_dn_scales, out):
    B, S, H = x.shape
    D = ctx_512.shape[2]
    E = gu_packed.shape[0]
    GU = gu_packed.shape[2]
    I = GU // 2
    NT = B * S // P
    TB = S // P
    HC = H // P
    IC = I // P
    GR = H // NIB
    G_GU = gu_scales.shape[1]
    RG = P // NIB
    NE = E + 1
    T = B * S
    ROW = H + E
    KMAX = T // P
    SLOTS = T * TOP_K // P + E
    DUMP = T
    assert D == P and H // G_GU == P and I // dn_scales.shape[1] == P and 2 * GR == P

    x_t = x.rearrange("b (i p) h -> b p i h", p=P)
    out_t = out[0:T].rearrange("(b i p) h -> b p i h", b=B, p=P)
    ctx_t = ctx_512.rearrange("b (i p) d -> b p i d", p=P)

    gu_s_dram = nc.dram_tensor("gu_scale_halves", (2, NE, G_GU, GU), F16, kind="Internal").ap()
    rows_dram = nc.dram_tensor("token_rows", (T + P, ROW), F32, kind="Internal").ap()
    dn_s_dram = nc.dram_tensor("dn_scale_halves", (2, NE, IC, H), F16, kind="Internal").ap()

    with ExitStack() as ctx:
        def sb(name, shape, dt):
            return ctx.enter_context(nc.sbuf_tensor(name, shape, dt))

        def psum(name, shape, dt):
            return ctx.enter_context(nc.psum_tensor(name, shape, dt))

        def sem(name):
            return ctx.enter_context(nc.semaphore(name))

        X = sb("X", [P, NT, H], F32)
        xT = sb("xT", [P, NT, 2, HC, P], F16)
        wgu = sb("wgu", [P, 2, 2, HC, GU], F16)
        wdn = sb("wdn", [P, 2, 2, IC, H], F16)
        gu_raw = sb("gu_raw", [P, 2, GU], I32)
        dn_raw = sb("dn_raw", [P, 2, IC, H], I32)
        gu_sc = sb("gu_sc", [P, 2, 2, GU], F16)
        dn_sc = sb("dn_sc", [P, 2, 2, IC, H], F16)
        gu_half = sb("gu_half", [P, GU], U16)
        dq_sign = sb("dq_sign", [P, GU], U16)
        dq_mag = sb("dq_mag", [P, GU], U16)
        dq_code = sb("dq_code", [P, GU], F16)
        dn_bits = sb("dn_bits", [P, H], I32)
        dn_code = sb("dn_code", [P, H], F16)
        dn_shift = sb("dn_shift", [P, 1], I32)
        sg = sb("sg", [P, 2, I], F32)
        act = sb("act", [P, 2, I], F32)
        acth = sb("acth", [P, 2, 2, I], F16)
        aT = sb("aT", [P, 2, 2, IC, P], F16)
        id16 = sb("id16", [P, P], F16)
        id32 = sb("id32", [P, P], F32)
        room_a = sb("room_a", [P, NT * D], F32)
        ctxs = room_a[:, :].rearrange("p (i d) -> p i d", d=D)
        room_b = sb("room_b", [P, B * S], F32)
        ctxT = room_b[:, :].rearrange("p (b s) -> p b s", b=B)
        wij = sb("wij", [P, 2], F32)
        wj_all = sb("wj_all", [P, P], F32)
        ones = sb("ones", [P, P], F32)
        bias = sb("bias", [P, 1], F32)
        gates = sb("gates", [P, 2], F32)
        tg = sb("tg", [P, 4], F32)
        si = sb("si", [P, NT], F32)
        stats = sb("stats", [P, NT, 6], F32)
        mv = sb("mv", [P, NT, 2], F32)
        stats2 = sb("stats2", [P, NT, 6], F32)
        mv2 = sb("mv2", [P, NT, 2], F32)
        veps = sb("veps", [P, 2, NT], F32)
        rstd = sb("rstd", [P, 2, NT], F32)
        mhalf = sb("mhalf", [P, NT], F32)
        lnA = sb("lnA", [P, NT], F32)
        lnB = sb("lnB", [P, NT], F32)
        xs2 = sb("xs2", [P, NT], F32)
        sig = sb("sig", [P, 2, H], F32)
        xmix = sb("xmix", [P, 2, H], F32)
        xn = sb("xn", [P, 2, H], F32)
        xhl = sb("xhl", [P, 2, 2, H], F16)
        gws = xn[0:E, 0, :]
        gw_hl = xn[0:E, 1, :].bitcast(F16).rearrange("e (a h) -> e a h", a=2)
        gwT = sb("gwT", [P, HC, 2 * E], F16)
        lgh = sb("lgh", [P, NT, E], F32)
        lg = sb("lg", [P, NT, E], F32)
        top8 = sb("top8", [P, NT, 8], F32)
        r_gt = sb("r_gt", [P, NT, E], F32)
        r_eq = sb("r_eq", [P, NT, E], F32)
        r_run = sb("r_run", [P, NT, E], F32)
        r_keep = sb("r_keep", [P, NT, E], F32)
        r_need = sb("r_need", [P, NT], F32)
        r_exp = sb("r_exp", [P, NT, E], F32)
        r_sum = sb("r_sum", [P, NT], F32)
        tick = sb("tick", [P, 1], F32)
        pool_tick = sb("pool_tick", [P, 1], F32)
        cw = sb("cw", [P, NT, E], F32)
        shared_w = sb("shared_w", [P, 1], F32)
        zeros = sb("zeros", [P, ROW // 4], F32)
        sc_rows, sd_rows = NE * G_GU, NE * IC
        sc_room = wgu[0:sc_rows, 1].rearrange("p a c n -> p (a c n)")
        sc_all = sc_room[:, 0:2 * GU].bitcast(F32)
        sc_top = sc_room[:, 2 * GU:4 * GU].bitcast(F32)
        sc_h = sc_room[:, 4 * GU:6 * GU].rearrange("p (a n) -> p a n", a=2)
        sd_room = wdn[0:sd_rows, 1].rearrange("p a c n -> p (a c n)")
        sd_all = sd_room[:, 0:2 * H].bitcast(F32)
        sd_top = sd_room[:, 2 * H:4 * H].bitcast(F32)
        sd_h = sd_room[:, 4 * H:6 * H].rearrange("p (a n) -> p a n", a=2)

        onehot = room_a[:, :].bitcast(F16).rearrange("p (b i q) -> p b i q", b=2, i=NT)
        values = wgu[:, 1].rearrange("p a c n -> p (a c n)")[:, 0:E * NT * KMAX]
        slot_room = wdn[:, 1].rearrange("p a c n -> p (a c n)")
        slot_ge = slot_room[:, 0:SLOTS * E].rearrange("p (s e) -> p s e", e=E)
        slot_nt = slot_room[:, SLOTS * E:2 * SLOTS * E].rearrange("p (s e) -> p s e", e=E)
        xg = room_b[:, 0:2 * ROW].rearrange("p (b n) -> p b n", b=2)
        at = [2 * ROW]

        def in_room_b(shape, dt):
            n = math.prod(shape[1:])
            piece = room_b[:, at[0]:at[0] + n]
            at[0] += n
            assert at[0] <= B * S
            if dt != F32:
                piece = piece.bitcast(dt)
            return piece.rearrange("p (a b) -> p a b", a=shape[1]) if len(shape) == 3 else piece
        tok = in_room_b([P, E * KMAX + 1], I32)
        tokf = in_room_b([P, E * KMAX], F32)
        tok0 = in_room_b([P, E * KMAX], F32)
        wide = wgu[:, 1].rearrange("p a c n -> p (a c n)")[:, E * NT * KMAX:].bitcast(F32)
        total = wide[:, 0:E * NT].rearrange("p (e i) -> p e i", i=NT)
        rank = wide[:, E * NT:2 * E * NT].rearrange("p (e i) -> p e i", i=NT)
        ranki = wide[:, 2 * E * NT:3 * E * NT].bitcast(I32)
        rankm = wide[:, 3 * E * NT:4 * E * NT].bitcast(I32)
        rank_k = sb("rank_k", [P, E * NT], F16)
        rank_q = sb("rank_q", [P, E, NT], F16)
        tri = sb("tri", [P, P], F16)
        ones16 = sb("ones16", [P, P], F16)
        sel16 = sb("sel16", [P, NT * E], F16)
        iota_q = sb("iota_q", [P, P], F16)
        iota_k = sb("iota_k", [P, KMAX], F16)
        token1 = sb("token1", [P, NT], F16)
        dump_row = sb("dump_row", [P, 1], F32)
        tiles_i = sb("tiles_i", [P, E], I32)
        tiles_f = sb("tiles_f", [P, E], F32)
        cum_f = sb("cum_f", [P, E], F32)
        odd_i = sb("odd_i", [P, 1], I32)
        odd_f = sb("odd_f", [P, 1], F32)
        first_i = sb("first_i", [P, E], I32)
        parts_i = sb("parts_i", [P, E], I32)
        later_i = sb("later_i", [P, E], I32)
        pairs_i = sb("pairs_i", [P, 1], I32)
        slot_f = sb("slot_f", [P, 2, SLOTS], F32)
        slot_i = sb("slot_i", [P, 2, SLOTS], I32)
        iota_s = sb("iota_s", [P, SLOTS], F32)
        idx_g = sb("idx_g", [P, 2], I32)
        idx_s = sb("idx_s", [P, 2], I32)
        wslot = sb("wslot", [P, 2, E], F32)
        xTs = xn[:, :, :].rearrange("p b h -> p (b h)").bitcast(F16).rearrange("p (b n) -> p b n", b=2)
        y_sb = xmix

        gu_ps = psum("gu_ps", [P, 4, 512], F32)
        bank = [gu_ps[:, i, :] for i in range(4)] + [psum(f"bank{i}", [P, 512], F32)[:, :] for i in range(4, 8)]
        g_ps, u_ps = bank[0:2], bank[2:4]
        at_ps = bank[4][:, 0:IC * P].bitcast(F16)
        y_ps = bank[5:7]
        sj_ps = bank[0:4]
        tp_ps = bank[4:6]
        lg_ps = bank[6]
        si_ps = bank[7]
        rt_ps = bank[7]
        xT_ps = bank[7].bitcast(F16)

        ld_const = sem("ld_const")
        ld_x = [sem(f"ld_x{b}") for b in range(B)]
        ld_ctx = [sem(f"ld_ctx{b}") for b in range(B)]
        ld_sc = sem("ld_sc")
        st_sc = sem("st_sc")
        ld_w = [sem("ld_w0"), sem("ld_w1")]
        pool_const = sem("pool_const")
        ctxT_ps_ready = sem("ctxT_ps_ready")
        ctxT_ready = sem("ctxT_ready")
        wj_ready = sem("wj_ready")
        si_ps_ready = sem("si_ps_ready")
        si_ready = sem("si_ready")
        sj_ready = sem("sj_ready")
        tg_ready = sem("tg_ready")
        ve_ready = sem("ve_ready")
        rstd_ready = sem("rstd_ready")
        sig_ready = sem("sig_ready")
        x1_ready = sem("x1_ready")
        xn_ready = sem("xn_ready")
        xh_ready = sem("xh_ready")
        xl_ready = sem("xl_ready")
        xT_ps_ready = sem("xT_ps_ready")
        xT_ready = sem("xT_ready")
        gw_ready = sem("gw_ready")
        gwT_ps_ready = sem("gwT_ps_ready")
        gwT_ready = sem("gwT_ready")
        lg_ps_ready = sem("lg_ps_ready")
        lgh_ready = sem("lgh_ready")
        lsub_ready = sem("lsub_ready")
        exp_ready = sem("exp_ready")
        half_ready = sem("half_ready")
        dq_ready = sem("dq_ready")
        gu_done = sem("gu_done")
        sg_done = sem("sg_done")
        act_done = sem("act_done")
        ah_done = sem("ah_done")
        al_done = sem("al_done")
        at_done = sem("at_done")
        aT_done = sem("aT_done")
        y_done = sem("y_done")
        acc_done = sem("acc_done")
        vs = sem("vector_step")
        dqs = sem("dequant_step")
        st_out = sem("st_out")
        st_rows = [sem("st_rows0"), sem("st_rows1")]
        st_cw = sem("st_cw")
        rows_zero = sem("rows_zero")
        sel_ready = sem("sel_ready")
        count_ready = sem("count_ready")
        onehot_ready = sem("onehot_ready")
        list_ready = sem("list_ready")
        route_ready = sem("route_ready")
        cw_ready = sem("cw_ready")
        xg_ld = [sem("xg_ld0"), sem("xg_ld1")]
        tx_done = sem("tx_done")
        xTs_done = sem("xTs_done")
        wslot_done = sem("wslot_done")
        yev_done = sem("yev_done")
        added = sem("added")
        idx_g_ready = sem("idx_g_ready")
        idx_s_ready = sem("idx_s_ready")

        block = ctx.enter_context(nc.Block())

        def tile_order_h(ap):
            return ap.rearrange("p (c f r) -> p r f c", f=2, r=GR)

        def natural_h(ap):
            return ap.rearrange("p (r f c) -> p r f c", f=2, c=HC)

        def tile_order_i(ap):
            return ap.rearrange("p (t j r) -> p t r j", j=NIB, r=RG)

        def natural_i(ap):
            return ap.rearrange("p (t r j) -> p t r j", j=NIB, r=RG)

        def load_expert(sp, gp, dp, buf, n):
            for f in range(2):
                rows = slice(f * GR, (f + 1) * GR)
                sp.dma_start(gu_raw[rows, buf, :], gp).then_inc(ld_w[buf], 16)
                for hl in range(2):
                    for g in range(G_GU):
                        r0 = f * GR + g * RG
                        sp.dma_start(gu_sc[r0:r0 + RG, buf, hl, :],
                                     gu_s_dram[hl, n, g].unsqueeze(0).broadcast_to([RG, GU])).then_inc(ld_w[buf], 16)
            for j in range(NIB):
                sp.dma_start(dn_raw[j * RG:(j + 1) * RG, buf, :, :],
                             dp.rearrange("(t r) n -> r t n", r=RG)).then_inc(ld_w[buf], 16)
            for hl in range(2):
                sp.dma_start(dn_sc[:, buf, hl, :, :],
                             dn_s_dram[hl, n].unsqueeze(0).broadcast_to([P, IC, H])).then_inc(ld_w[buf], 16)
        LOADS = 2 * (1 + 2 * G_GU) + NIB + 2

        def loaded(n):
            return 16 * LOADS * (n // 2 + 1)

        POOL_CONST = 16
        SPLIT_STEPS = 10

        @block.sync
        def _(sp):
            for k in range(2):
                sp.dma_start(wij[:, k:k + 1], xattn_w.rearrange("o (k p) -> k p o", p=P)[k],
                             allow_slow_non_contiguous=True).then_inc(ld_const, 16)
            sp.dma_start(bias[:, :], xattn_b.unsqueeze(0).broadcast_to([P, 1])).then_inc(ld_const, 16)
            sp.dma_start(gates[:, 0:1], g_xattn.unsqueeze(0).broadcast_to([P, 1])).then_inc(ld_const, 16)
            sp.dma_start(gates[:, 1:2], g_ffn.unsqueeze(0).broadcast_to([P, 1])).then_inc(ld_const, 16)
            sp.dma_start(gws[:, :], gate_w).then_inc(ld_const, 16)
            for b in range(B):
                sp.dma_start(ctxs[:, b * TB:(b + 1) * TB, :], ctx_t[b]).then_inc(ld_ctx[b], 16)
                sp.dma_start(X[:, b * TB:(b + 1) * TB, :], x_t[b]).then_inc(ld_x[b], 16)
            sp.dma_start(sc_all[0:G_GU, :], sh_gu_scales).then_inc(ld_sc, 16)
            sp.dma_start(sc_all[G_GU:NE * G_GU, :], gu_scales.rearrange("e g n -> (e g) n")).then_inc(ld_sc, 16)
            sp.dma_start(sd_all[0:IC, :], sh_dn_scales).then_inc(ld_sc, 16)
            sp.dma_start(sd_all[IC:NE * IC, :], dn_scales.rearrange("e g n -> (e g) n")).then_inc(ld_sc, 16)
            sp.wait_ge(vs, SPLIT_STEPS)
            for hl in range(2):
                sp.dma_start(gu_s_dram[hl].rearrange("e g n -> (e g) n"), sc_h[:, hl, :]).then_inc(st_sc, 16)
                sp.dma_start(dn_s_dram[hl].rearrange("e g n -> (e g) n"), sd_h[:, hl, :]).then_inc(st_sc, 16)
            sp.wait_ge(st_sc, 64)
            load_expert(sp, sh_gu_packed, sh_dn_packed, 0, 0)
            load_expert(sp, gu_packed[0], dn_packed[0], 1, 1)
            for i in range(NT):
                sp.wait_ge(xh_ready, i + 1)
                sp.wait_ge(xl_ready, i + 1)
                sp.dma_start(rows_dram[i * P:(i + 1) * P, 0:H],
                             xhl[:, i % 2].rearrange("p a h -> p (a h)").bitcast(F32))\
                    .then_inc(st_rows[i % 2], 16)
            sp.wait_ge(pool_const, POOL_CONST)
            sp.dma_start(rows_dram[T:T + P, :].rearrange("p (a n) -> p a n", a=4),
                         zeros[:, :].unsqueeze(1).broadcast_to([P, 4, ROW // 4])).then_inc(rows_zero, 16)
            sp.dma_start(out[T:T + P, :].rearrange("p (a n) -> p a n", a=4),
                         zeros[:, 0:H // 4].unsqueeze(1).broadcast_to([P, 4, H // 4])).then_inc(st_out, 16)
            sp.wait_ge(cw_ready, 1)
            sp.dma_start(rows_dram[0:T, H:ROW].rearrange("(i p) e -> p i e", p=P), cw[:, :, :])\
                .then_inc(st_cw, 16)
            sp.wait_ge(dq_ready, 1)
            load_expert(sp, gu_packed[1], dn_packed[1], 0, 2)
            for b in range(B):
                sp.wait_ge(acc_done, (b + 1) * TB)
                sp.dma_start(out_t[b], X[:, b * TB:(b + 1) * TB, :]).then_inc(st_out, 16)
            sp.wait_ge(dq_ready, 2)
            load_expert(sp, gu_packed[2], dn_packed[2], 1, 3)
            with sp.Fori(1, E // 2 - 1) as h:
                sp.wait_ge(dq_ready, 2 * h + 1)
                load_expert(sp, gu_packed[2 * h + 1], dn_packed[2 * h + 1], 0, 2 * h + 2)
                sp.wait_ge(dq_ready, 2 * h + 2)
                load_expert(sp, gu_packed[2 * h + 2], dn_packed[2 * h + 2], 1, 2 * h + 3)
            sp.wait_ge(dq_ready, E - 1)
            load_expert(sp, gu_packed[E - 1], dn_packed[E - 1], 0, E)
            sp.wait_ge(st_out, 16 * (B + 1))

        @block.gpsimd
        def _(pool):
            nc.gpsimd.memset(ones[:, :], 1.0).then_inc(pool_const, 1)
            nc.gpsimd.memset(id32[:, :], 0.0).then_inc(pool_const, 1)
            nc.gpsimd.memset(id16[:, :], 0.0).then_inc(pool_const, 1)
            nc.gpsimd.memset(mhalf[:, :], -0.5).then_inc(pool_const, 1)
            nc.gpsimd.iota(dn_shift[:, :], [[0, 1]], base=P - 1, channel_multiplier=-1).then_inc(pool_const, 1)
            nc.gpsimd.memset(zeros[:, :], 0.0).then_inc(pool_const, 1)
            nc.gpsimd.memset(tri[:, :], 1.0).then_inc(pool_const, 1)
            nc.gpsimd.memset(ones16[:, :], 1.0).then_inc(pool_const, 1)
            for dst, pattern, base, mult in ((iota_q[:, :], [[1, P]], 1, 0), (iota_k[:, :], [[1, KMAX]], 0, 0),
                                             (token1[:, :], [[P, NT]], 1, 1), (dump_row[:, :], [[0, 1]], DUMP + 1, 1),
                                             (iota_s[:, :], [[1, SLOTS]], 0, 0)):
                nc.gpsimd.iota(dst, pattern, base=base, channel_multiplier=mult,
                               allow_small_or_imprecise_dtypes=True).then_inc(pool_const, 1)
            pool.wait_ge(pool_const, 13)
            nc.gpsimd.affine_select(out=tri[:, :], in_=tri[:, :], compare_op=ALU.is_gt, fill=0.0, base=0,
                                    pattern=[[1, P]], channel_multiplier=-1).then_inc(pool_const, 1)
            for ident in (id32, id16):
                nc.gpsimd.affine_select(out=ident[:, :], in_=ident[:, :], compare_op=ALU.not_equal, fill=1.0,
                                        base=0, pattern=[[-1, P]], channel_multiplier=1).then_inc(pool_const, 1)
            for n in range(2 * B):
                pool.wait_ge(ve_ready, n + 1)
                k = 0 if n < B else 1
                cols = slice((n % B) * TB, (n % B + 1) * TB)
                nc.gpsimd.tensor_tensor(rstd[:, k, cols], veps[:, k, cols], mhalf[:, cols], ALU.pow).then_inc(rstd_ready, 1)

            pool.wait_ge(rows_zero, 16)
            for b in range(2):
                pool.wait_ge(st_rows[b], 16 * (NT // 2))
            pool.wait_ge(st_cw, 16)
            pool.wait_ge(route_ready, 1)
            inner = pool.value_load(pairs_i[0:1, 0:1], min_val=E // 2 - 2, max_val=SLOTS // 2 - 2)

            def hold_wait():
                nc.gpsimd.tensor_tensor(pool_tick[:, :], ones[:, 0:1], ones[:, 0:1], ALU.mult)

            def gather(s, b):
                col = pool.value_load(slot_i[0:1, 1, bass.ds(s, 1)], min_val=0, max_val=E * KMAX)
                if not isinstance(s, int) or s >= 2:
                    pool.wait_ge(tx_done, s - 1)
                    pool.wait_ge(wslot_done, s - 1)
                pool.wait_ge(route_ready, 1)
                nc.gpsimd.tensor_copy(idx_g[:, b:b + 1], tok[:, bass.ds(col, 1)]).then_inc(idx_g_ready, 1)
                pool.wait_ge(idx_g_ready, s + 1)
                hold_wait()
                nc.gpsimd.indirect_dma_start(xg[:, b, :], None, rows_dram[:, :],
                                             bass.IndirectOffsetOnAxis(idx_g[:, b:b + 1], 0)).then_inc(xg_ld[b], 16)

            def add(s, b):
                col = pool.value_load(slot_i[0:1, 1, bass.ds(s, 1)], min_val=0, max_val=E * KMAX)
                pool.wait_ge(yev_done, s + 1)
                if not isinstance(s, int) or s >= 1:
                    pool.wait_ge(added, 16 * s)
                pool.wait_ge(st_out, 16 * (B + 1))
                nc.gpsimd.tensor_copy(idx_s[:, b:b + 1], tok[:, bass.ds(col, 1)]).then_inc(idx_s_ready, 1)
                pool.wait_ge(idx_s_ready, s + 1)
                hold_wait()
                nc.gpsimd.indirect_dma_start(out[:, :], bass.IndirectOffsetOnAxis(idx_s[:, b:b + 1], 0), y_sb[:, b, :],
                                             None, compute_op=ALU.add).then_inc(added, 16)
            for s in range(4):
                gather(s, s % 2)
            with pool.Fori(1, inner + 1) as j:
                for b in range(2):
                    gather(2 * j + b + 2, b)
                    add(2 * j + b - 2, b)
            for k in range(-4, 0):
                add(2 * inner + 4 + k, k % 2)
            pool.wait_ge(added, 32 * inner + 64)

        @block.scalar
        def _(a):
            a.wait_ge(ld_const, 16 * 6)
            nc.scalar.activation(tg[:, 0:2], gates[:, :], ACT.Tanh).then_inc(tg_ready, 1)
            for b in range(B):
                a.wait_ge(ctxT_ps_ready, b + 1)
                nc.scalar.activation(ctxT[:, b, :], tp_ps[b % 2][:, :], ACT.Copy).then_inc(ctxT_ready, 1)
            for hl in range(2):
                a.wait_ge(gwT_ps_ready, hl + 1)
                nc.scalar.activation(gwT[:, :, hl * E:(hl + 1) * E],
                                     tp_ps[hl][:, 0:HC * E // 2].bitcast(F16).rearrange("p (c e) -> p c e", e=E),
                                     ACT.Copy).then_inc(gwT_ready, 1)
            for i in range(NT):
                a.wait_ge(si_ready, 1)
                a.wait_ge(sj_ready, i // TB + 1)
                if i >= 2:
                    a.wait_ge(x1_ready, i - 1)
                nc.scalar.activation(sig[:, i % 2, :], sj_ps[i // TB][:, :], ACT.Sigmoid,
                                     bias=si[:, i:i + 1]).then_inc(sig_ready, 1)

            def split_x(i):
                a.wait_ge(xn_ready, i + 1)
                if i >= 2:
                    a.wait_ge(xT_ps_ready, i - 1)
                    a.wait_ge(st_rows[i % 2], 16 * (i // 2))
                nc.scalar.activation(tile_order_h(xhl[:, i % 2, 0, :]), natural_h(xn[:, i % 2, :]),
                                     ACT.Copy).then_inc(xh_ready, 1)

            def copy_xT(i):
                a.wait_ge(xT_ps_ready, i + 1)
                nc.scalar.activation(xT[:, i].rearrange("p a c t -> p (a c t)"), tp_ps[i % 2][:, :].bitcast(F16),
                                     ACT.Copy).then_inc(xT_ready, 1)
            for i in range(NT):
                split_x(i)
                if i:
                    copy_xT(i - 1)
            copy_xT(NT - 1)

            def route():
                a.wait_ge(lg_ps_ready, NT)
                nc.scalar.activation(lgh[:, :, :], lg_ps[:, :].rearrange("p (t k e) -> p t k e", k=2, e=E)[:, :, 1, :],
                                     ACT.Copy).then_inc(lgh_ready, 1)
                a.wait_ge(lsub_ready, 1)
                nc.scalar.activation(r_exp[:, :, :], lg[:, :, :], ACT.Exp).then_inc(exp_ready, 1)

            def activate(s, b):
                a.wait_ge(gu_done, s + 1)
                if not isinstance(s, int) or s >= 2:
                    a.wait_ge(act_done, s - 1)
                nc.scalar.activation(sg[:, b, :], g_ps[b][:, 0:I], ACT.Silu,
                                     scale=1.0 / (X_SCALE * W_SCALE)).then_inc(sg_done, 1)
                a.wait_ge(act_done, s + 1)
                if not isinstance(s, int) or s >= 2:
                    a.wait_ge(at_done, s - 1)
                nc.scalar.activation(tile_order_i(acth[:, b, 0, :]), natural_i(act[:, b, :]), ACT.Copy).then_inc(ah_done, 1)

            def take_rows(r, b):
                a.wait_ge(xg_ld[b], 8 * (r - b) + 16)
                if not isinstance(r, int) or r >= 2:
                    a.wait_ge(act_done, NT + r - 1)
                nc.scalar.activation(wslot[:, b, :], xg[:, b, H:ROW], ACT.Copy).then_inc(wslot_done, 1)
                a.wait_ge(tx_done, r + 1)
                if not isinstance(r, int) or r >= 2:
                    a.wait_ge(gu_done, NT + r - 1)
                nc.scalar.activation(xTs[:, b, :], xT_ps, ACT.Copy).then_inc(xTs_done, 1)

            def take_y(r, b):
                a.wait_ge(y_done, NT + r + 1)
                if not isinstance(r, int) or r >= 2:
                    a.wait_ge(added, 16 * (r - 1))
                nc.scalar.activation(y_sb[:, b, :], y_ps[b][:, :], ACT.Copy, scale=1.0 / W_SCALE).then_inc(yev_done, 1)

            for i in range(NT):
                if i == NT - 1:
                    take_rows(0, 0)
                activate(i, i % 2)
                if i == 0:
                    route()
            a.wait_ge(route_ready, 1)
            inner = a.value_load(pairs_i[0:1, 0:1], min_val=E // 2 - 2, max_val=SLOTS // 2 - 2)

            def slot(r, b, rows=True):
                if rows:
                    take_rows(r + 1, 1 - b)
                activate(NT + r, b)
                if not isinstance(r, int) or r >= 1:
                    take_y(r - 1, 1 - b)
            slot(0, 0)
            slot(1, 1)
            with a.Fori(1, inner + 1) as j:
                slot(2 * j, 0)
                slot(2 * j + 1, 1)
            slot(2 * inner + 2, 0)
            slot(2 * inner + 3, 1, rows=False)
            take_y(2 * inner + 3, 1)

        @block.vector
        def _(v):
            count = [0]

            def step(ins, wait=True):
                count[0] += 1
                ins.then_inc(vs, 1)
                if wait:
                    v.wait_ge(vs, count[0])

            v.wait_ge(ld_sc, 64)
            for whole, top, half in ((sc_all, sc_top, sc_h), (sd_all, sd_top, sd_h)):
                rest = half[:, :, :].rearrange("p a n -> p (a n)").bitcast(F32)
                step(nc.vector.tensor_scalar(top[:, :], whole[:, :], SPLITTER, None, ALU.mult))
                step(nc.vector.tensor_tensor(rest, top[:, :], whole[:, :], ALU.subtract))
                step(nc.vector.tensor_tensor(top[:, :], top[:, :], rest, ALU.subtract))
                step(nc.vector.tensor_scalar(half[:, 0, :], top[:, :], W_SCALE, None, ALU.mult))
                step(nc.vector.scalar_tensor_tensor(half[:, 1, :], whole[:, :], W_SCALE, half[:, 0, :], ALU.mult, ALU.subtract))
            assert count[0] == SPLIT_STEPS
            v.wait_ge(ld_const, 16 * 6)
            v.wait_ge(pool_const, POOL_CONST)
            step(nc.vector.tensor_scalar(dn_shift[:, :], dn_shift[:, :], 4, 2, ALU.logical_shift_right,
                                         ALU.logical_shift_left))
            nc.vector.tensor_scalar(wj_all[:, :], ones[:, :], wij[:, 1:2], None, ALU.mult).then_inc(wj_ready, 1)
            step(nc.vector.tensor_scalar(gws[:, :], gws[:, :], R_SCALE, None, ALU.mult))
            step(nc.vector.tensor_copy(tile_order_h(gw_hl[:, 0, :]), natural_h(gws[:, :])))
            nc.vector.tensor_tensor(tile_order_h(gw_hl[:, 1, :]), natural_h(gws[:, :]), tile_order_h(gw_hl[:, 0, :]),
                                    ALU.subtract).then_inc(gw_ready, 1)
            v.wait_ge(tg_ready, 1)
            step(nc.vector.tensor_scalar(tg[:, 2:3], tg[:, 0:1], P_ASEM, None, ALU.mult), wait=False)
            step(nc.vector.tensor_scalar(tg[:, 3:4], tg[:, 0:1], 1.0 - P_ASEM, None, ALU.mult))

            def norm_stats(st, agg, k, b):
                for i in range(b * TB, (b + 1) * TB):
                    step(nc.vector.bn_stats(st[:, i, :], X[:, i, :]))
                    step(nc.vector.bn_aggr(agg[:, i, :], st[:, i, :]))
                nc.vector.tensor_scalar(veps[:, k, b * TB:(b + 1) * TB], agg[:, b * TB:(b + 1) * TB, 1], LN_EPS, None,
                                        ALU.add).then_inc(ve_ready, 1)
            for b in range(B):
                v.wait_ge(ld_x[b], 16)
                norm_stats(stats, mv, 0, b)
            v.wait_ge(si_ps_ready, 1)
            nc.vector.tensor_scalar(si[:, :], si_ps[:, 0:NT], bias[:, 0:1], None, ALU.add).then_inc(si_ready, 1)
            v.wait_ge(rstd_ready, B)
            step(nc.vector.tensor_scalar(lnA[:, :], rstd[:, 0, :], tg[:, 3:4], None, ALU.mult))
            step(nc.vector.tensor_tensor(lnB[:, :], lnA[:, :], mv[:, :, 0], ALU.mult))
            step(nc.vector.tensor_scalar(lnB[:, :], lnB[:, :], -1.0, None, ALU.mult), wait=False)
            step(nc.vector.tensor_scalar(lnA[:, :], lnA[:, :], 1.0, None, ALU.add))
            for b in range(B):
                for i in range(b * TB, (b + 1) * TB):
                    step(nc.vector.tensor_scalar(xmix[:, i % 2, :], X[:, i, :], lnA[:, i:i + 1], lnB[:, i:i + 1],
                                                 ALU.mult, ALU.add))
                    v.wait_ge(sig_ready, i + 1)
                    nc.vector.scalar_tensor_tensor(X[:, i, :], sig[:, i % 2, :], tg[:, 2:3], xmix[:, i % 2, :],
                                                   ALU.mult, ALU.add).then_inc(x1_ready, 1)
                    v.wait_ge(x1_ready, i + 1)
                norm_stats(stats2, mv2, 1, b)
            v.wait_ge(rstd_ready, 2 * B)
            step(nc.vector.tensor_scalar(xs2[:, :], rstd[:, 1, :], X_SCALE, None, ALU.mult))
            for i in range(NT):
                if i >= 2:
                    v.wait_ge(xh_ready, i - 1)
                    v.wait_ge(st_rows[i % 2], 16 * (i // 2))
                nc.vector.tensor_scalar(xn[:, i % 2, :], X[:, i, :], mv2[:, i, 0:1], xs2[:, i:i + 1],
                                        ALU.subtract, ALU.mult).then_inc(xn_ready, 1)
                v.wait_ge(xh_ready, i + 1)
                nc.vector.tensor_tensor(tile_order_h(xhl[:, i % 2, 1, :]), natural_h(xn[:, i % 2, :]),
                                        tile_order_h(xhl[:, i % 2, 0, :]), ALU.subtract).then_inc(xl_ready, 1)

            step(nc.vector.tensor_scalar(shared_w[:, :], tg[:, 1:2], 1.0 / (X_SCALE * W_SCALE), None, ALU.mult))

            def route():
                v.wait_ge(lgh_ready, 1)
                step(nc.vector.tensor_tensor(lg[:, :, :], lg_ps[:, :].rearrange("p (t k e) -> p t k e", k=2, e=E)[:, :, 0, :],
                                             lgh[:, :, :], ALU.add))
                step(nc.vector.tensor_scalar(lg[:, :, :], lg[:, :, :], 1.0 / (X_SCALE * R_SCALE), None, ALU.mult))
                for i in range(NT):
                    step(nc.vector.max(top8[:, i, :], lg[:, i, :]), wait=(i == NT - 1))
                kth = top8[:, :, TOP_K - 1:TOP_K].broadcast_to([P, NT, E])
                step(nc.vector.tensor_tensor(r_gt[:, :, :], lg[:, :, :], kth, ALU.is_gt), wait=False)
                step(nc.vector.tensor_tensor(r_eq[:, :, :], lg[:, :, :], kth, ALU.is_equal))
                nc.vector.tensor_tensor(lg[:, :, :], lg[:, :, :], top8[:, :, 0:1].broadcast_to([P, NT, E]),
                                        ALU.subtract).then_inc(lsub_ready, 1)
                step(nc.vector.tensor_reduce(r_need[:, :], r_gt[:, :, :], AX, ALU.add), wait=False)
                step(nc.vector.memset(r_keep[:, :, :], 1.0))
                step(nc.vector.memset(r_keep[:, :, 0:1], 0.0))
                step(nc.vector.tensor_tensor_scan(r_run[:, :, :].rearrange("p t e -> p (t e)"),
                                                  r_keep[:, :, :].rearrange("p t e -> p (t e)"),
                                                  r_eq[:, :, :].rearrange("p t e -> p (t e)"), 0.0, ALU.mult, ALU.add))
                step(nc.vector.tensor_tensor(r_run[:, :, :], r_run[:, :, :],
                                             r_need[:, :].unsqueeze(2).broadcast_to([P, NT, E]), ALU.add))
                step(nc.vector.tensor_scalar(r_run[:, :, :], r_run[:, :, :], float(TOP_K), None, ALU.is_le))
                step(nc.vector.tensor_tensor(r_eq[:, :, :], r_eq[:, :, :], r_run[:, :, :], ALU.mult))
                step(nc.vector.tensor_tensor(r_gt[:, :, :], r_gt[:, :, :], r_eq[:, :, :], ALU.add))
                nc.vector.tensor_copy(sel16[:, :], r_gt[:, :, :].rearrange("p t e -> p (t e)")).then_inc(sel_ready, 1)
                v.wait_ge(exp_ready, 1)
                step(nc.vector.tensor_tensor(r_exp[:, :, :], r_exp[:, :, :], r_gt[:, :, :], ALU.mult))
                step(nc.vector.tensor_reduce(r_sum[:, :], r_exp[:, :, :], AX, ALU.add))
                step(nc.vector.reciprocal(r_sum[:, :], r_sum[:, :]))
                step(nc.vector.tensor_scalar(r_sum[:, :], r_sum[:, :], shared_w[:, 0:1], None, ALU.mult))
                nc.vector.tensor_tensor(cw[:, :, :], r_exp[:, :, :], r_sum[:, :].unsqueeze(2).broadcast_to([P, NT, E]),
                                        ALU.mult).then_inc(cw_ready, 1)

            def ranks():
                v.wait_ge(count_ready, 1)
                step(nc.vector.tensor_copy(total, rt_ps[:, NT * E:2 * NT * E].rearrange("p (i e) -> p e i", e=E)))
                step(nc.vector.tensor_tensor_scan(r_run[:, :, :].rearrange("p e i -> p (e i)"),
                                                  r_keep[:, :, :].rearrange("p e i -> p (e i)"),
                                                  total.rearrange("p e i -> p (e i)"), 0.0, ALU.mult, ALU.add))
                step(nc.vector.tensor_tensor(rank, r_run[:, :, :], total, ALU.subtract))
                step(nc.vector.tensor_tensor(ranki.rearrange("p (e i) -> p e i", i=NT), rank,
                                             rt_ps[:, 0:NT * E].rearrange("p (i e) -> p e i", e=E), ALU.add))
                step(nc.vector.tensor_scalar(rankm, ranki, 7, None, ALU.logical_shift_right))
                step(nc.vector.tensor_copy(rank_k[:, :], rankm))
                step(nc.vector.tensor_scalar(ranki, ranki, P - 1, None, ALU.bitwise_and))
                step(nc.vector.scalar_tensor_tensor(rank_q[:, :, :], ranki.rearrange("p (e i) -> p e i", i=NT), 1.0,
                                                    r_gt[:, :, :].rearrange("p i e -> p e i"), ALU.add, ALU.mult))
                cells = values.rearrange("p (g k) -> p g k", k=KMAX)
                step(nc.vector.tensor_tensor(cells, rank_k[:, :].unsqueeze(2).broadcast_to([P, E * NT, KMAX]),
                                             iota_k[:, :].unsqueeze(1).broadcast_to([P, E * NT, KMAX]), ALU.is_equal))
                cells = values.rearrange("p (e i k) -> p e i k", i=NT, k=KMAX)
                step(nc.vector.tensor_tensor(cells, cells, token1[:, :].unsqueeze(1).unsqueeze(3).broadcast_to([P, E, NT, KMAX]),
                                             ALU.mult))

            def tables():
                step(nc.vector.tensor_scalar(tiles_i[:, :], r_run[:, :, NT - 1], float(P - 1), None, ALU.add))
                step(nc.vector.tensor_scalar(tiles_i[:, :], tiles_i[:, :], 7, None, ALU.logical_shift_right))
                step(nc.vector.tensor_scalar(tiles_f[:, :], tiles_i[:, :], 1.0, None, ALU.max))
                step(nc.vector.tensor_tensor_scan(cum_f[:, :], ones[:, 0:E], tiles_f[:, :], 0.0, ALU.mult, ALU.add))
                step(nc.vector.tensor_copy(odd_i[:, :], cum_f[:, E - 1:E]))
                step(nc.vector.tensor_scalar(odd_i[:, :], odd_i[:, :], 1, None, ALU.bitwise_and))
                step(nc.vector.tensor_copy(odd_f[:, :], odd_i[:, :]))
                for t in (tiles_f, cum_f):
                    step(nc.vector.tensor_tensor(t[:, E - 1:E], t[:, E - 1:E], odd_f[:, :], ALU.add))
                step(nc.vector.tensor_copy(tiles_i[:, :], tiles_f[:, :]), wait=False)
                step(nc.vector.tensor_tensor(first_i[:, :], cum_f[:, :], tiles_f[:, :], ALU.subtract), wait=False)
                step(nc.vector.tensor_scalar(pairs_i[:, :], cum_f[:, E - 1:E], 0.5, -2.0, ALU.mult, ALU.add), wait=False)
                step(nc.vector.tensor_scalar(parts_i[:, :], tiles_f[:, :], float(PARTS), -1.0, ALU.min, ALU.mult))
                step(nc.vector.tensor_scalar(later_i[:, :], parts_i[:, :], -1.0, -1.0, ALU.mult, ALU.add), wait=False)
                step(nc.vector.tensor_scalar(parts_i[:, :], parts_i[:, :], float(PARTS + 1), None, ALU.add))
                by_expert = [P, SLOTS, E]
                step(nc.vector.tensor_tensor(slot_ge, iota_s[:, :].unsqueeze(2).broadcast_to(by_expert),
                                             cum_f[:, :].unsqueeze(1).broadcast_to(by_expert), ALU.is_ge))
                step(nc.vector.tensor_tensor(slot_nt, slot_ge, tiles_f[:, :].unsqueeze(1).broadcast_to(by_expert), ALU.mult))
                for k, t in enumerate((slot_ge, slot_nt)):
                    step(nc.vector.tensor_reduce(slot_f[:, k, :], t, AX, ALU.add))
                step(nc.vector.tensor_copy(slot_i[:, 0, :], slot_f[:, 0, :]), wait=False)
                step(nc.vector.scalar_tensor_tensor(slot_f[:, 1, :], slot_f[:, 0, :], float(KMAX), slot_f[:, 1, :],
                                                    ALU.mult, ALU.subtract))
                step(nc.vector.tensor_tensor(slot_i[:, 1, :], slot_f[:, 1, :], iota_s[:, :], ALU.add))

            def mark_places(e):
                if e >= 2:
                    v.wait_ge(list_ready, e - 1)
                nc.vector.tensor_tensor(onehot[:, e % 2], rank_q[:, e, :].unsqueeze(2).broadcast_to([P, NT, P]),
                                        iota_q[:, :].unsqueeze(1).broadcast_to([P, NT, P]),
                                        ALU.is_equal).then_inc(onehot_ready, 1)

            def lists():
                v.wait_ge(list_ready, E)
                ps = rt_ps[:, 0:E * KMAX]
                step(nc.vector.tensor_scalar(tok0, ps, 0.0, None, ALU.is_equal))
                step(nc.vector.scalar_tensor_tensor(tokf, tok0, dump_row[:, 0:1], ps, ALU.mult, ALU.add))
                step(nc.vector.tensor_scalar(tok[:, 0:E * KMAX], tokf, -1.0, None, ALU.add))
                step(nc.vector.tensor_scalar(tok[:, E * KMAX:], dump_row[:, :], -1.0, None, ALU.add))
                nc.vector.memset(tick[:, 0:1], 0.0).then_inc(route_ready, 1)

            PARTS = HC
            COLS = IC * H // PARTS
            STEPS = 12
            N_STEPS = 2 + PARTS * STEPS

            def dequant(n, buf, k):
                done = n * N_STEPS + 2 + k * STEPS
                c = HC - 1 - k
                at = [0]

                def link(ins, wait=True):
                    at[0] += 1
                    ins.then_inc(dqs, 1)
                    if wait:
                        v.wait_ge(dqs, done + at[0])
                cols = slice(k * COLS, (k + 1) * COLS) if isinstance(k, int) else bass.ds(k * COLS, COLS)
                raw = dn_raw[:, buf].rearrange("p t n -> p (t n)")[:, cols]
                v.wait_ge(dqs, done)
                link(nc.vector.tensor_scalar(dq_sign[:, :], gu_half[:, :], 0x8000, None, ALU.bitwise_and), wait=False)
                link(nc.vector.tensor_scalar(dq_mag[:, :], gu_half[:, :], 3, 0x0E00, ALU.logical_shift_right,
                                             ALU.bitwise_and), wait=False)
                link(nc.vector.tensor_scalar(dn_bits[:, 0:COLS], raw, dn_shift[:, 0:1], None,
                                             ALU.logical_shift_left))
                link(nc.vector.tensor_tensor(dq_mag[:, :], dq_mag[:, :], dq_sign[:, :], ALU.bitwise_or), wait=False)
                link(nc.vector.tensor_scalar(dn_bits[:, 0:COLS], dn_bits[:, 0:COLS], 3, 0x8E000000 - (1 << 32),
                                             ALU.arith_shift_right, ALU.bitwise_and))
                link(nc.vector.tensor_scalar(dq_code[:, :], dq_mag[:, :].bitcast(F16), CODE_SCALE, None, ALU.mult),
                     wait=False)
                link(nc.vector.tensor_scalar(dn_code[:, 0:COLS],
                                             dn_bits[:, 0:COLS].bitcast(F16).rearrange("p (n f) -> p n f", f=2)[:, :, 1],
                                             CODE_SCALE, None, ALU.mult))
                link(nc.vector.tensor_scalar(gu_half[:, :], gu_half[:, :], 4, None, ALU.logical_shift_left), wait=False)
                for hl in range(2):
                    link(nc.vector.tensor_tensor(wgu[:, buf, hl, c, :], dq_code[:, :], gu_sc[:, buf, hl, :], ALU.mult),
                         wait=False)
                for hl in range(2):
                    link(nc.vector.tensor_tensor(wdn[:, buf, hl].rearrange("p t n -> p (t n)")[:, cols],
                                                 dn_code[:, 0:COLS],
                                                 dn_sc[:, buf, hl].rearrange("p t n -> p (t n)")[:, cols], ALU.mult),
                         wait=False)
                assert at[0] == STEPS

            def start_dequant(n, buf):
                if not isinstance(n, int) or n:
                    v.wait_ge(dqs, n * N_STEPS)
                v.wait_ge(ld_w[buf], loaded(n))
                words = gu_raw[:, buf, :].bitcast(U16).rearrange("p (n f) -> p n f", f=2)
                for f in range(2):
                    rows = slice(f * GR, (f + 1) * GR)
                    nc.vector.tensor_copy(gu_half[rows, :], words[rows, :, f]).then_inc(dqs, 1)

            def end_dequant(n):
                v.wait_ge(dqs, (n + 1) * N_STEPS)
                nc.vector.memset(tick[:, 0:1], 0.0).then_inc(dq_ready, 1)

            start_dequant(0, 0)
            for k in range(PARTS):
                dequant(0, 0, k)
            end_dequant(0)

            def slot(s, b, weight, y_tile=None):
                if not isinstance(s, int) or s >= 1:
                    v.wait_ge(at_done, s)
                    if not isinstance(s, int) or s >= 3:
                        v.wait_ge(y_done, s - 2)
                    nc.vector.tensor_scalar(aT[:, 1 - b].rearrange("p a c t -> p (a c t)"), at_ps, 1.0, None,
                                            ALU.mult).then_inc(aT_done, 1)
                v.wait_ge(sg_done, s + 1)
                if y_tile is None:
                    v.wait_ge(wslot_done, s + 1 - NT)
                nc.vector.scalar_tensor_tensor(act[:, b, :], gu_ps[:, 2 + b, 0:I], weight, sg[:, b, :], ALU.mult,
                                               ALU.mult).then_inc(act_done, 1)
                v.wait_ge(ah_done, s + 1)
                nc.vector.tensor_tensor(tile_order_i(acth[:, b, 1, :]), natural_i(act[:, b, :]),
                                        tile_order_i(acth[:, b, 0, :]), ALU.subtract).then_inc(al_done, 1)

            def add_y(i):
                v.wait_ge(y_done, i + 1)
                nc.vector.scalar_tensor_tensor(X[:, i, :], y_ps[i % 2][:, :], 1.0 / W_SCALE, X[:, i, :], ALU.mult,
                                               ALU.add).then_inc(acc_done, 1)

            def part_1(k):
                if k == 0:
                    v.wait_ge(list_ready, E)
                    start_dequant(1, 1)
                dequant(1, 1, k)

            work = {0: [route], 2: [ranks, tables], NT - 4: [lists]}
            for e in range(E):
                work.setdefault(3 + e // 2, []).append(lambda e=e: mark_places(e))
            for k in range(PARTS):
                work.setdefault(NT - PARTS + k, []).append(lambda k=k: part_1(k))
            for i in range(NT):
                slot(i, i % 2, shared_w[:, 0:1], y_tile=i)
                if i:
                    add_y(i - 1)
                for w in work.get(i, []):
                    w()
            end_dequant(1)

            def routed_slot(r, e):
                b = r % 2
                slot(r + NT, b, wslot[:, b, bass.ds(e, 1)])

            def expert(e, buf_next, add_last=False):
                at_e = bass.ds(e, 1)
                first = v.value_load(first_i[0:1, at_e], min_val=0, max_val=SLOTS)
                tiles = v.value_load(tiles_i[0:1, at_e], min_val=1, max_val=KMAX + 1)
                n = e + 2
                routed_slot(first, e)
                if add_last:
                    add_y(NT - 1)
                if buf_next is None:
                    with v.If(tiles > 1):
                        with v.Fori(1, tiles) as k:
                            routed_slot(first + k, e)
                    return
                parts = v.value_load(parts_i[0:1, at_e], min_val=1, max_val=PARTS)
                v.wait_ge(y_done, first + NT)
                start_dequant(n, buf_next)
                with v.Fori(0, parts) as k:
                    dequant(n, buf_next, k)
                later = v.value_load(later_i[0:1, at_e], min_val=0, max_val=PARTS - 1)
                with v.If(later > 0):
                    with v.Fori(0, later) as k:
                        routed_slot(first + k + 1, e)
                        dequant(n, buf_next, nc.s_assert_within(parts + k, 1, PARTS - 1,
                                                                   skip_runtime_bounds_check_because='later = PARTS - parts'))
                end_dequant(n)
                with v.If(tiles > PARTS):
                    with v.Fori(PARTS, tiles) as k:
                        routed_slot(first + k, e)

            v.wait_ge(route_ready, 1)
            expert(0, 0, add_last=True)
            expert(1, 1)
            with v.Fori(1, E // 2 - 1) as h:
                expert(2 * h, 0)
                expert(2 * h + 1, 1)
            expert(E - 2, 0)
            expert(E - 1, None)
            inner = v.value_load(pairs_i[0:1, 0:1], min_val=E // 2 - 2, max_val=SLOTS // 2 - 2)
            v.wait_ge(at_done, 2 * inner + NT + 4)
            nc.vector.tensor_scalar(aT[:, 1].rearrange("p a c t -> p (a c t)"), at_ps, 1.0, None,
                                    ALU.mult).then_inc(aT_done, 1)

        @block.tensor
        def _(pe):
            pe.wait_ge(pool_const, POOL_CONST)
            for b in range(B):
                pe.wait_ge(ld_ctx[b], 16)
                if b >= 2:
                    pe.wait_ge(ctxT_ready, b - 1)
                for t in range(TB):
                    mm = nc.tensor.transpose(tp_ps[b % 2][:, t * P:(t + 1) * P], ctxs[:, b * TB + t, :], id32[:, :])
                mm.then_inc(ctxT_ps_ready, 1)
            pe.wait_ge(wj_ready, 1)
            pe.wait_ge(ld_const, 16 * 6)
            for b in range(B):
                pe.wait_ge(ctxT_ready, b + 1)
                nc.tensor.matmul(sj_ps[b][:, :], wj_all[:, :], ctxT[:, b, :], start=True, stop=True).then_inc(sj_ready, 1)
                for t in range(TB):
                    i = b * TB + t
                    mm = nc.tensor.matmul(si_ps[:, i:i + 1], ctxT[:, b, t * P:(t + 1) * P], wij[:, 0:1], start=True,
                                          stop=True)
            mm.then_inc(si_ps_ready, 1)
            pe.wait_ge(gw_ready, 1)
            for hl in range(2):
                dst = tp_ps[hl][:, 0:HC * E // 2].bitcast(F16)
                for c in range(HC):
                    mm = nc.tensor.transpose(dst[:, c * E:(c + 1) * E], gw_hl[:, hl, c * P:(c + 1) * P], id16[0:E, 0:E])
                mm.then_inc(gwT_ps_ready, 1)
            pe.wait_ge(gwT_ready, 2)

            def transpose_x(i):
                pe.wait_ge(xl_ready, i + 1)
                if i >= 2:
                    pe.wait_ge(xT_ready, i - 1)
                dst = tp_ps[i % 2][:, :].bitcast(F16)
                for k in range(2 * HC):
                    mm = nc.tensor.transpose(dst[:, k * P:(k + 1) * P], xhl[:, i % 2].rearrange("p a h -> p (a h)")[:, k * P:(k + 1) * P],
                                             id16[:, :])
                mm.then_inc(xT_ps_ready, 1)

            def route(i):
                pe.wait_ge(xT_ready, i + 1)
                for k in range(2 * HC):
                    mm = nc.tensor.matmul(lg_ps[:, i * 2 * E:(i + 1) * 2 * E], xT[:, i, k // HC, k % HC, :], gwT[:, k % HC, :],
                                          start=(k == 0), stop=(k == 2 * HC - 1))
                mm.then_inc(lg_ps_ready, 1)
            for i in range(NT):
                transpose_x(i)
                if i:
                    route(i - 1)
            route(NT - 1)

            def gate_up(s, b, x, w, half):
                if half == 0 and (not isinstance(s, int) or s >= 2):
                    pe.wait_ge(act_done, s - 1)
                for c in range(half * HC // 2, (half + 1) * HC // 2):
                    for xp, wp in ((0, 0), (0, 1), (1, 0)):
                        for ps, col in ((g_ps, 0), (u_ps, I)):
                            mm = nc.tensor.matmul(ps[b][:, 0:I], x(xp * HC + c), wgu[:, w, wp, c, col:col + I],
                                                  start=(c == 0 and xp == 0 and wp == 0),
                                                  stop=(c == HC - 1 and xp == 1), skip_group_check=True)
                if half == 1:
                    mm.then_inc(gu_done, 1)

            def transpose_act(s, b):
                pe.wait_ge(ah_done, s + 1)
                pe.wait_ge(al_done, s + 1)
                if not isinstance(s, int) or s >= 1:
                    pe.wait_ge(aT_done, s)
                for hl in range(2):
                    for t in range(IC):
                        k = hl * IC + t
                        mm = nc.tensor.transpose(at_ps[:, k * P:(k + 1) * P], acth[:, b, hl, t * P:(t + 1) * P], id16[:, :])
                mm.then_inc(at_done, 1)

            def down(s, b, w, routed):
                pe.wait_ge(aT_done, s + 1)
                if isinstance(s, int) and 2 <= s < NT + 2:
                    pe.wait_ge(acc_done, s - 1)
                elif not isinstance(s, int) or s >= 2:
                    pe.wait_ge(yev_done, s - 1 - NT)
                n = 0
                for t in range(IC):
                    for ap, wp in ((0, 0), (0, 1), (1, 0)):
                        mm = nc.tensor.matmul(y_ps[b][:, :], aT[:, b, ap, t, :], wdn[:, w, wp, t, :],
                                              start=(n == 0), stop=(n == 3 * IC - 1))
                        n += 1
                mm.then_inc(y_done, 1)

            def transpose_rows(r, b):
                pe.wait_ge(xg_ld[b], 8 * (r - b) + 16)
                if not isinstance(r, int) or r >= 1:
                    pe.wait_ge(xTs_done, r)
                halves = xg[:, b, 0:H].bitcast(F16)
                for k in range(2 * HC):
                    mm = nc.tensor.transpose(xT_ps[:, k * P:(k + 1) * P], halves[:, k * P:(k + 1) * P], id16[:, :])
                mm.then_inc(tx_done, 1)

            def count():
                pe.wait_ge(sel_ready, 1)
                nc.tensor.matmul(rt_ps[:, 0:NT * E], tri[:, :], sel16[:, :], start=True, stop=True)
                nc.tensor.matmul(rt_ps[:, NT * E:2 * NT * E], ones16[:, :], sel16[:, :], start=True,
                                 stop=True).then_inc(count_ready, 1)

            def list_tokens(e):
                pe.wait_ge(onehot_ready, e + 1)
                cells = values.rearrange("p (e i k) -> p e i k", i=NT, k=KMAX)
                for i in range(NT):
                    mm = nc.tensor.matmul(rt_ps[:, e * KMAX:(e + 1) * KMAX], onehot[:, e % 2, i, :], cells[:, e, i, :],
                                          start=(i == 0), stop=(i == NT - 1))
                mm.then_inc(list_ready, 1)

            pe.wait_ge(dq_ready, 1)
            for i in range(NT):
                def x(k, i=i):
                    return xT[:, i, k // HC, k % HC, :]
                b = i % 2
                gate_up(i, b, x, 0, 0)
                if i:
                    transpose_act(i - 1, 1 - b)
                if i == 1:
                    count()
                if 4 <= i < 4 + E // 2:
                    list_tokens(2 * (i - 4))
                    list_tokens(2 * (i - 4) + 1)
                if i == NT - 1:
                    pe.wait_ge(route_ready, 1)
                    transpose_rows(0, 0)
                gate_up(i, b, x, 0, 1)
                if i:
                    down(i - 1, 1 - b, 0, False)

            inner = pe.value_load(pairs_i[0:1, 0:1], min_val=E // 2 - 2, max_val=SLOTS // 2 - 2)

            def slot(r, b, rows=True):
                s = NT + r
                e = pe.value_load(slot_i[0:1, 0, bass.ds(r, 1)], min_val=0, max_val=E - 1)
                w = (e + 1) % 2

                def x(k):
                    return xTs[:, b, k * P:(k + 1) * P]
                pe.wait_ge(dq_ready, e + 2)
                pe.wait_ge(xTs_done, r + 1)
                gate_up(s, b, x, w, 0)
                transpose_act(s - 1, 1 - b)
                if rows:
                    transpose_rows(r + 1, 1 - b)
                gate_up(s, b, x, w, 1)
                if isinstance(r, int) and r == 0:
                    w_prev = 0
                else:
                    e_prev = pe.value_load(slot_i[0:1, 0, bass.ds(r - 1, 1)], min_val=0, max_val=E - 1)
                    w_prev = (e_prev + 1) % 2
                down(s - 1, 1 - b, w_prev, True)
            slot(0, 0)
            slot(1, 1)
            with pe.Fori(1, inner + 1) as j:
                slot(2 * j, 0)
                slot(2 * j + 1, 1)
            slot(2 * inner + 2, 0)
            slot(2 * inner + 3, 1, rows=False)
            transpose_act(2 * inner + 3 + NT, 1)
            e_last = pe.value_load(slot_i[0:1, 0, bass.ds(2 * inner + 3, 1)], min_val=0, max_val=E - 1)
            down(2 * inner + 3 + NT, 1, (e_last + 1) % 2, True)


_NAMES = ["x", "ctx_512", "g_xattn", "g_ffn", "L0_xattn_W", "L0_xattn_b", "L0_ffn_gate_w", "L0_ffn_gate_up_packed",
          "L0_ffn_gate_up_scales", "L0_ffn_down_packed", "L0_ffn_down_scales", "L0_ffn_shared_gate_up_packed",
          "L0_ffn_shared_gate_up_scales", "L0_ffn_shared_down_packed", "L0_ffn_shared_down_scales"]


def kernel(**inputs):
    import numpy as np
    import concourse.bacc as bacc
    from concourse.bass_utils import run_bass_kernel_spmd

    nc = bacc.Bacc("TRN2", target_bir_lowering=False, num_devices=1)
    arrays, args = {}, []
    for name in _NAMES:
        a = np.ascontiguousarray(inputs[name])
        arrays[f"in_{name}"] = a
        args.append(nc.dram_tensor(f"in_{name}", a.shape, mybir.dt.from_np(a.dtype), kind="ExternalInput").ap())
    b, n, h = inputs["x"].shape
    out = nc.dram_tensor("out", (b * n + P, h), F32, kind="ExternalOutput").ap()
    gated_xattn_moe(nc, *args, out)
    r = run_bass_kernel_spmd(nc, [arrays], core_ids=[0])
    return r.results[0]["out"][:b * n].reshape(b, n, h)
```

```python
import math
from contextlib import ExitStack

import concourse.bass as bass
from concourse import mybir

F32, F16 = mybir.dt.float32, mybir.dt.float16
I32, U16 = mybir.dt.int32, mybir.dt.uint16
ALU = mybir.AluOpType
ACT = mybir.ActivationFunctionType
AX = mybir.AxisListType.X

P = 128
LN_EPS = 1e-5
P_ASEM = 0.6
TOP_K = 4
NIB = 8
NIB_HALF = NIB // 2

X_SCALE = 2.0 ** 4
W_SCALE = 2.0 ** 8
R_SCALE = 2.0 ** 6
CODE_SCALE = 2.0 ** 14
SPLITTER = 2.0 ** 15 + 1


def gated_xattn_moe(nc, x, ctx_512, g_xattn, g_ffn, xattn_w, xattn_b, gate_w, gu_packed, gu_scales,
                    dn_packed, dn_scales, sh_gu_packed, sh_gu_scales, sh_dn_packed, sh_dn_scales, out):
    B, S, H = x.shape
    D = ctx_512.shape[2]
    E = gu_packed.shape[0]
    GU = gu_packed.shape[2]
    I = GU // 2
    NT = B * S // P
    TB = S // P
    HC = H // P
    IC = I // P
    GR = H // NIB
    G_GU = gu_scales.shape[1]
    RG = P // NIB
    NE = E + 1
    T = B * S
    ROW = H + E
    KMAX = T // P
    SLOTS = T * TOP_K // P + E
    DUMP = T
    assert D == P and H // G_GU == P and I // dn_scales.shape[1] == P and 2 * GR == P

    x_t = x.rearrange("b (i p) h -> b p i h", p=P)
    out_t = out[0:T].rearrange("(b i p) h -> b p i h", b=B, p=P)
    ctx_t = ctx_512.rearrange("b (i p) d -> b p i d", p=P)

    gu_s_dram = nc.dram_tensor("gu_scale_halves", (2, NE, G_GU, GU), F16, kind="Internal").ap()
    rows_dram = nc.dram_tensor("token_rows", (T + P, ROW), F32, kind="Internal").ap()
    dn_s_dram = nc.dram_tensor("dn_scale_halves", (2, NE, IC, H), F16, kind="Internal").ap()

    with ExitStack() as ctx:
        def sb(name, shape, dt):
            return ctx.enter_context(nc.sbuf_tensor(name, shape, dt))

        def psum(name, shape, dt):
            return ctx.enter_context(nc.psum_tensor(name, shape, dt))

        def sem(name):
            return ctx.enter_context(nc.semaphore(name))

        X = sb("X", [P, NT, H], F32)
        xT = sb("xT", [P, NT, 2, HC, P], F16)
        wgu = sb("wgu", [P, 2, 2, HC, GU], F16)
        wdn = sb("wdn", [P, 2, 2, IC, H], F16)
        gu_raw = sb("gu_raw", [P, 2, GU], I32)
        dn_raw = sb("dn_raw", [P, 2, IC, H], I32)
        gu_sc = sb("gu_sc", [P, 2, 2, GU], F16)
        dn_sc = sb("dn_sc", [P, 2, 2, IC, H], F16)
        gu_half = sb("gu_half", [P, GU], U16)
        dq_sign = sb("dq_sign", [P, GU], U16)
        dq_mag = sb("dq_mag", [P, GU], U16)
        dq_code = sb("dq_code", [P, GU], F16)
        dn_bits = sb("dn_bits", [P, H], I32)
        dn_code = sb("dn_code", [P, H], F16)
        dn_shift = sb("dn_shift", [P, 1], I32)
        sg = sb("sg", [P, 2, I], F32)
        act = sb("act", [P, 2, I], F32)
        acth = sb("acth", [P, 2, 2, I], F16)
        aT = sb("aT", [P, 2, 2, IC, P], F16)
        id16 = sb("id16", [P, P], F16)
        id32 = sb("id32", [P, P], F32)
        room_a = sb("room_a", [P, NT * D], F32)
        ctxs = room_a[:, :].rearrange("p (i d) -> p i d", d=D)
        room_b = sb("room_b", [P, B * S], F32)
        ctxT = room_b[:, :].rearrange("p (b s) -> p b s", b=B)
        wij = sb("wij", [P, 2], F32)
        wj_all = sb("wj_all", [P, P], F32)
        ones = sb("ones", [P, P], F32)
        bias = sb("bias", [P, 1], F32)
        gates = sb("gates", [P, 2], F32)
        tg = sb("tg", [P, 4], F32)
        si = sb("si", [P, NT], F32)
        stats = sb("stats", [P, NT, 6], F32)
        mv = sb("mv", [P, NT, 2], F32)
        stats2 = sb("stats2", [P, NT, 6], F32)
        mv2 = sb("mv2", [P, NT, 2], F32)
        veps = sb("veps", [P, 2, NT], F32)
        rstd = sb("rstd", [P, 2, NT], F32)
        mhalf = sb("mhalf", [P, NT], F32)
        lnA = sb("lnA", [P, NT], F32)
        lnB = sb("lnB", [P, NT], F32)
        xs2 = sb("xs2", [P, NT], F32)
        mix_room = sb("mix_room", [P, 3, 2, H], F32)
        sig, xmix, xn = (mix_room[:, k] for k in range(3))
        ROWS_AHEAD = 4
        xhl = room_a[:, :].bitcast(F16).rearrange("p (b a h) -> p b a h", b=ROWS_AHEAD, a=2)
        gws = xn[0:E, 0, :]
        gw_hl = xn[0:E, 1, :].bitcast(F16).rearrange("e (a h) -> e a h", a=2)
        gwT = sb("gwT", [P, HC, 2 * E], F16)
        lgh = sb("lgh", [P, NT, E], F32)
        lg = sb("lg", [P, NT, E], F32)
        top8 = sb("top8", [P, NT, 8], F32)
        r_gt = sb("r_gt", [P, NT, E], F32)
        r_eq = sb("r_eq", [P, NT, E], F32)
        r_run = sb("r_run", [P, NT, E], F32)
        r_keep = sb("r_keep", [P, NT, E], F32)
        r_need = sb("r_need", [P, NT], F32)
        r_exp = sb("r_exp", [P, NT, E], F32)
        r_sum = sb("r_sum", [P, NT], F32)
        tick = sb("tick", [P, 1], F32)
        pool_tick = sb("pool_tick", [P, 1], F32)
        cw = sb("cw", [P, NT, E], F32)
        shared_w = sb("shared_w", [P, 1], F32)
        zeros = sb("zeros", [P, ROW // 4], F32)
        sc_rows, sd_rows = NE * G_GU, NE * IC
        sc_room = wgu[0:sc_rows, 1].rearrange("p a c n -> p (a c n)")
        sc_all = sc_room[:, 0:2 * GU].bitcast(F32)
        sc_top = sc_room[:, 2 * GU:4 * GU].bitcast(F32)
        sc_h = sc_room[:, 4 * GU:6 * GU].rearrange("p (a n) -> p a n", a=2)
        sd_room = wdn[0:sd_rows, 1].rearrange("p a c n -> p (a c n)")
        sd_all = sd_room[:, 0:2 * H].bitcast(F32)
        sd_top = sd_room[:, 2 * H:4 * H].bitcast(F32)
        sd_h = sd_room[:, 4 * H:6 * H].rearrange("p (a n) -> p a n", a=2)

        onehot = room_a[:, :].bitcast(F16).rearrange("p (b q i) -> p b q i", b=2, i=NT)
        values = mix_room[:, 1:3].rearrange("p k b h -> p (k b h)").bitcast(F16).rearrange("p (k e i) -> p k e i", e=E, i=NT)
        place = sig.rearrange("p b h -> p (b h)").bitcast(F16).rearrange("p (q i) -> p q i", i=NT)
        slot_room = wdn[:, 1].rearrange("p a c n -> p (a c n)")
        slot_ge = slot_room[:, 0:SLOTS * E].rearrange("p (s e) -> p s e", e=E)
        slot_nt = slot_room[:, SLOTS * E:2 * SLOTS * E].rearrange("p (s e) -> p s e", e=E)
        xg = room_b[:, 0:2 * ROW].rearrange("p (b n) -> p b n", b=2)
        at = [2 * ROW]

        def in_room_b(shape, dt):
            n = math.prod(shape[1:])
            piece = room_b[:, at[0]:at[0] + n]
            at[0] += n
            assert at[0] <= B * S
            if dt != F32:
                piece = piece.bitcast(dt)
            return piece.rearrange("p (a b) -> p a b", a=shape[1]) if len(shape) == 3 else piece
        tok = in_room_b([P, E * KMAX + 1], I32)
        tokf = in_room_b([P, E * KMAX], F32)
        tok0 = in_room_b([P, E * KMAX], F32)
        wide = wgu[:, 1].rearrange("p a c n -> p (a c n)")[:, 0:8 * E * NT].bitcast(F32)
        total = wide[:, 0:E * NT].rearrange("p (e i) -> p e i", i=NT)
        rank = wide[:, E * NT:2 * E * NT].rearrange("p (e i) -> p e i", i=NT)
        ranki = wide[:, 2 * E * NT:3 * E * NT].bitcast(I32)
        rankm = wide[:, 3 * E * NT:4 * E * NT].bitcast(I32)
        rank_k = sb("rank_k", [P, E * NT], F16)
        rank_q = sb("rank_q", [P, E, NT], F16)
        tri = sb("tri", [P, P], F16)
        ones16 = sb("ones16", [P, P], F16)
        sel16 = sb("sel16", [P, NT * E], F16)
        token1 = sb("token1", [P, NT], F16)
        dump_row = sb("dump_row", [P, 1], F32)
        tiles_i = sb("tiles_i", [P, E], I32)
        tiles_f = sb("tiles_f", [P, E], F32)
        cum_f = sb("cum_f", [P, E], F32)
        odd_i = sb("odd_i", [P, 1], I32)
        odd_f = sb("odd_f", [P, 1], F32)
        first_f = sb("first_f", [P, E], F32)
        TILES_ROOM = 2 * KMAX
        first_tiles_i = sb("first_tiles_i", [P, E], I32)
        pairs_i = sb("pairs_i", [P, 1], I32)
        slot_f = sb("slot_f", [P, 2, SLOTS], F32)
        slot_i = sb("slot_i", [P, 2, SLOTS], I32)
        iota_s = sb("iota_s", [P, SLOTS], F32)
        idx_g = sb("idx_g", [P, 2], I32)
        idx_s = sb("idx_s", [P, 2], I32)
        wslot = sb("wslot", [P, 2, E], F32)
        xTs = xn.rearrange("p b h -> p (b h)").bitcast(F16).rearrange("p (b n) -> p b n", b=2)
        y_sb = xmix

        gu_ps = psum("gu_ps", [P, 4, 512], F32)
        bank = [gu_ps[:, i, :] for i in range(4)] + [psum(f"bank{i}", [P, 512], F32)[:, :] for i in range(4, 8)]
        g_ps, u_ps = bank[0:2], bank[2:4]
        at_ps = bank[4][:, 0:IC * P].bitcast(F16)
        y_ps = bank[5:7]
        sj_ps = bank[0:4]
        tp_ps = bank[4:6]
        lg_ps = bank[6]
        si_ps = bank[7]
        rt_ps = bank[7]
        xT_ps = bank[7].bitcast(F16)

        ld_const = sem("ld_const")
        ld_x = [sem(f"ld_x{b}") for b in range(B)]
        ld_ctx = [sem(f"ld_ctx{b}") for b in range(B)]
        ld_sc = sem("ld_sc")
        st_sc = sem("st_sc")
        ld_w = [sem("ld_w0"), sem("ld_w1")]
        pool_const = sem("pool_const")
        ctxT_ps_ready = sem("ctxT_ps_ready")
        ctxT_ready = sem("ctxT_ready")
        wj_ready = sem("wj_ready")
        si_ps_ready = sem("si_ps_ready")
        si_ready = sem("si_ready")
        sj_ready = sem("sj_ready")
        tg_ready = sem("tg_ready")
        ve_ready = sem("ve_ready")
        rstd_ready = sem("rstd_ready")
        sig_ready = sem("sig_ready")
        x1_ready = sem("x1_ready")
        xn_ready = sem("xn_ready")
        xh_ready = sem("xh_ready")
        xl_ready = sem("xl_ready")
        xT_ps_ready = sem("xT_ps_ready")
        xT_ready = sem("xT_ready")
        gw_ready = sem("gw_ready")
        gwT_ps_ready = sem("gwT_ps_ready")
        gwT_ready = sem("gwT_ready")
        lg_ps_ready = sem("lg_ps_ready")
        lgh_ready = sem("lgh_ready")
        lsub_ready = sem("lsub_ready")
        exp_ready = sem("exp_ready")
        half_ready = sem("half_ready")
        dqg_ready = sem("dqg_ready")
        dq_ready = sem("dq_ready")
        gu_done = sem("gu_done")
        sg_done = sem("sg_done")
        act_done = sem("act_done")
        ah_done = sem("ah_done")
        al_done = sem("al_done")
        at_done = sem("at_done")
        aT_done = sem("aT_done")
        y_done = sem("y_done")
        acc_done = sem("acc_done")
        vs = sem("vector_step")
        dqs = sem("dequant_step")
        st_out = sem("st_out")
        st_rows = [sem(f"st_rows{k}") for k in range(ROWS_AHEAD)]
        st_cw = sem("st_cw")
        rows_zero = sem("rows_zero")
        sel_ready = sem("sel_ready")
        count_ready = sem("count_ready")
        onehot_ready = sem("onehot_ready")
        place_ready = sem("place_ready")
        ln_ready = sem("ln_ready")
        xmix_ready = sem("xmix_ready")
        list_ready = sem("list_ready")
        route_ready = sem("route_ready")
        cw_ready = sem("cw_ready")
        xg_ld = [sem("xg_ld0"), sem("xg_ld1")]
        tx_done = sem("tx_done")
        xTs_done = sem("xTs_done")
        wslot_done = sem("wslot_done")
        yev_done = sem("yev_done")
        added = sem("added")
        idx_g_ready = sem("idx_g_ready")
        idx_s_ready = sem("idx_s_ready")

        block = ctx.enter_context(nc.Block())

        def tile_order_h(ap):
            return ap.rearrange("p (c f r) -> p r f c", f=2, r=GR)

        def natural_h(ap):
            return ap.rearrange("p (r f c) -> p r f c", f=2, c=HC)

        def tile_order_i(ap):
            return ap.rearrange("p (t j r) -> p t r j", j=NIB, r=RG)

        def natural_i(ap):
            return ap.rearrange("p (t r j) -> p t r j", j=NIB, r=RG)

        def load_expert(sp, gp, dp, buf, n):
            for f in range(2):
                rows = slice(f * GR, (f + 1) * GR)
                sp.dma_start(gu_raw[rows, buf, :].bitcast(U16)[:, 0:2 * GU - f], gp.bitcast(U16)[:, f:])\
                    .then_inc(ld_w[buf], 16)
                for hl in range(2):
                    for g in range(G_GU):
                        r0 = f * GR + g * RG
                        sp.dma_start(gu_sc[r0:r0 + RG, buf, hl, :],
                                     gu_s_dram[hl, n, g].unsqueeze(0).broadcast_to([RG, GU])).then_inc(ld_w[buf], 16)
            for j in range(NIB):
                sp.dma_start(dn_raw[j * RG:(j + 1) * RG, buf, :, :],
                             dp.rearrange("(t r) n -> r t n", r=RG)).then_inc(ld_w[buf], 16)
            for hl in range(2):
                sp.dma_start(dn_sc[:, buf, hl, :, :],
                             dn_s_dram[hl, n].unsqueeze(0).broadcast_to([P, IC, H])).then_inc(ld_w[buf], 16)
        LOADS = 2 * (1 + 2 * G_GU) + NIB + 2

        def loaded(n):
            return 16 * LOADS * (n // 2 + 1)

        POOL_CONST = 14
        SPLIT_STEPS = 10

        @block.sync
        def _(sp):
            for k in range(2):
                sp.dma_start(wij[:, k:k + 1], xattn_w.rearrange("o (k p) -> k p o", p=P)[k],
                             allow_slow_non_contiguous=True).then_inc(ld_const, 16)
            sp.dma_start(bias[:, :], xattn_b.unsqueeze(0).broadcast_to([P, 1])).then_inc(ld_const, 16)
            sp.dma_start(gates[:, 0:1], g_xattn.unsqueeze(0).broadcast_to([P, 1])).then_inc(ld_const, 16)
            sp.dma_start(gates[:, 1:2], g_ffn.unsqueeze(0).broadcast_to([P, 1])).then_inc(ld_const, 16)
            sp.dma_start(gws[:, :], gate_w).then_inc(ld_const, 16)
            sp.dma_start(sc_all[0:G_GU, :], sh_gu_scales).then_inc(ld_sc, 16)
            sp.dma_start(sc_all[G_GU:NE * G_GU, :], gu_scales.rearrange("e g n -> (e g) n")).then_inc(ld_sc, 16)
            sp.dma_start(sd_all[0:IC, :], sh_dn_scales).then_inc(ld_sc, 16)
            sp.dma_start(sd_all[IC:NE * IC, :], dn_scales.rearrange("e g n -> (e g) n")).then_inc(ld_sc, 16)
            for b in range(B):
                sp.dma_start(ctxs[:, b * TB:(b + 1) * TB, :], ctx_t[b]).then_inc(ld_ctx[b], 16)
            for b in range(B):
                sp.dma_start(X[:, b * TB:(b + 1) * TB, :], x_t[b]).then_inc(ld_x[b], 16)
            sp.wait_ge(vs, SPLIT_STEPS)
            for hl in range(2):
                sp.dma_start(gu_s_dram[hl].rearrange("e g n -> (e g) n"), sc_h[:, hl, :]).then_inc(st_sc, 16)
                sp.dma_start(dn_s_dram[hl].rearrange("e g n -> (e g) n"), sd_h[:, hl, :]).then_inc(st_sc, 16)
            sp.wait_ge(st_sc, 64)
            load_expert(sp, sh_gu_packed, sh_dn_packed, 0, 0)
            load_expert(sp, gu_packed[0], dn_packed[0], 1, 1)
            for i in range(NT):
                sp.wait_ge(xh_ready, i + 1)
                sp.wait_ge(xl_ready, i + 1)
                sp.dma_start(rows_dram[i * P:(i + 1) * P, 0:H],
                             xhl[:, i % ROWS_AHEAD].rearrange("p a h -> p (a h)").bitcast(F32))\
                    .then_inc(st_rows[i % ROWS_AHEAD], 16)
            sp.wait_ge(pool_const, POOL_CONST)
            sp.dma_start(rows_dram[T:T + P, :].rearrange("p (a n) -> p a n", a=4),
                         zeros[:, :].unsqueeze(1).broadcast_to([P, 4, ROW // 4])).then_inc(rows_zero, 16)
            sp.dma_start(out[T:T + P, :].rearrange("p (a n) -> p a n", a=4),
                         zeros[:, 0:H // 4].unsqueeze(1).broadcast_to([P, 4, H // 4])).then_inc(st_out, 16)
            sp.wait_ge(cw_ready, 1)
            sp.dma_start(rows_dram[0:T, H:ROW].rearrange("(i p) e -> p i e", p=P), cw[:, :, :])\
                .then_inc(st_cw, 16)
            sp.wait_ge(dq_ready, 1)
            load_expert(sp, gu_packed[1], dn_packed[1], 0, 2)
            for b in range(B):
                sp.wait_ge(acc_done, (b + 1) * TB)
                sp.dma_start(out_t[b], X[:, b * TB:(b + 1) * TB, :]).then_inc(st_out, 16)
            sp.wait_ge(dq_ready, 2)
            load_expert(sp, gu_packed[2], dn_packed[2], 1, 3)
            with sp.Fori(1, E // 2 - 1) as h:
                sp.wait_ge(dq_ready, 2 * h + 1)
                load_expert(sp, gu_packed[2 * h + 1], dn_packed[2 * h + 1], 0, 2 * h + 2)
                sp.wait_ge(dq_ready, 2 * h + 2)
                load_expert(sp, gu_packed[2 * h + 2], dn_packed[2 * h + 2], 1, 2 * h + 3)
            sp.wait_ge(dq_ready, E - 1)
            load_expert(sp, gu_packed[E - 1], dn_packed[E - 1], 0, E)
            sp.wait_ge(st_out, 16 * (B + 1))

        @block.gpsimd
        def _(pool):
            nc.gpsimd.memset(ones[:, :], 1.0).then_inc(pool_const, 1)
            nc.gpsimd.memset(id32[:, :], 0.0).then_inc(pool_const, 1)
            nc.gpsimd.memset(id16[:, :], 0.0).then_inc(pool_const, 1)
            nc.gpsimd.memset(mhalf[:, :], -0.5).then_inc(pool_const, 1)
            nc.gpsimd.iota(dn_shift[:, :], [[0, 1]], base=P - 1, channel_multiplier=-1).then_inc(pool_const, 1)
            nc.gpsimd.memset(zeros[:, :], 0.0).then_inc(pool_const, 1)
            nc.gpsimd.memset(tri[:, :], 1.0).then_inc(pool_const, 1)
            nc.gpsimd.memset(ones16[:, :], 1.0).then_inc(pool_const, 1)
            for dst, pattern, base, mult in ((token1[:, :], [[P, NT]], 1, 1), (dump_row[:, :], [[0, 1]], DUMP + 1, 1),
                                             (iota_s[:, :], [[1, SLOTS]], 0, 0)):
                nc.gpsimd.iota(dst, pattern, base=base, channel_multiplier=mult,
                               allow_small_or_imprecise_dtypes=True).then_inc(pool_const, 1)
            pool.wait_ge(pool_const, 11)
            nc.gpsimd.affine_select(out=tri[:, :], in_=tri[:, :], compare_op=ALU.is_gt, fill=0.0, base=0,
                                    pattern=[[1, P]], channel_multiplier=-1).then_inc(pool_const, 1)
            for ident in (id32, id16):
                nc.gpsimd.affine_select(out=ident[:, :], in_=ident[:, :], compare_op=ALU.not_equal, fill=1.0,
                                        base=0, pattern=[[-1, P]], channel_multiplier=1).then_inc(pool_const, 1)
            def inverse_std(k, b):
                pool.wait_ge(ve_ready, k * B + b + 1)
                cols = slice(b * TB, (b + 1) * TB)
                nc.gpsimd.tensor_tensor(rstd[:, k, cols], veps[:, k, cols], mhalf[:, cols], ALU.pow).then_inc(rstd_ready, 1)

            def scaled_x(b):
                pool.wait_ge(ln_ready, b + 1)
                for i in range(b * TB, (b + 1) * TB):
                    if i >= 2:
                        pool.wait_ge(x1_ready, i - 1)
                    nc.gpsimd.tensor_scalar(xmix[:, i % 2, :], X[:, i, :], lnA[:, i:i + 1], lnB[:, i:i + 1],
                                            ALU.mult, ALU.add).then_inc(xmix_ready, 1)
            for b in range(B):
                inverse_std(0, b)
            for b in range(B):
                scaled_x(b)
                if b:
                    inverse_std(1, b - 1)
            inverse_std(1, B - 1)

            pool.wait_ge(x1_ready, NT)
            nc.gpsimd.iota(place, [[1, P], [0, NT]], base=1, channel_multiplier=0,
                           allow_small_or_imprecise_dtypes=True).then_inc(place_ready, 1)

            pool.wait_ge(rows_zero, 16)
            for k in range(ROWS_AHEAD):
                pool.wait_ge(st_rows[k], 16 * (NT // ROWS_AHEAD))
            pool.wait_ge(st_cw, 16)
            pool.wait_ge(route_ready, 1)
            inner = pool.value_load(pairs_i[0:1, 0:1], min_val=E // 2 - 2, max_val=SLOTS // 2 - 2)

            def hold_wait():
                nc.gpsimd.tensor_tensor(pool_tick[:, :], ones[:, 0:1], ones[:, 0:1], ALU.mult)

            def gather(s, b):
                col = pool.value_load(slot_i[0:1, 1, bass.ds(s, 1)], min_val=0, max_val=E * KMAX)
                if not isinstance(s, int) or s >= 2:
                    pool.wait_ge(tx_done, s - 1)
                    pool.wait_ge(wslot_done, s - 1)
                pool.wait_ge(route_ready, 1)
                nc.gpsimd.tensor_copy(idx_g[:, b:b + 1], tok[:, bass.ds(col, 1)]).then_inc(idx_g_ready, 1)
                pool.wait_ge(idx_g_ready, s + 1)
                hold_wait()
                nc.gpsimd.indirect_dma_start(xg[:, b, :], None, rows_dram[:, :],
                                             bass.IndirectOffsetOnAxis(idx_g[:, b:b + 1], 0)).then_inc(xg_ld[b], 16)

            def add(s, b):
                col = pool.value_load(slot_i[0:1, 1, bass.ds(s, 1)], min_val=0, max_val=E * KMAX)
                pool.wait_ge(yev_done, s + 1)
                if not isinstance(s, int) or s >= 1:
                    pool.wait_ge(added, 16 * s)
                pool.wait_ge(st_out, 16 * (B + 1))
                nc.gpsimd.tensor_copy(idx_s[:, b:b + 1], tok[:, bass.ds(col, 1)]).then_inc(idx_s_ready, 1)
                pool.wait_ge(idx_s_ready, s + 1)
                hold_wait()
                nc.gpsimd.indirect_dma_start(out[:, :], bass.IndirectOffsetOnAxis(idx_s[:, b:b + 1], 0), y_sb[:, b, :],
                                             None, compute_op=ALU.add).then_inc(added, 16)
            for s in range(4):
                gather(s, s % 2)
            with pool.Fori(1, inner + 1) as j:
                for b in range(2):
                    gather(2 * j + b + 2, b)
                    add(2 * j + b - 2, b)
            for k in range(-4, 0):
                add(2 * inner + 4 + k, k % 2)
            pool.wait_ge(added, 32 * inner + 64)

        @block.scalar
        def _(a):
            a.wait_ge(ld_const, 16 * 6)
            nc.scalar.activation(tg[:, 0:2], gates[:, :], ACT.Tanh).then_inc(tg_ready, 1)
            for b in range(B):
                a.wait_ge(ctxT_ps_ready, b + 1)
                nc.scalar.activation(ctxT[:, b, :], tp_ps[b % 2][:, :], ACT.Copy).then_inc(ctxT_ready, 1)
            for hl in range(2):
                a.wait_ge(gwT_ps_ready, hl + 1)
                nc.scalar.activation(gwT[:, :, hl * E:(hl + 1) * E],
                                     tp_ps[hl][:, 0:HC * E // 2].bitcast(F16).rearrange("p (c e) -> p c e", e=E),
                                     ACT.Copy).then_inc(gwT_ready, 1)
            a.wait_ge(si_ready, 1)

            def scores(b):
                a.wait_ge(sj_ready, b + 1)
                for i in range(b * TB, (b + 1) * TB):
                    if i >= 2:
                        a.wait_ge(x1_ready, i - 1)
                    nc.scalar.activation(sig[:, i % 2, :], sj_ps[b][:, :], ACT.Sigmoid,
                                         bias=si[:, i:i + 1]).then_inc(sig_ready, 1)

            def split_x(i):
                a.wait_ge(xn_ready, i + 1)
                if i >= ROWS_AHEAD:
                    a.wait_ge(xT_ps_ready, i - ROWS_AHEAD + 1)
                    a.wait_ge(st_rows[i % ROWS_AHEAD], 16 * (i // ROWS_AHEAD))
                nc.scalar.activation(tile_order_h(xhl[:, i % ROWS_AHEAD, 0, :]), natural_h(xn[:, i % 2, :]),
                                     ACT.Copy).then_inc(xh_ready, 1)

            def copy_xT(i):
                a.wait_ge(xT_ps_ready, i + 1)
                nc.scalar.activation(xT[:, i].rearrange("p a c t -> p (a c t)"), tp_ps[i % 2][:, :].bitcast(F16),
                                     ACT.Copy).then_inc(xT_ready, 1)

            def halves(b):
                for i in range(b * TB, (b + 1) * TB):
                    split_x(i)
                    if i:
                        copy_xT(i - 1)
            for b in range(B):
                scores(b)
                if b:
                    halves(b - 1)
            halves(B - 1)
            copy_xT(NT - 1)

            def route():
                a.wait_ge(lg_ps_ready, NT)
                nc.scalar.activation(lgh[:, :, :], lg_ps[:, :].rearrange("p (t k e) -> p t k e", k=2, e=E)[:, :, 1, :],
                                     ACT.Copy).then_inc(lgh_ready, 1)
                a.wait_ge(lsub_ready, 1)
                nc.scalar.activation(r_exp[:, :, :], lg[:, :, :], ACT.Exp).then_inc(exp_ready, 1)

            def activate(s, b):
                a.wait_ge(gu_done, s + 1)
                if not isinstance(s, int) or s >= 2:
                    a.wait_ge(act_done, s - 1)
                nc.scalar.activation(sg[:, b, :], g_ps[b][:, 0:I], ACT.Silu,
                                     scale=1.0 / (X_SCALE * W_SCALE)).then_inc(sg_done, 1)
                a.wait_ge(act_done, s + 1)
                if not isinstance(s, int) or s >= 2:
                    a.wait_ge(at_done, s - 1)
                nc.scalar.activation(tile_order_i(acth[:, b, 0, :]), natural_i(act[:, b, :]), ACT.Copy).then_inc(ah_done, 1)

            def copy_aT(s, b):
                a.wait_ge(at_done, s + 1)
                if not isinstance(s, int) or s >= 2:
                    a.wait_ge(y_done, s - 1)
                nc.scalar.activation(aT[:, b].rearrange("p a c t -> p (a c t)"), at_ps, ACT.Copy).then_inc(aT_done, 1)

            def take_rows(r, b):
                a.wait_ge(xg_ld[b], 8 * (r - b) + 16)
                if not isinstance(r, int) or r >= 2:
                    a.wait_ge(act_done, NT + r - 1)
                nc.scalar.activation(wslot[:, b, :], xg[:, b, H:ROW], ACT.Copy).then_inc(wslot_done, 1)
                a.wait_ge(tx_done, r + 1)
                if not isinstance(r, int) or r >= 2:
                    a.wait_ge(gu_done, NT + r - 1)
                nc.scalar.activation(xTs[:, b, :], xT_ps, ACT.Copy).then_inc(xTs_done, 1)

            def take_y(r, b):
                a.wait_ge(y_done, NT + r + 1)
                if not isinstance(r, int) or r >= 2:
                    a.wait_ge(added, 16 * (r - 1))
                nc.scalar.activation(y_sb[:, b, :], y_ps[b][:, :], ACT.Copy, scale=1.0 / W_SCALE).then_inc(yev_done, 1)

            route()
            for i in range(NT):
                if i:
                    copy_aT(i - 1, (i - 1) % 2)
                if i == NT - 1:
                    take_rows(0, 0)
                activate(i, i % 2)
            a.wait_ge(route_ready, 1)
            inner = a.value_load(pairs_i[0:1, 0:1], min_val=E // 2 - 2, max_val=SLOTS // 2 - 2)

            def slot(r, b, rows=True):
                copy_aT(r + (NT - 1), 1 - b)
                if rows:
                    take_rows(r + 1, 1 - b)
                activate(NT + r, b)
                if not isinstance(r, int) or r >= 1:
                    take_y(r - 1, 1 - b)
            slot(0, 0)
            slot(1, 1)
            with a.Fori(1, inner + 1) as j:
                slot(2 * j, 0)
                slot(2 * j + 1, 1)
            slot(2 * inner + 2, 0)
            slot(2 * inner + 3, 1, rows=False)
            copy_aT(2 * inner + 3 + NT, 1)
            take_y(2 * inner + 3, 1)

        @block.vector
        def _(v):
            count = [0]

            def step(ins, wait=True):
                count[0] += 1
                ins.then_inc(vs, 1)
                if wait:
                    v.wait_ge(vs, count[0])

            v.wait_ge(ld_const, 16 * 6)
            v.wait_ge(pool_const, POOL_CONST)
            nc.vector.tensor_scalar(wj_all[:, :], ones[:, :], wij[:, 1:2], None, ALU.mult).then_inc(wj_ready, 1)
            v.wait_ge(ld_sc, 64)
            both = []
            for whole, top, half in ((sc_all, sc_top, sc_h), (sd_all, sd_top, sd_h)):
                rest = half[:, :, :].rearrange("p a n -> p (a n)").bitcast(F32)
                both.append((whole, top, half, rest))
            for k, (whole, top, half, rest) in enumerate(both):
                step(nc.vector.tensor_scalar(top[:, :], whole[:, :], SPLITTER, None, ALU.mult), wait=k == 1)
            for k, (whole, top, half, rest) in enumerate(both):
                step(nc.vector.tensor_tensor(rest, top[:, :], whole[:, :], ALU.subtract), wait=k == 1)
            for k, (whole, top, half, rest) in enumerate(both):
                step(nc.vector.tensor_tensor(top[:, :], top[:, :], rest, ALU.subtract), wait=k == 1)
            for k, (whole, top, half, rest) in enumerate(both):
                step(nc.vector.tensor_scalar(half[:, 0, :], top[:, :], W_SCALE, None, ALU.mult), wait=k == 1)
            for k, (whole, top, half, rest) in enumerate(both):
                step(nc.vector.scalar_tensor_tensor(half[:, 1, :], whole[:, :], W_SCALE, half[:, 0, :], ALU.mult,
                                                    ALU.subtract), wait=k == 1)
            assert count[0] == SPLIT_STEPS
            step(nc.vector.tensor_scalar(dn_shift[:, :], dn_shift[:, :], 4, 2, ALU.logical_shift_right,
                                         ALU.logical_shift_left), wait=False)
            step(nc.vector.tensor_scalar(gws[:, :], gws[:, :], R_SCALE, None, ALU.mult))
            step(nc.vector.tensor_copy(tile_order_h(gw_hl[:, 0, :]), natural_h(gws[:, :])))
            nc.vector.tensor_tensor(tile_order_h(gw_hl[:, 1, :]), natural_h(gws[:, :]), tile_order_h(gw_hl[:, 0, :]),
                                    ALU.subtract).then_inc(gw_ready, 1)
            v.wait_ge(tg_ready, 1)
            step(nc.vector.tensor_scalar(tg[:, 2:3], tg[:, 0:1], P_ASEM, None, ALU.mult), wait=False)
            step(nc.vector.tensor_scalar(tg[:, 3:4], tg[:, 0:1], 1.0 - P_ASEM, None, ALU.mult))

            def norm_stats(st, agg, k, b):
                tiles = range(b * TB, (b + 1) * TB)
                for i in tiles:
                    step(nc.vector.bn_stats(st[:, i, :], X[:, i, :]), wait=i == tiles[-1])
                for i in tiles:
                    step(nc.vector.bn_aggr(agg[:, i, :], st[:, i, :]), wait=i == tiles[-1])
                nc.vector.tensor_scalar(veps[:, k, b * TB:(b + 1) * TB], agg[:, b * TB:(b + 1) * TB, 1], LN_EPS, None,
                                        ALU.add).then_inc(ve_ready, 1)

            def x_factors(b):
                v.wait_ge(rstd_ready, b + 1)
                at = slice(b * TB, (b + 1) * TB)
                step(nc.vector.tensor_scalar(lnA[:, at], rstd[:, 0, at], tg[:, 3:4], None, ALU.mult))
                step(nc.vector.tensor_tensor(lnB[:, at], lnA[:, at], mv[:, at, 0], ALU.mult))
                step(nc.vector.tensor_scalar(lnB[:, at], lnB[:, at], -1.0, None, ALU.mult), wait=False)
                nc.vector.tensor_scalar(lnA[:, at], lnA[:, at], 1.0, None, ALU.add).then_inc(ln_ready, 1)

            def attend(b):
                for i in range(b * TB, (b + 1) * TB):
                    v.wait_ge(xmix_ready, i + 1)
                    v.wait_ge(sig_ready, i + 1)
                    nc.vector.scalar_tensor_tensor(X[:, i, :], sig[:, i % 2, :], tg[:, 2:3], xmix[:, i % 2, :],
                                                   ALU.mult, ALU.add).then_inc(x1_ready, 1)
                v.wait_ge(x1_ready, (b + 1) * TB)
                norm_stats(stats2, mv2, 1, b)

            def low_x(i):
                v.wait_ge(xh_ready, i + 1)
                nc.vector.tensor_tensor(tile_order_h(xhl[:, i % ROWS_AHEAD, 1, :]), natural_h(xn[:, i % 2, :]),
                                        tile_order_h(xhl[:, i % ROWS_AHEAD, 0, :]), ALU.subtract).then_inc(xl_ready, 1)

            def normalise(b):
                at = slice(b * TB, (b + 1) * TB)
                v.wait_ge(rstd_ready, B + b + 1)
                step(nc.vector.tensor_scalar(xs2[:, at], rstd[:, 1, at], X_SCALE, None, ALU.mult))
                for i in range(b * TB, (b + 1) * TB):
                    if i >= 2:
                        v.wait_ge(xh_ready, i - 1)
                        v.wait_ge(xl_ready, i - 1)
                    else:
                        v.wait_ge(gwT_ready, 2)
                    nc.vector.tensor_scalar(xn[:, i % 2, :], X[:, i, :], mv2[:, i, 0:1], xs2[:, i:i + 1],
                                            ALU.subtract, ALU.mult).then_inc(xn_ready, 1)
                    if i:
                        low_x(i - 1)
            step(nc.vector.tensor_scalar(shared_w[:, :], tg[:, 1:2], 1.0 / (X_SCALE * W_SCALE), None, ALU.mult))

            def route():
                v.wait_ge(lgh_ready, 1)
                step(nc.vector.tensor_tensor(lg[:, :, :], lg_ps[:, :].rearrange("p (t k e) -> p t k e", k=2, e=E)[:, :, 0, :],
                                             lgh[:, :, :], ALU.add))
                step(nc.vector.tensor_scalar(lg[:, :, :], lg[:, :, :], 1.0 / (X_SCALE * R_SCALE), None, ALU.mult))
                for i in range(NT):
                    step(nc.vector.max(top8[:, i, :], lg[:, i, :]), wait=(i == NT - 1))
                kth = top8[:, :, TOP_K - 1:TOP_K].broadcast_to([P, NT, E])
                step(nc.vector.tensor_tensor(r_gt[:, :, :], lg[:, :, :], kth, ALU.is_gt), wait=False)
                step(nc.vector.tensor_tensor(r_eq[:, :, :], lg[:, :, :], kth, ALU.is_equal))
                nc.vector.tensor_tensor(lg[:, :, :], lg[:, :, :], top8[:, :, 0:1].broadcast_to([P, NT, E]),
                                        ALU.subtract).then_inc(lsub_ready, 1)
                step(nc.vector.tensor_reduce(r_need[:, :], r_gt[:, :, :], AX, ALU.add), wait=False)
                step(nc.vector.memset(r_keep[:, :, :], 1.0))
                step(nc.vector.memset(r_keep[:, :, 0:1], 0.0))
                step(nc.vector.tensor_tensor_scan(r_run[:, :, :].rearrange("p t e -> p (t e)"),
                                                  r_keep[:, :, :].rearrange("p t e -> p (t e)"),
                                                  r_eq[:, :, :].rearrange("p t e -> p (t e)"), 0.0, ALU.mult, ALU.add))
                step(nc.vector.tensor_tensor(r_run[:, :, :], r_run[:, :, :],
                                             r_need[:, :].unsqueeze(2).broadcast_to([P, NT, E]), ALU.add))
                step(nc.vector.tensor_scalar(r_run[:, :, :], r_run[:, :, :], float(TOP_K), None, ALU.is_le))
                step(nc.vector.tensor_tensor(r_eq[:, :, :], r_eq[:, :, :], r_run[:, :, :], ALU.mult))
                step(nc.vector.tensor_tensor(r_gt[:, :, :], r_gt[:, :, :], r_eq[:, :, :], ALU.add))
                nc.vector.tensor_copy(sel16[:, :], r_gt[:, :, :].rearrange("p t e -> p (t e)")).then_inc(sel_ready, 1)
                v.wait_ge(exp_ready, 1)
                step(nc.vector.tensor_tensor(r_exp[:, :, :], r_exp[:, :, :], r_gt[:, :, :], ALU.mult))
                step(nc.vector.tensor_reduce(r_sum[:, :], r_exp[:, :, :], AX, ALU.add))
                step(nc.vector.reciprocal(r_sum[:, :], r_sum[:, :]))
                step(nc.vector.tensor_scalar(r_sum[:, :], r_sum[:, :], shared_w[:, 0:1], None, ALU.mult))
                nc.vector.tensor_tensor(cw[:, :, :], r_exp[:, :, :], r_sum[:, :].unsqueeze(2).broadcast_to([P, NT, E]),
                                        ALU.mult).then_inc(cw_ready, 1)

            def ranks():
                v.wait_ge(count_ready, 1)
                step(nc.vector.tensor_copy(total, rt_ps[:, NT * E:2 * NT * E].rearrange("p (i e) -> p e i", e=E)))
                step(nc.vector.tensor_tensor_scan(r_run[:, :, :].rearrange("p e i -> p (e i)"),
                                                  r_keep[:, :, :].rearrange("p e i -> p (e i)"),
                                                  total.rearrange("p e i -> p (e i)"), 0.0, ALU.mult, ALU.add))
                step(nc.vector.tensor_tensor(rank, r_run[:, :, :], total, ALU.subtract))
                step(nc.vector.tensor_tensor(ranki.rearrange("p (e i) -> p e i", i=NT), rank,
                                             rt_ps[:, 0:NT * E].rearrange("p (i e) -> p e i", e=E), ALU.add))
                step(nc.vector.tensor_scalar(rankm, ranki, 7, None, ALU.logical_shift_right))
                step(nc.vector.tensor_copy(rank_k[:, :], rankm))
                step(nc.vector.tensor_scalar(ranki, ranki, P - 1, None, ALU.bitwise_and))
                step(nc.vector.scalar_tensor_tensor(rank_q[:, :, :], ranki.rearrange("p (e i) -> p e i", i=NT), 1.0,
                                                    r_gt[:, :, :].rearrange("p i e -> p e i"), ALU.add, ALU.mult), wait=False)

            def token_values():
                for k in range(KMAX):
                    step(nc.vector.tensor_scalar(values[:, k].rearrange("p e i -> p (e i)"), rank_k[:, :], float(k), None,
                                                 ALU.is_equal), wait=k == KMAX - 1)
                cells = values.rearrange("p k e i -> p (k e) i")
                step(nc.vector.tensor_tensor(cells, cells, token1[:, :].unsqueeze(1).broadcast_to([P, KMAX * E, NT]),
                                             ALU.mult))

            def tables():
                step(nc.vector.tensor_scalar(tiles_i[:, :], r_run[:, :, NT - 1], float(P - 1), None, ALU.add))
                step(nc.vector.tensor_scalar(tiles_i[:, :], tiles_i[:, :], 7, None, ALU.logical_shift_right))
                step(nc.vector.tensor_scalar(tiles_f[:, :], tiles_i[:, :], 1.0, None, ALU.max))
                step(nc.vector.tensor_tensor_scan(cum_f[:, :], ones[:, 0:E], tiles_f[:, :], 0.0, ALU.mult, ALU.add))
                step(nc.vector.tensor_copy(odd_i[:, :], cum_f[:, E - 1:E]))
                step(nc.vector.tensor_scalar(odd_i[:, :], odd_i[:, :], 1, None, ALU.bitwise_and))
                step(nc.vector.tensor_copy(odd_f[:, :], odd_i[:, :]))
                for t in (tiles_f, cum_f):
                    step(nc.vector.tensor_tensor(t[:, E - 1:E], t[:, E - 1:E], odd_f[:, :], ALU.add))
                step(nc.vector.tensor_tensor(first_f[:, :], cum_f[:, :], tiles_f[:, :], ALU.subtract), wait=False)
                step(nc.vector.tensor_scalar(pairs_i[:, :], cum_f[:, E - 1:E], 0.5, -2.0, ALU.mult, ALU.add))
                step(nc.vector.scalar_tensor_tensor(first_tiles_i[:, :], first_f[:, :], float(TILES_ROOM), tiles_f[:, :],
                                                    ALU.mult, ALU.add))

            def slot_tables(part):
                by_expert = [P, SLOTS, E]
                if part == 0:
                    step(nc.vector.tensor_tensor(slot_ge, iota_s[:, :].unsqueeze(2).broadcast_to(by_expert),
                                                 cum_f[:, :].unsqueeze(1).broadcast_to(by_expert), ALU.is_ge))
                elif part == 1:
                    step(nc.vector.tensor_tensor(slot_nt, slot_ge, tiles_f[:, :].unsqueeze(1).broadcast_to(by_expert),
                                                 ALU.mult))
                elif part == 2:
                    step(nc.vector.tensor_reduce(slot_f[:, 0, :], slot_ge, AX, ALU.add))
                    step(nc.vector.tensor_copy(slot_i[:, 0, :], slot_f[:, 0, :]), wait=False)
                else:
                    step(nc.vector.tensor_reduce(slot_f[:, 1, :], slot_nt, AX, ALU.add))
                    step(nc.vector.scalar_tensor_tensor(slot_f[:, 1, :], slot_f[:, 0, :], float(KMAX), slot_f[:, 1, :],
                                                        ALU.mult, ALU.subtract))
                    step(nc.vector.tensor_tensor(slot_i[:, 1, :], slot_f[:, 1, :], iota_s[:, :], ALU.add))

            def lists():
                v.wait_ge(list_ready, E)
                ps = rt_ps[:, 0:E * KMAX]
                step(nc.vector.tensor_scalar(tok0, ps, 0.0, None, ALU.is_equal))
                step(nc.vector.scalar_tensor_tensor(tokf, tok0, dump_row[:, 0:1], ps, ALU.mult, ALU.add))
                step(nc.vector.tensor_scalar(tok[:, 0:E * KMAX], tokf, -1.0, None, ALU.add))
                step(nc.vector.tensor_scalar(tok[:, E * KMAX:], dump_row[:, :], -1.0, None, ALU.add))
                nc.vector.memset(tick[:, 0:1], 0.0).then_inc(route_ready, 1)

            PARTS = HC
            COLS = IC * H // PARTS
            G_STEPS, D_STEPS = 7, 5
            N_STEPS = 1 + PARTS * (G_STEPS + D_STEPS)

            def dequant(n, buf, g, d, fill=None, free=None):
                if d is None:
                    done = n * N_STEPS + 1
                elif g is None:
                    done = (n + 1) * N_STEPS - D_STEPS
                else:
                    done = n * N_STEPS + 1 + G_STEPS + d * (G_STEPS + D_STEPS)
                at = [0]

                def link(ins, wait=True):
                    at[0] += 1
                    ins.then_inc(dqs, 1)
                    if wait:
                        v.wait_ge(dqs, done + at[0])
                v.wait_ge(dqs, done)
                if g is not None:
                    c = HC - 1 - g
                    link(nc.vector.tensor_scalar(dq_sign[:, :], gu_half[:, :], 0x8000, None, ALU.bitwise_and), wait=False)
                    link(nc.vector.tensor_scalar(dq_mag[:, :], gu_half[:, :], 3, 0x0E00, ALU.logical_shift_right,
                                                 ALU.bitwise_and), wait=d is None)
                if d is not None:
                    cols = slice(d * COLS, (d + 1) * COLS) if isinstance(d, int) else bass.ds(d * COLS, COLS)
                    raw = dn_raw[:, buf].rearrange("p t n -> p (t n)")[:, cols]
                    link(nc.vector.tensor_scalar(dn_bits[:, 0:COLS], raw, dn_shift[:, 0:1], None,
                                                 ALU.logical_shift_left))
                if g is not None:
                    link(nc.vector.tensor_tensor(dq_mag[:, :], dq_mag[:, :], dq_sign[:, :], ALU.bitwise_or),
                         wait=d is None)
                if fill:
                    fill()
                if d is not None:
                    link(nc.vector.tensor_scalar(dn_bits[:, 0:COLS], dn_bits[:, 0:COLS], 3, 0x8E000000 - (1 << 32),
                                                 ALU.arith_shift_right, ALU.bitwise_and))
                if g is not None:
                    link(nc.vector.tensor_scalar(dq_code[:, :], dq_mag[:, :].bitcast(F16), CODE_SCALE, None, ALU.mult),
                         wait=d is None)
                if d is not None:
                    link(nc.vector.tensor_scalar(dn_code[:, 0:COLS],
                                                 dn_bits[:, 0:COLS].bitcast(F16).rearrange("p (n f) -> p n f", f=2)[:, :, 1],
                                                 CODE_SCALE, None, ALU.mult))
                if g is not None:
                    link(nc.vector.tensor_scalar(gu_half[:, :], gu_half[:, :], 4, None, ALU.logical_shift_left), wait=False)
                    for hl in range(2):
                        link(nc.vector.tensor_tensor(wgu[:, buf, hl, c, :], dq_code[:, :], gu_sc[:, buf, hl, :], ALU.mult),
                             wait=False)
                if d is not None:
                    if free is not None:
                        v.wait_ge(y_done, free)
                    for hl in range(2):
                        link(nc.vector.tensor_tensor(wdn[:, buf, hl].rearrange("p t n -> p (t n)")[:, cols],
                                                     dn_code[:, 0:COLS],
                                                     dn_sc[:, buf, hl].rearrange("p t n -> p (t n)")[:, cols], ALU.mult),
                             wait=False)
                assert at[0] == (g is not None) * G_STEPS + (d is not None) * D_STEPS

            def start_dequant(n, buf):
                if not isinstance(n, int) or n:
                    v.wait_ge(dqs, n * N_STEPS)
                v.wait_ge(ld_w[buf], loaded(n))
                words = gu_raw[:, buf, :].bitcast(U16).rearrange("p (n f) -> p n f", f=2)
                nc.vector.tensor_copy(gu_half[:, :], words[:, :, 0]).then_inc(dqs, 1)
                dequant(n, buf, 0, None)

            def end_gate_up(n):
                v.wait_ge(dqs, (n + 1) * N_STEPS - D_STEPS)
                nc.vector.memset(tick[:, 0:1], 0.0).then_inc(dqg_ready, 1)

            def end_dequant(n):
                v.wait_ge(dqs, (n + 1) * N_STEPS)
                nc.vector.memset(tick[:, 0:1], 0.0).then_inc(dq_ready, 1)

            for b in range(B):
                v.wait_ge(ld_x[b], 16)
                norm_stats(stats, mv, 0, b)
                if b:
                    x_factors(b - 1)
            v.wait_ge(si_ps_ready, 1)
            nc.vector.tensor_scalar(si[:, :], si_ps[:, 0:NT], bias[:, 0:1], None, ALU.add).then_inc(si_ready, 1)
            x_factors(B - 1)
            for b in range(B):
                attend(b)
                if b == 1:
                    start_dequant(0, 0)
                elif b > 1:
                    dequant(0, 0, b - 1, b - 2)
                if b:
                    normalise(b - 1)
            dequant(0, 0, PARTS - 1, PARTS - 2)
            end_gate_up(0)
            normalise(B - 1)
            low_x(NT - 1)
            dequant(0, 0, None, PARTS - 1)
            end_dequant(0)

            def activations(s, b, weight):
                if not isinstance(s, int) or s >= 2:
                    v.wait_ge(at_done, s - 1)
                v.wait_ge(sg_done, s + 1)
                nc.vector.scalar_tensor_tensor(act[:, b, :], gu_ps[:, 2 + b, 0:I], weight, sg[:, b, :], ALU.mult,
                                               ALU.mult).then_inc(act_done, 1)

            def low_halves(s, b):
                v.wait_ge(ah_done, s + 1)
                nc.vector.tensor_tensor(tile_order_i(acth[:, b, 1, :]), natural_i(act[:, b, :]),
                                        tile_order_i(acth[:, b, 0, :]), ALU.subtract).then_inc(al_done, 1)

            def add_y(i):
                v.wait_ge(y_done, i + 1)
                nc.vector.scalar_tensor_tensor(X[:, i, :], y_ps[i % 2][:, :], 1.0 / W_SCALE, X[:, i, :], ALU.mult,
                                               ALU.add).then_inc(acc_done, 1)

            def first_weights(k):
                if k == 0:
                    start_dequant(1, 1)
                elif k < PARTS:
                    dequant(1, 1, k, k - 1)
                else:
                    end_gate_up(1)
                    dequant(1, 1, None, PARTS - 1)
                    end_dequant(1)
                    start_dequant(2, 0)

            def mark(e):
                if e >= 2:
                    v.wait_ge(list_ready, e - 1)
                else:
                    v.wait_ge(place_ready, 1)
                    for k in range(ROWS_AHEAD):
                        v.wait_ge(st_rows[k], 16 * (NT // ROWS_AHEAD))
                nc.vector.tensor_tensor(onehot[:, e % 2], rank_q[:, e, :].unsqueeze(1).broadcast_to([P, P, NT]), place,
                                        ALU.is_equal).then_inc(onehot_ready, 1)
            work = {1: [ranks], 2: [token_values], 3: [tables], NT - 4: [lambda: first_weights(1), lists]}
            for e in range(E):
                work.setdefault(3 + e // 2, []).append(lambda e=e: mark(e))
            for k in range(4):
                work[4 + k].append(lambda k=k: slot_tables(k))
            work[8].append(lambda: first_weights(0))
            for k in range(2, PARTS + 1):
                work.setdefault(NT - 5 + k, []).append(lambda k=k: first_weights(k))
            route()
            for i in range(NT):
                activations(i, i % 2, shared_w[:, 0:1])
                low_halves(i, i % 2)
                if i:
                    add_y(i - 1)
                for w in work.get(i, []):
                    w()

            def head(r, e):
                b = r % 2
                v.wait_ge(wslot_done, r + 1)
                activations(r + NT, b, wslot[:, b, bass.ds(e, 1)])

            def routed_slot(r, e):
                head(r, e)
                low_halves(r + NT, r % 2)

            def expert(e, buf_next, add_last=False):
                at_e = bass.ds(e, 1)
                both = v.value_load(first_tiles_i[0:1, at_e], min_val=1, max_val=(SLOTS + 1) * TILES_ROOM - 1)
                first, tiles = both // TILES_ROOM, both % TILES_ROOM
                n = e + 2
                if buf_next is None:
                    routed_slot(first, e)
                    with v.If(tiles > 1):
                        with v.Fori(1, tiles) as k:
                            routed_slot(first + k, e)
                    return
                head(first, e)
                dequant(n, buf_next, 1, 0, fill=lambda: low_halves(first + NT, first % 2), free=first + NT)
                if add_last:
                    add_y(NT - 1)
                for k in range(1, PARTS - 1):
                    with v.If(tiles > k):
                        head(first + k, e)
                        dequant(n, buf_next, k + 1, k, fill=lambda: low_halves(first + k + NT, (first + k) % 2))
                    with v.Else():
                        dequant(n, buf_next, k + 1, k)
                end_gate_up(n)
                with v.If(tiles > PARTS - 1):
                    routed_slot(first + PARTS - 1, e)
                dequant(n, buf_next, None, PARTS - 1)
                end_dequant(n)
                with v.If(tiles > PARTS):
                    with v.Fori(PARTS, tiles) as k:
                        routed_slot(first + k, e)
                if not isinstance(e, int) or e < E - 2:
                    start_dequant(n + 1, 1 - buf_next)

            v.wait_ge(route_ready, 1)
            expert(0, 0, add_last=True)
            expert(1, 1)
            with v.Fori(1, E // 2 - 1) as h:
                expert(2 * h, 0)
                expert(2 * h + 1, 1)
            expert(E - 2, 0)
            expert(E - 1, None)

        @block.tensor
        def _(pe):
            pe.wait_ge(pool_const, POOL_CONST)
            for b in range(B):
                pe.wait_ge(ld_ctx[b], 16)
                if b >= 2:
                    pe.wait_ge(ctxT_ready, b - 1)
                for t in range(TB):
                    mm = nc.tensor.transpose(tp_ps[b % 2][:, t * P:(t + 1) * P], ctxs[:, b * TB + t, :], id32[:, :])
                mm.then_inc(ctxT_ps_ready, 1)
            pe.wait_ge(wj_ready, 1)
            pe.wait_ge(ld_const, 16 * 6)
            for b in range(B):
                pe.wait_ge(ctxT_ready, b + 1)
                nc.tensor.matmul(sj_ps[b][:, :], wj_all[:, :], ctxT[:, b, :], start=True, stop=True).then_inc(sj_ready, 1)
                for t in range(TB):
                    i = b * TB + t
                    mm = nc.tensor.matmul(si_ps[:, i:i + 1], ctxT[:, b, t * P:(t + 1) * P], wij[:, 0:1], start=True,
                                          stop=True)
            mm.then_inc(si_ps_ready, 1)
            pe.wait_ge(gw_ready, 1)
            for hl in range(2):
                dst = tp_ps[hl][:, 0:HC * E // 2].bitcast(F16)
                for c in range(HC):
                    mm = nc.tensor.transpose(dst[:, c * E:(c + 1) * E], gw_hl[:, hl, c * P:(c + 1) * P], id16[0:E, 0:E])
                mm.then_inc(gwT_ps_ready, 1)
            pe.wait_ge(gwT_ready, 2)

            def transpose_x(i):
                pe.wait_ge(xl_ready, i + 1)
                if i >= 2:
                    pe.wait_ge(xT_ready, i - 1)
                dst = tp_ps[i % 2][:, :].bitcast(F16)
                for k in range(2 * HC):
                    mm = nc.tensor.transpose(dst[:, k * P:(k + 1) * P], xhl[:, i % ROWS_AHEAD].rearrange("p a h -> p (a h)")[:, k * P:(k + 1) * P],
                                             id16[:, :])
                mm.then_inc(xT_ps_ready, 1)

            def route(i):
                pe.wait_ge(xT_ready, i + 1)
                for k in range(2 * HC):
                    mm = nc.tensor.matmul(lg_ps[:, i * 2 * E:(i + 1) * 2 * E], xT[:, i, k // HC, k % HC, :], gwT[:, k % HC, :],
                                          start=(k == 0), stop=(k == 2 * HC - 1))
                mm.then_inc(lg_ps_ready, 1)
            for i in range(NT):
                transpose_x(i)
                if i:
                    route(i - 1)
            route(NT - 1)

            def gate_up(s, b, x, w, half):
                if half == 0 and (not isinstance(s, int) or s >= 2):
                    pe.wait_ge(act_done, s - 1)
                for c in range(half * HC // 2, (half + 1) * HC // 2):
                    for xp, wp in ((0, 0), (0, 1), (1, 0)):
                        for ps, col in ((g_ps, 0), (u_ps, I)):
                            mm = nc.tensor.matmul(ps[b][:, 0:I], x(xp * HC + c), wgu[:, w, wp, c, col:col + I],
                                                  start=(c == 0 and xp == 0 and wp == 0),
                                                  stop=(c == HC - 1 and xp == 1), skip_group_check=True)
                if half == 1:
                    mm.then_inc(gu_done, 1)

            def transpose_act(s, b):
                pe.wait_ge(ah_done, s + 1)
                pe.wait_ge(al_done, s + 1)
                if not isinstance(s, int) or s >= 1:
                    pe.wait_ge(aT_done, s)
                for hl in range(2):
                    for t in range(IC):
                        k = hl * IC + t
                        mm = nc.tensor.transpose(at_ps[:, k * P:(k + 1) * P], acth[:, b, hl, t * P:(t + 1) * P], id16[:, :])
                mm.then_inc(at_done, 1)

            def down(s, b, w, routed):
                pe.wait_ge(aT_done, s + 1)
                if isinstance(s, int) and 2 <= s < NT + 2:
                    pe.wait_ge(acc_done, s - 1)
                elif not isinstance(s, int) or s >= 2:
                    pe.wait_ge(yev_done, s - 1 - NT)
                n = 0
                for t in range(IC):
                    for ap, wp in ((0, 0), (0, 1), (1, 0)):
                        mm = nc.tensor.matmul(y_ps[b][:, :], aT[:, b, ap, t, :], wdn[:, w, wp, t, :],
                                              start=(n == 0), stop=(n == 3 * IC - 1))
                        n += 1
                mm.then_inc(y_done, 1)

            def transpose_rows(r, b):
                pe.wait_ge(xg_ld[b], 8 * (r - b) + 16)
                if not isinstance(r, int) or r >= 1:
                    pe.wait_ge(xTs_done, r)
                halves = xg[:, b, 0:H].bitcast(F16)
                for k in range(2 * HC):
                    mm = nc.tensor.transpose(xT_ps[:, k * P:(k + 1) * P], halves[:, k * P:(k + 1) * P], id16[:, :])
                mm.then_inc(tx_done, 1)

            def count():
                pe.wait_ge(sel_ready, 1)
                nc.tensor.matmul(rt_ps[:, 0:NT * E], tri[:, :], sel16[:, :], start=True, stop=True)
                nc.tensor.matmul(rt_ps[:, NT * E:2 * NT * E], ones16[:, :], sel16[:, :], start=True,
                                 stop=True).then_inc(count_ready, 1)

            def list_tokens(e):
                pe.wait_ge(onehot_ready, e + 1)
                for i in range(NT):
                    mm = nc.tensor.matmul(rt_ps[:, e * KMAX:(e + 1) * KMAX], onehot[:, e % 2, :, i], values[:, :, e, i],
                                          start=(i == 0), stop=(i == NT - 1))
                mm.then_inc(list_ready, 1)

            pe.wait_ge(dqg_ready, 1)
            for i in range(NT):
                def x(k, i=i):
                    return xT[:, i, k // HC, k % HC, :]
                b = i % 2
                gate_up(i, b, x, 0, 0)
                if i:
                    transpose_act(i - 1, 1 - b)
                if i == 1:
                    count()
                if i == NT - 1:
                    pe.wait_ge(route_ready, 1)
                    transpose_rows(0, 0)
                gate_up(i, b, x, 0, 1)
                if i == 1:
                    pe.wait_ge(dq_ready, 1)
                if i:
                    down(i - 1, 1 - b, 0, False)
                if 4 <= i < 4 + E // 2:
                    list_tokens(2 * (i - 4))
                    list_tokens(2 * (i - 4) + 1)

            inner = pe.value_load(pairs_i[0:1, 0:1], min_val=E // 2 - 2, max_val=SLOTS // 2 - 2)

            def slot(r, b, rows=True):
                s = NT + r
                e = pe.value_load(slot_i[0:1, 0, bass.ds(r, 1)], min_val=0, max_val=E - 1)
                w = (e + 1) % 2

                def x(k):
                    return xTs[:, b, k * P:(k + 1) * P]
                pe.wait_ge(dqg_ready, e + 2)
                pe.wait_ge(xTs_done, r + 1)
                gate_up(s, b, x, w, 0)
                transpose_act(s - 1, 1 - b)
                if rows:
                    transpose_rows(r + 1, 1 - b)
                gate_up(s, b, x, w, 1)
                if isinstance(r, int) and r == 0:
                    w_prev = 0
                else:
                    e_prev = pe.value_load(slot_i[0:1, 0, bass.ds(r - 1, 1)], min_val=0, max_val=E - 1)
                    w_prev = (e_prev + 1) % 2
                    pe.wait_ge(dq_ready, e_prev + 2)
                down(s - 1, 1 - b, w_prev, True)
            slot(0, 0)
            slot(1, 1)
            with pe.Fori(1, inner + 1) as j:
                slot(2 * j, 0)
                slot(2 * j + 1, 1)
            slot(2 * inner + 2, 0)
            slot(2 * inner + 3, 1, rows=False)
            transpose_act(2 * inner + 3 + NT, 1)
            e_last = pe.value_load(slot_i[0:1, 0, bass.ds(2 * inner + 3, 1)], min_val=0, max_val=E - 1)
            down(2 * inner + 3 + NT, 1, (e_last + 1) % 2, True)


_NAMES = ["x", "ctx_512", "g_xattn", "g_ffn", "L0_xattn_W", "L0_xattn_b", "L0_ffn_gate_w", "L0_ffn_gate_up_packed",
          "L0_ffn_gate_up_scales", "L0_ffn_down_packed", "L0_ffn_down_scales", "L0_ffn_shared_gate_up_packed",
          "L0_ffn_shared_gate_up_scales", "L0_ffn_shared_down_packed", "L0_ffn_shared_down_scales"]


def kernel(**inputs):
    import numpy as np
    import concourse.bacc as bacc
    from concourse.bass_utils import run_bass_kernel_spmd

    nc = bacc.Bacc("TRN2", target_bir_lowering=False, num_devices=1)
    arrays, args = {}, []
    for name in _NAMES:
        a = np.ascontiguousarray(inputs[name])
        arrays[f"in_{name}"] = a
        args.append(nc.dram_tensor(f"in_{name}", a.shape, mybir.dt.from_np(a.dtype), kind="ExternalInput").ap())
    b, n, h = inputs["x"].shape
    out = nc.dram_tensor("out", (b * n + P, h), F32, kind="ExternalOutput").ap()
    gated_xattn_moe(nc, *args, out)
    r = run_bass_kernel_spmd(nc, [arrays], core_ids=[0])
    return r.results[0]["out"][:b * n].reshape(b, n, h)
```

```python
import math
from contextlib import ExitStack

import concourse.bass as bass
from concourse import mybir

F32, F16 = mybir.dt.float32, mybir.dt.float16
I32, U16 = mybir.dt.int32, mybir.dt.uint16
ALU = mybir.AluOpType
ACT = mybir.ActivationFunctionType
AX = mybir.AxisListType.X

P = 128
LN_EPS = 1e-5
P_ASEM = 0.6
TOP_K = 4
NIB = 8
NIB_HALF = NIB // 2

X_SCALE = 2.0 ** 4
W_SCALE = 2.0 ** 8
R_SCALE = 2.0 ** 6
CODE_SCALE = 2.0 ** 14
SPLITTER = 2.0 ** 15 + 1


def gated_xattn_moe(nc, x, ctx_512, g_xattn, g_ffn, xattn_w, xattn_b, gate_w, gu_packed, gu_scales,
                    dn_packed, dn_scales, sh_gu_packed, sh_gu_scales, sh_dn_packed, sh_dn_scales, out):
    B, S, H = x.shape
    D = ctx_512.shape[2]
    E = gu_packed.shape[0]
    GU = gu_packed.shape[2]
    I = GU // 2
    NT = B * S // P
    TB = S // P
    HC = H // P
    IC = I // P
    GR = H // NIB
    G_GU = gu_scales.shape[1]
    RG = P // NIB
    NE = E + 1
    T = B * S
    ROW = H + E
    KMAX = T // P
    SLOTS = T * TOP_K // P + E
    DUMP = T
    assert B == 4
    assert T <= 2048
    assert D == P and H // G_GU == P and I // dn_scales.shape[1] == P and 2 * GR == P

    x_t = x.rearrange("b (i p) h -> b p i h", p=P)
    out_t = out[0:T].rearrange("(b i p) h -> b p i h", b=B, p=P)
    ctx_t = ctx_512.rearrange("b (i p) d -> b p i d", p=P)

    gu_s_dram = nc.dram_tensor("gu_scale_halves", (2, NE, G_GU, GU), F16, kind="Internal").ap()
    rows_dram = nc.dram_tensor("token_rows", (T + P, ROW), F32, kind="Internal").ap()
    dn_s_dram = nc.dram_tensor("dn_scale_halves", (2, NE, IC, H), F16, kind="Internal").ap()

    with ExitStack() as ctx:
        def sb(name, shape, dt):
            return ctx.enter_context(nc.sbuf_tensor(name, shape, dt))

        def psum(name, shape, dt):
            return ctx.enter_context(nc.psum_tensor(name, shape, dt))

        def sem(name):
            return ctx.enter_context(nc.semaphore(name))

        X = sb("X", [P, NT, H], F32)
        xT = sb("xT", [P, NT, 2, HC, P], F16)
        wgu = sb("wgu", [P, 2, 2, HC, GU], F16)
        wdn = sb("wdn", [P, 2, 2, IC, H], F16)
        gu_raw = sb("gu_raw", [P, 2, GU], I32)
        dn_raw = sb("dn_raw", [P, 2, IC, H], I32)
        gu_sc = sb("gu_sc", [P, 2, 2, GU], F16)
        dn_sc = sb("dn_sc", [P, 2, 2, IC, H], F16)
        gu_half = sb("gu_half", [P, GU], U16)
        dq_sign = sb("dq_sign", [P, GU], U16)
        dq_mag = sb("dq_mag", [P, GU], U16)
        dq_code = sb("dq_code", [P, GU], F16)
        dn_bits = sb("dn_bits", [P, H], I32)
        dn_code = sb("dn_code", [P, H], F16)
        dn_shift = sb("dn_shift", [P, 1], I32)
        sg = sb("sg", [P, 2, I], F32)
        act = sb("act", [P, 2, I], F32)
        acth = sb("acth", [P, 2, 2, I], F16)
        aT = sb("aT", [P, 2, 2, IC, P], F16)
        id16 = sb("id16", [P, P], F16)
        id32 = sb("id32", [P, P], F32)
        room_a = sb("room_a", [P, NT * D], F32)
        ctxs = room_a[:, :].rearrange("p (i d) -> p i d", d=D)
        room_b = sb("room_b", [P, B * S], F32)
        ctxT = room_b[:, :].rearrange("p (b s) -> p b s", b=B)
        wij = sb("wij", [P, 2], F32)
        wj_all = sb("wj_all", [P, P], F32)
        ones = sb("ones", [P, P], F32)
        bias = sb("bias", [P, 1], F32)
        gates = sb("gates", [P, 2], F32)
        tg = sb("tg", [P, 4], F32)
        si = sb("si", [P, NT], F32)
        stats = sb("stats", [P, NT, 6], F32)
        mv = sb("mv", [P, NT, 2], F32)
        stats2 = sb("stats2", [P, NT, 6], F32)
        mv2 = sb("mv2", [P, NT, 2], F32)
        veps = sb("veps", [P, 2, NT], F32)
        rstd = sb("rstd", [P, 2, NT], F32)
        mhalf = sb("mhalf", [P, NT], F32)
        lnA = sb("lnA", [P, NT], F32)
        lnB = sb("lnB", [P, NT], F32)
        xs2 = sb("xs2", [P, NT], F32)
        xm2 = sb("xm2", [P, NT], F32)
        mix_room = sb("mix_room", [P, 3, 2, H], F32)
        sig, xmix, xn = (mix_room[:, k] for k in range(3))
        ROWS_AHEAD = 4
        xhl = room_a[:, :].bitcast(F16).rearrange("p (b a h) -> p b a h", b=ROWS_AHEAD, a=2)
        gws = xn[0:E, 0, :]
        gw_hl = xn[0:E, 1, :].bitcast(F16).rearrange("e (a h) -> e a h", a=2)
        gwT = sb("gwT", [P, HC, 2 * E], F16)
        lgh = sb("lgh", [P, NT, E], F32)
        lg = sb("lg", [P, NT, E], F32)
        top8 = sb("top8", [P, NT, 8], F32)
        r_gt = sb("r_gt", [P, NT, E], F32)
        r_eq = sb("r_eq", [P, NT, E], F32)
        r_run = sb("r_run", [P, NT, E], F32)
        r_keep = sb("r_keep", [P, NT, E], F32)
        r_need = sb("r_need", [P, NT], F32)
        r_exp = sb("r_exp", [P, NT, E], F32)
        r_sum = sb("r_sum", [P, NT], F32)
        tick = sb("tick", [P, 1], F32)
        pool_tick = sb("pool_tick", [P, 1], F32)
        cw = sb("cw", [P, NT, E], F32)
        shared_w = sb("shared_w", [P, 1], F32)
        zeros = sb("zeros", [P, ROW // 4], F32)
        sc_rows, sd_rows = NE * G_GU, NE * IC
        sc_room = wgu[0:sc_rows, 1].rearrange("p a c n -> p (a c n)")
        sc_all = sc_room[:, 0:2 * GU].bitcast(F32)
        sc_top = sc_room[:, 2 * GU:4 * GU].bitcast(F32)
        sc_h = sc_room[:, 4 * GU:6 * GU].rearrange("p (a n) -> p a n", a=2)
        sd_room = wdn[0:sd_rows, 1].rearrange("p a c n -> p (a c n)")
        sd_all = sd_room[:, 0:2 * H].bitcast(F32)
        sd_top = sd_room[:, 2 * H:4 * H].bitcast(F32)
        sd_h = sd_room[:, 4 * H:6 * H].rearrange("p (a n) -> p a n", a=2)

        onehot = room_a[:, :].bitcast(F16).rearrange("p (b q i) -> p b q i", b=2, i=NT)
        values = mix_room[:, 1:3].rearrange("p k b h -> p (k b h)").bitcast(F16).rearrange("p (k e i) -> p k e i", e=E, i=NT)
        place = sig.rearrange("p b h -> p (b h)").bitcast(F16).rearrange("p (q i) -> p q i", i=NT)
        slot_room = wdn[:, 1].rearrange("p a c n -> p (a c n)")
        slot_ge = slot_room[:, 0:SLOTS * E].rearrange("p (s e) -> p s e", e=E)
        slot_nt = slot_room[:, SLOTS * E:2 * SLOTS * E].rearrange("p (s e) -> p s e", e=E)
        xg = room_b[:, 0:2 * ROW].rearrange("p (b n) -> p b n", b=2)
        at = [2 * ROW]

        def in_room_b(shape, dt):
            n = math.prod(shape[1:])
            piece = room_b[:, at[0]:at[0] + n]
            at[0] += n
            assert at[0] <= B * S
            if dt != F32:
                piece = piece.bitcast(dt)
            return piece.rearrange("p (a b) -> p a b", a=shape[1]) if len(shape) == 3 else piece
        tok = in_room_b([P, E * KMAX + 1], I32)
        tokf = in_room_b([P, E * KMAX], F32)
        tok0 = in_room_b([P, E * KMAX], F32)
        wide = wgu[:, 1].rearrange("p a c n -> p (a c n)")[:, 0:8 * E * NT].bitcast(F32)
        total = wide[:, 0:E * NT].rearrange("p (e i) -> p e i", i=NT)
        rank = wide[:, E * NT:2 * E * NT].rearrange("p (e i) -> p e i", i=NT)
        ranki = wide[:, 2 * E * NT:3 * E * NT].bitcast(I32)
        rankm = wide[:, 3 * E * NT:4 * E * NT].bitcast(I32)
        rank_k = sb("rank_k", [P, E * NT], F16)
        rank_q = sb("rank_q", [P, E, NT], F16)
        tri = sb("tri", [P, P], F16)
        ones16 = sb("ones16", [P, P], F16)
        sel16 = sb("sel16", [P, NT * E], F16)
        token1 = sb("token1", [P, NT], F16)
        dump_row = sb("dump_row", [P, 1], F32)
        tiles_i = sb("tiles_i", [P, E], I32)
        tiles_f = sb("tiles_f", [P, E], F32)
        cum_f = sb("cum_f", [P, E], F32)
        odd_i = sb("odd_i", [P, 1], I32)
        odd_f = sb("odd_f", [P, 1], F32)
        first_f = sb("first_f", [P, E], F32)
        TILES_ROOM = 2 * KMAX
        first_tiles_i = sb("first_tiles_i", [P, E], I32)
        pairs_i = sb("pairs_i", [P, 1], I32)
        slot_f = sb("slot_f", [P, 2, SLOTS], F32)
        slot_i = sb("slot_i", [P, 2, SLOTS], I32)
        iota_s = sb("iota_s", [P, SLOTS], F32)
        idx_g = sb("idx_g", [P, 2], I32)
        idx_s = sb("idx_s", [P, 2], I32)
        wslot = sb("wslot", [P, 2, E], F32)
        xTs = xn.rearrange("p b h -> p (b h)").bitcast(F16).rearrange("p (b n) -> p b n", b=2)
        y_sb = xmix

        gu_ps = psum("gu_ps", [P, 4, 512], F32)
        bank = [gu_ps[:, i, :] for i in range(4)] + [psum(f"bank{i}", [P, 512], F32)[:, :] for i in range(4, 8)]
        g_ps, u_ps = bank[0:2], bank[2:4]
        at_ps = bank[4][:, 0:IC * P].bitcast(F16)
        y_ps = bank[5:7]
        sj_ps = bank[0:4]
        tp_ps = bank[4:6]
        lg_ps = bank[6]
        si_ps = bank[7]
        rt_ps = bank[7]
        xT_ps = bank[7].bitcast(F16)

        ld_const = sem("ld_const")
        ld_x = [sem(f"ld_x{b}") for b in range(B)]
        ld_ctx = [sem(f"ld_ctx{b}") for b in range(B)]
        ld_sc = sem("ld_sc")
        st_sc = sem("st_sc")
        ld_w = [sem("ld_w0"), sem("ld_w1")]
        pool_const = sem("pool_const")
        ctxT_ps_ready = sem("ctxT_ps_ready")
        ctxT_ready = sem("ctxT_ready")
        wj_ready = sem("wj_ready")
        si_ps_ready = sem("si_ps_ready")
        si_ready = sem("si_ready")
        sj_ready = sem("sj_ready")
        tg_ready = sem("tg_ready")
        ve_ready = [sem("ve_ready0"), sem("ve_ready1")]
        rstd_ready = [sem("rstd_ready0"), sem("rstd_ready1")]
        sig_ready = sem("sig_ready")
        x1_ready = sem("x1_ready")
        xn_ready = sem("xn_ready")
        xs2_ready = sem("xs2_ready")
        xh_ready = sem("xh_ready")
        xl_ready = sem("xl_ready")
        xT_ps_ready = sem("xT_ps_ready")
        xT_ready = sem("xT_ready")
        gw_ready = sem("gw_ready")
        gwT_ps_ready = sem("gwT_ps_ready")
        gwT_ready = sem("gwT_ready")
        lg_ps_ready = sem("lg_ps_ready")
        lgh_ready = sem("lgh_ready")
        lsub_ready = sem("lsub_ready")
        exp_ready = sem("exp_ready")
        half_ready = sem("half_ready")
        dqg_ready = sem("dqg_ready")
        dq_ready = sem("dq_ready")
        gu_done = sem("gu_done")
        sg_done = sem("sg_done")
        act_done = sem("act_done")
        ah_done = sem("ah_done")
        al_done = sem("al_done")
        at_done = sem("at_done")
        aT_done = sem("aT_done")
        y_done = sem("y_done")
        acc_done = sem("acc_done")
        vs = sem("vector_step")
        dqs = sem("dequant_step")
        st_out = sem("st_out")
        st_rows = [sem(f"st_rows{k}") for k in range(ROWS_AHEAD)]
        st_cw = sem("st_cw")
        rows_zero = sem("rows_zero")
        sel_ready = sem("sel_ready")
        count_ready = sem("count_ready")
        onehot_ready = sem("onehot_ready")
        place_ready = sem("place_ready")
        ln_ready = sem("ln_ready")
        xmix_ready = sem("xmix_ready")
        list_ready = sem("list_ready")
        route_ready = sem("route_ready")
        cw_ready = sem("cw_ready")
        xg_ld = [sem("xg_ld0"), sem("xg_ld1")]
        tx_done = sem("tx_done")
        xTs_done = sem("xTs_done")
        wslot_done = sem("wslot_done")
        yev_done = sem("yev_done")
        added = sem("added")
        idx_g_ready = sem("idx_g_ready")
        idx_s_ready = sem("idx_s_ready")

        block = ctx.enter_context(nc.Block())

        def tile_order_h(ap):
            return ap.rearrange("p (c f r) -> p r f c", f=2, r=GR)

        def natural_h(ap):
            return ap.rearrange("p (r f c) -> p r f c", f=2, c=HC)

        def tile_order_i(ap):
            return ap.rearrange("p (t j r) -> p t r j", j=NIB, r=RG)

        def natural_i(ap):
            return ap.rearrange("p (t r j) -> p t r j", j=NIB, r=RG)

        def load_expert(sp, gp, dp, buf, n):
            for f in range(2):
                rows = slice(f * GR, (f + 1) * GR)
                sp.dma_start(gu_raw[rows, buf, :].bitcast(U16)[:, 0:2 * GU - f], gp.bitcast(U16)[:, f:])\
                    .then_inc(ld_w[buf], 16)
                for hl in range(2):
                    sp.dma_start(gu_sc[rows, buf, hl, :],
                                 gu_s_dram[hl, n].unsqueeze(1).broadcast_to([G_GU, RG, GU])).then_inc(ld_w[buf], 16)
            for t in range(IC):
                sp.dma_start(dn_raw[:, buf, t, :],
                             dp[t * RG:(t + 1) * RG].unsqueeze(0).broadcast_to([NIB, RG, H])).then_inc(ld_w[buf], 16)
            for hl in range(2):
                sp.dma_start(dn_sc[:, buf, hl, :, :],
                             dn_s_dram[hl, n].unsqueeze(0).broadcast_to([P, IC, H])).then_inc(ld_w[buf], 16)
        LOADS = 2 * (1 + 2) + IC + 2

        def loaded(n):
            return 16 * LOADS * (n // 2 + 1)

        POOL_CONST = 14
        SPLIT_STEPS = 10

        @block.sync
        def _(sp):
            for k in range(2):
                sp.dma_start(wij[:, k:k + 1], xattn_w.rearrange("o (k p) -> k p o", p=P)[k],
                             allow_slow_non_contiguous=True).then_inc(ld_const, 16)
            sp.dma_start(bias[:, :], xattn_b.unsqueeze(0).broadcast_to([P, 1])).then_inc(ld_const, 16)
            sp.dma_start(gates[:, 0:1], g_xattn.unsqueeze(0).broadcast_to([P, 1])).then_inc(ld_const, 16)
            sp.dma_start(gates[:, 1:2], g_ffn.unsqueeze(0).broadcast_to([P, 1])).then_inc(ld_const, 16)
            sp.dma_start(gws[:, :], gate_w).then_inc(ld_const, 16)
            sp.dma_start(sc_all[0:G_GU, :], sh_gu_scales).then_inc(ld_sc, 16)
            sp.dma_start(sc_all[G_GU:NE * G_GU, :], gu_scales.rearrange("e g n -> (e g) n")).then_inc(ld_sc, 16)
            sp.dma_start(sd_all[0:IC, :], sh_dn_scales).then_inc(ld_sc, 16)
            sp.dma_start(sd_all[IC:NE * IC, :], dn_scales.rearrange("e g n -> (e g) n")).then_inc(ld_sc, 16)
            for b in range(B):
                sp.dma_start(ctxs[:, b * TB:(b + 1) * TB, :], ctx_t[b]).then_inc(ld_ctx[b], 16)
            for b in range(B):
                sp.dma_start(X[:, b * TB:(b + 1) * TB, :], x_t[b]).then_inc(ld_x[b], 16)
            sp.wait_ge(vs, SPLIT_STEPS)
            for hl in range(2):
                sp.dma_start(gu_s_dram[hl].rearrange("e g n -> (e g) n"), sc_h[:, hl, :]).then_inc(st_sc, 16)
                sp.dma_start(dn_s_dram[hl].rearrange("e g n -> (e g) n"), sd_h[:, hl, :]).then_inc(st_sc, 16)
            sp.wait_ge(st_sc, 64)
            load_expert(sp, sh_gu_packed, sh_dn_packed, 0, 0)
            load_expert(sp, gu_packed[0], dn_packed[0], 1, 1)
            for i in range(NT):
                sp.wait_ge(xh_ready, i + 1)
                sp.wait_ge(xl_ready, i + 1)
                sp.dma_start(rows_dram[i * P:(i + 1) * P, 0:H],
                             xhl[:, i % ROWS_AHEAD].rearrange("p a h -> p (a h)").bitcast(F32))\
                    .then_inc(st_rows[i % ROWS_AHEAD], 16)
            sp.wait_ge(pool_const, POOL_CONST)
            sp.dma_start(rows_dram[T:T + P, :].rearrange("p (a n) -> p a n", a=4),
                         zeros[:, :].unsqueeze(1).broadcast_to([P, 4, ROW // 4])).then_inc(rows_zero, 16)
            sp.dma_start(out[T:T + P, :].rearrange("p (a n) -> p a n", a=4),
                         zeros[:, 0:H // 4].unsqueeze(1).broadcast_to([P, 4, H // 4])).then_inc(st_out, 16)
            sp.wait_ge(cw_ready, 1)
            sp.dma_start(rows_dram[0:T, H:ROW].rearrange("(i p) e -> p i e", p=P), cw[:, :, :])\
                .then_inc(st_cw, 16)
            sp.wait_ge(dq_ready, 1)
            load_expert(sp, gu_packed[1], dn_packed[1], 0, 2)
            for b in range(B):
                sp.wait_ge(acc_done, (b + 1) * TB)
                sp.dma_start(out_t[b], X[:, b * TB:(b + 1) * TB, :]).then_inc(st_out, 16)
            sp.wait_ge(dq_ready, 2)
            load_expert(sp, gu_packed[2], dn_packed[2], 1, 3)
            with sp.Fori(1, E // 2 - 1) as h:
                sp.wait_ge(dq_ready, 2 * h + 1)
                load_expert(sp, gu_packed[2 * h + 1], dn_packed[2 * h + 1], 0, 2 * h + 2)
                sp.wait_ge(dq_ready, 2 * h + 2)
                load_expert(sp, gu_packed[2 * h + 2], dn_packed[2 * h + 2], 1, 2 * h + 3)
            sp.wait_ge(dq_ready, E - 1)
            load_expert(sp, gu_packed[E - 1], dn_packed[E - 1], 0, E)
            sp.wait_ge(st_out, 16 * (B + 1))

        @block.gpsimd
        def _(pool):
            nc.gpsimd.memset(ones[:, :], 1.0).then_inc(pool_const, 1)
            nc.gpsimd.memset(id32[:, :], 0.0).then_inc(pool_const, 1)
            nc.gpsimd.memset(id16[:, :], 0.0).then_inc(pool_const, 1)
            nc.gpsimd.memset(mhalf[:, :], -0.5).then_inc(pool_const, 1)
            nc.gpsimd.iota(dn_shift[:, :], [[0, 1]], base=P - 1, channel_multiplier=-1).then_inc(pool_const, 1)
            nc.gpsimd.memset(zeros[:, :], 0.0).then_inc(pool_const, 1)
            nc.gpsimd.memset(tri[:, :], 1.0).then_inc(pool_const, 1)
            nc.gpsimd.memset(ones16[:, :], 1.0).then_inc(pool_const, 1)
            for dst, pattern, base, mult in ((token1[:, :], [[P, NT]], 1, 1), (dump_row[:, :], [[0, 1]], DUMP + 1, 1),
                                             (iota_s[:, :], [[1, SLOTS]], 0, 0)):
                nc.gpsimd.iota(dst, pattern, base=base, channel_multiplier=mult,
                               allow_small_or_imprecise_dtypes=True).then_inc(pool_const, 1)
            pool.wait_ge(pool_const, 11)
            nc.gpsimd.affine_select(out=tri[:, :], in_=tri[:, :], compare_op=ALU.is_gt, fill=0.0, base=0,
                                    pattern=[[1, P]], channel_multiplier=-1).then_inc(pool_const, 1)
            for ident in (id32, id16):
                nc.gpsimd.affine_select(out=ident[:, :], in_=ident[:, :], compare_op=ALU.not_equal, fill=1.0,
                                        base=0, pattern=[[-1, P]], channel_multiplier=1).then_inc(pool_const, 1)

            def inverse_std(k, b):
                pool.wait_ge(ve_ready[k], b + 1)
                cols = slice(b * TB, (b + 1) * TB)
                nc.gpsimd.tensor_tensor(rstd[:, k, cols], veps[:, k, cols], mhalf[:, cols], ALU.pow).then_inc(rstd_ready[k], 1)

            def scaled_x(b):
                pool.wait_ge(ln_ready, b + 1)
                for i in range(b * TB, (b + 1) * TB):
                    if i >= 2:
                        pool.wait_ge(x1_ready, i - 1)
                    nc.gpsimd.tensor_scalar(xmix[:, i % 2, :], X[:, i, :], lnA[:, i:i + 1], lnB[:, i:i + 1],
                                            ALU.mult, ALU.add).then_inc(xmix_ready, 1)

            def normalised(b):
                pool.wait_ge(rstd_ready[1], b + 1)
                at = slice(b * TB, (b + 1) * TB)
                nc.gpsimd.tensor_scalar(xs2[:, at], rstd[:, 1, at], X_SCALE, None, ALU.mult).then_inc(xs2_ready, 1)
                nc.gpsimd.tensor_scalar(xm2[:, at], rstd[:, 1, at], -X_SCALE, None, ALU.mult).then_inc(xs2_ready, 1)
                pool.wait_ge(xs2_ready, 3 * b + 2)
                nc.gpsimd.tensor_tensor(xm2[:, at], xm2[:, at], mv2[:, at, 0], ALU.mult).then_inc(xs2_ready, 1)
                pool.wait_ge(xs2_ready, 3 * b + 3)
                for i in range(b * TB, (b + 1) * TB):
                    if i >= 2:
                        pool.wait_ge(xh_ready, i - 1)
                        pool.wait_ge(xl_ready, i - 1)
                    else:
                        pool.wait_ge(gwT_ready, 2)
                    nc.gpsimd.tensor_scalar(xn[:, i % 2, :], X[:, i, :], xs2[:, i:i + 1], xm2[:, i:i + 1],
                                            ALU.mult, ALU.add).then_inc(xn_ready, 1)
            inverse_std(0, 0)
            inverse_std(0, 1)
            scaled_x(0)
            inverse_std(0, 2)
            scaled_x(1)
            inverse_std(0, 3)
            for b in range(B - 1):
                inverse_std(1, b)
                normalised(b)
                if b + 2 < B:
                    scaled_x(b + 2)
            inverse_std(1, B - 1)
            normalised(B - 1)

            pool.wait_ge(x1_ready, NT)
            nc.gpsimd.iota(place, [[1, P], [0, NT]], base=1, channel_multiplier=0,
                           allow_small_or_imprecise_dtypes=True).then_inc(place_ready, 1)

            pool.wait_ge(rows_zero, 16)
            for k in range(ROWS_AHEAD):
                pool.wait_ge(st_rows[k], 16 * (NT // ROWS_AHEAD))
            pool.wait_ge(st_cw, 16)
            pool.wait_ge(route_ready, 1)
            inner = pool.value_load(pairs_i[0:1, 0:1], min_val=E // 2 - 2, max_val=SLOTS // 2 - 2)

            def hold_wait():
                nc.gpsimd.tensor_tensor(pool_tick[:, :], ones[:, 0:1], ones[:, 0:1], ALU.mult)

            def gather(s, b):
                col = pool.value_load(slot_i[0:1, 1, bass.ds(s, 1)], min_val=0, max_val=E * KMAX)
                if not isinstance(s, int) or s >= 2:
                    pool.wait_ge(tx_done, s - 1)
                    pool.wait_ge(wslot_done, s - 1)
                pool.wait_ge(route_ready, 1)
                nc.gpsimd.tensor_copy(idx_g[:, b:b + 1], tok[:, bass.ds(col, 1)]).then_inc(idx_g_ready, 1)
                pool.wait_ge(idx_g_ready, s + 1)
                hold_wait()
                nc.gpsimd.indirect_dma_start(xg[:, b, :], None, rows_dram[:, :],
                                             bass.IndirectOffsetOnAxis(idx_g[:, b:b + 1], 0)).then_inc(xg_ld[b], 16)

            def add(s, b):
                col = pool.value_load(slot_i[0:1, 1, bass.ds(s, 1)], min_val=0, max_val=E * KMAX)
                pool.wait_ge(yev_done, s + 1)
                if not isinstance(s, int) or s >= 1:
                    pool.wait_ge(added, 16 * s)
                pool.wait_ge(st_out, 16 * (B + 1))
                nc.gpsimd.tensor_copy(idx_s[:, b:b + 1], tok[:, bass.ds(col, 1)]).then_inc(idx_s_ready, 1)
                pool.wait_ge(idx_s_ready, s + 1)
                hold_wait()
                nc.gpsimd.indirect_dma_start(out[:, :], bass.IndirectOffsetOnAxis(idx_s[:, b:b + 1], 0), y_sb[:, b, :],
                                             None, compute_op=ALU.add).then_inc(added, 16)
            for s in range(4):
                gather(s, s % 2)
            for b in range(2):
                gather(b + 4, b)
                add(b, b)
            with pool.Fori(2, inner + 1) as j:
                for b in range(2):
                    gather(2 * j + b + 2, b)
                    add(2 * j + b - 2, b)
            for k in range(-4, 0):
                add(2 * inner + 4 + k, k % 2)
            pool.wait_ge(added, 32 * inner + 64)

        @block.scalar
        def _(a):
            a.wait_ge(ld_const, 16 * 6)
            nc.scalar.activation(tg[:, 0:2], gates[:, :], ACT.Tanh).then_inc(tg_ready, 1)
            for b in range(B):
                a.wait_ge(ctxT_ps_ready, b + 1)
                nc.scalar.activation(ctxT[:, b, :], tp_ps[b % 2][:, :], ACT.Copy).then_inc(ctxT_ready, 1)
            for hl in range(2):
                a.wait_ge(gwT_ps_ready, hl + 1)
                nc.scalar.activation(gwT[:, :, hl * E:(hl + 1) * E],
                                     tp_ps[hl][:, 0:HC * E // 2].bitcast(F16).rearrange("p (c e) -> p c e", e=E),
                                     ACT.Copy).then_inc(gwT_ready, 1)
            a.wait_ge(si_ready, 1)

            def scores(b):
                a.wait_ge(sj_ready, b + 1)
                for i in range(b * TB, (b + 1) * TB):
                    if i >= 2:
                        a.wait_ge(x1_ready, i - 1)
                    nc.scalar.activation(sig[:, i % 2, :], sj_ps[b][:, :], ACT.Sigmoid,
                                         bias=si[:, i:i + 1]).then_inc(sig_ready, 1)
                    if b >= 2 and i % TB in (1, 2):
                        copy_xT(i - 2 * TB + 1)

            def split_x(i):
                a.wait_ge(xn_ready, i + 1)
                if i >= ROWS_AHEAD:
                    a.wait_ge(xT_ps_ready, i - ROWS_AHEAD + 1)
                    a.wait_ge(st_rows[i % ROWS_AHEAD], 16 * (i // ROWS_AHEAD))
                nc.scalar.activation(tile_order_h(xhl[:, i % ROWS_AHEAD, 0, :]), natural_h(xn[:, i % 2, :]),
                                     ACT.Copy).then_inc(xh_ready, 1)

            def copy_xT(i):
                a.wait_ge(xT_ps_ready, i + 1)
                nc.scalar.activation(xT[:, i].rearrange("p a c t -> p (a c t)"), tp_ps[i % 2][:, :].bitcast(F16),
                                     ACT.Copy).then_inc(xT_ready, 1)

            def halves(b):
                for i in range(b * TB, (b + 1) * TB):
                    split_x(i)
                    if i % TB >= 2 or b == B - 1:
                        copy_xT(i - 2)
            for b in range(B):
                scores(b)
                if b:
                    halves(b - 1)
            halves(B - 1)
            copy_xT(NT - 2)
            copy_xT(NT - 1)

            def activate(s, b):
                gate(s, b)
                high_halves(s, b)

            def gate(s, b):
                a.wait_ge(gu_done, s + 1)
                if not isinstance(s, int) or s >= 2:
                    a.wait_ge(act_done, s - 1)
                nc.scalar.activation(sg[:, b, :], g_ps[b][:, 0:I], ACT.Silu,
                                     scale=1.0 / (X_SCALE * W_SCALE)).then_inc(sg_done, 1)

            def high_halves(s, b):
                a.wait_ge(act_done, s + 1)
                if not isinstance(s, int) or s >= 2:
                    a.wait_ge(at_done, s - 1)
                nc.scalar.activation(tile_order_i(acth[:, b, 0, :]), natural_i(act[:, b, :]), ACT.Copy).then_inc(ah_done, 1)

            def copy_aT(s, b):
                a.wait_ge(at_done, s + 1)
                if not isinstance(s, int) or s >= 2:
                    a.wait_ge(y_done, s - 1)
                nc.scalar.activation(aT[:, b].rearrange("p a c t -> p (a c t)"), at_ps, ACT.Copy).then_inc(aT_done, 1)

            def take_rows(r, b):
                a.wait_ge(xg_ld[b], 8 * (r - b) + 16)
                if not isinstance(r, int) or r >= 2:
                    a.wait_ge(act_done, NT + r - 1)
                nc.scalar.activation(wslot[:, b, :], xg[:, b, H:ROW], ACT.Copy).then_inc(wslot_done, 1)
                a.wait_ge(tx_done, r + 1)
                if not isinstance(r, int) or r >= 2:
                    a.wait_ge(gu_done, NT + r - 1)
                nc.scalar.activation(xTs[:, b, :], xT_ps, ACT.Copy).then_inc(xTs_done, 1)

            def take_y(r, b):
                a.wait_ge(y_done, NT + r + 1)
                if not isinstance(r, int) or r >= 2:
                    a.wait_ge(added, 16 * (r - 1))
                nc.scalar.activation(y_sb[:, b, :], y_ps[b][:, :], ACT.Copy, scale=1.0 / W_SCALE).then_inc(yev_done, 1)

            for i in range(2):
                gate(i, i)
            for i in range(2):
                high_halves(i, i)
            a.wait_ge(lg_ps_ready, NT)
            nc.scalar.activation(lgh[:, :, :], lg_ps[:, :].rearrange("p (t k e) -> p t k e", k=2, e=E)[:, :, 1, :],
                                 ACT.Copy).then_inc(lgh_ready, 1)
            copy_aT(0, 0)
            a.wait_ge(lsub_ready, 1)
            nc.scalar.activation(r_exp[:, :, :], lg[:, :, :], ACT.Exp).then_inc(exp_ready, 1)
            for i in range(2, NT):
                copy_aT(i - 1, (i - 1) % 2)
                if i == NT - 1:
                    take_rows(0, 0)
                activate(i, i % 2)
            a.wait_ge(route_ready, 1)
            inner = a.value_load(pairs_i[0:1, 0:1], min_val=E // 2 - 2, max_val=SLOTS // 2 - 2)

            def slot(r, b, rows=True):
                copy_aT(r + (NT - 1), 1 - b)
                if rows:
                    take_rows(r + 1, 1 - b)
                activate(NT + r, b)
                if not isinstance(r, int) or r >= 1:
                    take_y(r - 1, 1 - b)
            for r in range(4):
                slot(r, r % 2)
            with a.Fori(2, inner + 1) as j:
                slot(2 * j, 0)
                slot(2 * j + 1, 1)
            slot(2 * inner + 2, 0)
            slot(2 * inner + 3, 1, rows=False)
            copy_aT(2 * inner + 3 + NT, 1)
            take_y(2 * inner + 3, 1)

        @block.vector
        def _(v):
            count = [0]

            def step(ins, wait=True):
                count[0] += 1
                ins.then_inc(vs, 1)
                if wait:
                    v.wait_ge(vs, count[0])

            v.wait_ge(ld_const, 16 * 6)
            v.wait_ge(pool_const, POOL_CONST)
            nc.vector.tensor_scalar(wj_all[:, :], ones[:, :], wij[:, 1:2], None, ALU.mult).then_inc(wj_ready, 1)
            v.wait_ge(ld_sc, 64)
            both = []
            for whole, top, half in ((sc_all, sc_top, sc_h), (sd_all, sd_top, sd_h)):
                rest = half[:, :, :].rearrange("p a n -> p (a n)").bitcast(F32)
                both.append((whole, top, half, rest))
            for k, (whole, top, half, rest) in enumerate(both):
                step(nc.vector.tensor_scalar(top[:, :], whole[:, :], SPLITTER, None, ALU.mult), wait=k == 1)
            for k, (whole, top, half, rest) in enumerate(both):
                step(nc.vector.tensor_tensor(rest, top[:, :], whole[:, :], ALU.subtract), wait=k == 1)
            for k, (whole, top, half, rest) in enumerate(both):
                step(nc.vector.tensor_tensor(top[:, :], top[:, :], rest, ALU.subtract), wait=k == 1)
            for k, (whole, top, half, rest) in enumerate(both):
                step(nc.vector.tensor_scalar(half[:, 0, :], top[:, :], W_SCALE, None, ALU.mult), wait=k == 1)
            for k, (whole, top, half, rest) in enumerate(both):
                step(nc.vector.scalar_tensor_tensor(half[:, 1, :], whole[:, :], W_SCALE, half[:, 0, :], ALU.mult,
                                                    ALU.subtract), wait=k == 1)
            assert count[0] == SPLIT_STEPS
            step(nc.vector.tensor_scalar(dn_shift[:, :], dn_shift[:, :], 4, 2, ALU.logical_shift_right,
                                         ALU.logical_shift_left), wait=False)
            step(nc.vector.tensor_scalar(gws[:, :], gws[:, :], R_SCALE, None, ALU.mult))
            step(nc.vector.tensor_copy(tile_order_h(gw_hl[:, 0, :]), natural_h(gws[:, :])))
            nc.vector.tensor_tensor(tile_order_h(gw_hl[:, 1, :]), natural_h(gws[:, :]), tile_order_h(gw_hl[:, 0, :]),
                                    ALU.subtract).then_inc(gw_ready, 1)
            v.wait_ge(tg_ready, 1)
            step(nc.vector.tensor_scalar(tg[:, 2:3], tg[:, 0:1], P_ASEM, None, ALU.mult), wait=False)
            step(nc.vector.tensor_scalar(tg[:, 3:4], tg[:, 0:1], 1.0 - P_ASEM, None, ALU.mult))

            def norm_stats(st, agg, k, b):
                tiles = range(b * TB, (b + 1) * TB)
                for i in tiles:
                    step(nc.vector.bn_stats(st[:, i, :], X[:, i, :]), wait=i == tiles[-1])
                for i in tiles:
                    step(nc.vector.bn_aggr(agg[:, i, :], st[:, i, :]), wait=i == tiles[-1])
                nc.vector.tensor_scalar(veps[:, k, b * TB:(b + 1) * TB], agg[:, b * TB:(b + 1) * TB, 1], LN_EPS, None,
                                        ALU.add).then_inc(ve_ready[k], 1)

            def x_factors(b):
                v.wait_ge(rstd_ready[0], b + 1)
                at = slice(b * TB, (b + 1) * TB)
                step(nc.vector.tensor_scalar(lnA[:, at], rstd[:, 0, at], tg[:, 3:4], None, ALU.mult))
                step(nc.vector.tensor_tensor(lnB[:, at], lnA[:, at], mv[:, at, 0], ALU.mult))
                step(nc.vector.tensor_scalar(lnB[:, at], lnB[:, at], -1.0, None, ALU.mult), wait=False)
                nc.vector.tensor_scalar(lnA[:, at], lnA[:, at], 1.0, None, ALU.add).then_inc(ln_ready, 1)

            def attend(b):
                for i in range(b * TB, (b + 1) * TB):
                    v.wait_ge(xmix_ready, i + 1)
                    v.wait_ge(sig_ready, i + 1)
                    nc.vector.scalar_tensor_tensor(X[:, i, :], sig[:, i % 2, :], tg[:, 2:3], xmix[:, i % 2, :],
                                                   ALU.mult, ALU.add).then_inc(x1_ready, 1)
                v.wait_ge(x1_ready, (b + 1) * TB)
                norm_stats(stats2, mv2, 1, b)

            def low_halves_x(b):
                for i in range(b * TB, (b + 1) * TB):
                    low_x(i)

            def low_x(i):
                v.wait_ge(xn_ready, i + 1)
                v.wait_ge(xh_ready, i + 1)
                nc.vector.tensor_tensor(tile_order_h(xhl[:, i % ROWS_AHEAD, 1, :]), natural_h(xn[:, i % 2, :]),
                                        tile_order_h(xhl[:, i % ROWS_AHEAD, 0, :]), ALU.subtract).then_inc(xl_ready, 1)

            step(nc.vector.tensor_scalar(shared_w[:, :], tg[:, 1:2], 1.0 / (X_SCALE * W_SCALE), None, ALU.mult))

            def route():
                v.wait_ge(lgh_ready, 1)
                step(nc.vector.tensor_tensor(lg[:, :, :], lg_ps[:, :].rearrange("p (t k e) -> p t k e", k=2, e=E)[:, :, 0, :],
                                             lgh[:, :, :], ALU.add))
                step(nc.vector.tensor_scalar(lg[:, :, :], lg[:, :, :], 1.0 / (X_SCALE * R_SCALE), None, ALU.mult))
                for i in range(NT):
                    step(nc.vector.max(top8[:, i, :], lg[:, i, :]), wait=(i == NT - 1))
                kth = top8[:, :, TOP_K - 1:TOP_K].broadcast_to([P, NT, E])
                step(nc.vector.tensor_tensor(r_gt[:, :, :], lg[:, :, :], kth, ALU.is_gt), wait=False)
                step(nc.vector.tensor_tensor(r_eq[:, :, :], lg[:, :, :], kth, ALU.is_equal))
                nc.vector.tensor_tensor(lg[:, :, :], lg[:, :, :], top8[:, :, 0:1].broadcast_to([P, NT, E]),
                                        ALU.subtract).then_inc(lsub_ready, 1)
                step(nc.vector.tensor_reduce(r_need[:, :], r_gt[:, :, :], AX, ALU.add), wait=False)
                step(nc.vector.memset(r_keep[:, :, :], 1.0))
                step(nc.vector.memset(r_keep[:, :, 0:1], 0.0))
                step(nc.vector.tensor_tensor_scan(r_run[:, :, :].rearrange("p t e -> p (t e)"),
                                                  r_keep[:, :, :].rearrange("p t e -> p (t e)"),
                                                  r_eq[:, :, :].rearrange("p t e -> p (t e)"), 0.0, ALU.mult, ALU.add))
                step(nc.vector.tensor_tensor(r_run[:, :, :], r_run[:, :, :],
                                             r_need[:, :].unsqueeze(2).broadcast_to([P, NT, E]), ALU.add))
                step(nc.vector.tensor_scalar(r_run[:, :, :], r_run[:, :, :], float(TOP_K), None, ALU.is_le))
                step(nc.vector.tensor_tensor(r_eq[:, :, :], r_eq[:, :, :], r_run[:, :, :], ALU.mult))
                step(nc.vector.tensor_tensor(r_gt[:, :, :], r_gt[:, :, :], r_eq[:, :, :], ALU.add))
                nc.vector.tensor_copy(sel16[:, :], r_gt[:, :, :].rearrange("p t e -> p (t e)")).then_inc(sel_ready, 1)
                v.wait_ge(exp_ready, 1)
                step(nc.vector.tensor_tensor(r_exp[:, :, :], r_exp[:, :, :], r_gt[:, :, :], ALU.mult))
                step(nc.vector.tensor_reduce(r_sum[:, :], r_exp[:, :, :], AX, ALU.add))
                step(nc.vector.reciprocal(r_sum[:, :], r_sum[:, :]))
                step(nc.vector.tensor_scalar(r_sum[:, :], r_sum[:, :], shared_w[:, 0:1], None, ALU.mult))
                nc.vector.tensor_tensor(cw[:, :, :], r_exp[:, :, :], r_sum[:, :].unsqueeze(2).broadcast_to([P, NT, E]),
                                        ALU.mult).then_inc(cw_ready, 1)

            def ranks():
                v.wait_ge(count_ready, 1)
                step(nc.vector.tensor_copy(total, rt_ps[:, NT * E:2 * NT * E].rearrange("p (i e) -> p e i", e=E)))
                step(nc.vector.tensor_tensor_scan(r_run[:, :, :].rearrange("p e i -> p (e i)"),
                                                  r_keep[:, :, :].rearrange("p e i -> p (e i)"),
                                                  total.rearrange("p e i -> p (e i)"), 0.0, ALU.mult, ALU.add))
                step(nc.vector.tensor_tensor(rank, r_run[:, :, :], total, ALU.subtract))
                step(nc.vector.tensor_tensor(ranki.rearrange("p (e i) -> p e i", i=NT), rank,
                                             rt_ps[:, 0:NT * E].rearrange("p (i e) -> p e i", e=E), ALU.add))
                step(nc.vector.tensor_scalar(rankm, ranki, 7, None, ALU.logical_shift_right))
                step(nc.vector.tensor_copy(rank_k[:, :], rankm))
                step(nc.vector.tensor_scalar(ranki, ranki, P - 1, None, ALU.bitwise_and))
                step(nc.vector.scalar_tensor_tensor(rank_q[:, :, :], ranki.rearrange("p (e i) -> p e i", i=NT), 1.0,
                                                    r_gt[:, :, :].rearrange("p i e -> p e i"), ALU.add, ALU.mult), wait=False)

            def token_values():
                for k in range(KMAX):
                    step(nc.vector.tensor_scalar(values[:, k].rearrange("p e i -> p (e i)"), rank_k[:, :], float(k), None,
                                                 ALU.is_equal), wait=k == KMAX - 1)
                cells = values.rearrange("p k e i -> p (k e) i")
                step(nc.vector.tensor_tensor(cells, cells, token1[:, :].unsqueeze(1).broadcast_to([P, KMAX * E, NT]),
                                             ALU.mult))

            def tables():
                step(nc.vector.tensor_scalar(tiles_i[:, :], r_run[:, :, NT - 1], float(P - 1), None, ALU.add))
                step(nc.vector.tensor_scalar(tiles_i[:, :], tiles_i[:, :], 7, None, ALU.logical_shift_right))
                step(nc.vector.tensor_scalar(tiles_f[:, :], tiles_i[:, :], 1.0, None, ALU.max))
                step(nc.vector.tensor_tensor_scan(cum_f[:, :], ones[:, 0:E], tiles_f[:, :], 0.0, ALU.mult, ALU.add))
                step(nc.vector.tensor_copy(odd_i[:, :], cum_f[:, E - 1:E]))
                step(nc.vector.tensor_scalar(odd_i[:, :], odd_i[:, :], 1, None, ALU.bitwise_and))
                step(nc.vector.tensor_copy(odd_f[:, :], odd_i[:, :]))
                for t in (tiles_f, cum_f):
                    step(nc.vector.tensor_tensor(t[:, E - 1:E], t[:, E - 1:E], odd_f[:, :], ALU.add))
                step(nc.vector.tensor_tensor(first_f[:, :], cum_f[:, :], tiles_f[:, :], ALU.subtract), wait=False)
                step(nc.vector.tensor_scalar(pairs_i[:, :], cum_f[:, E - 1:E], 0.5, -2.0, ALU.mult, ALU.add))
                step(nc.vector.scalar_tensor_tensor(first_tiles_i[:, :], first_f[:, :], float(TILES_ROOM), tiles_f[:, :],
                                                    ALU.mult, ALU.add))

            def slot_tables(part):
                by_expert = [P, SLOTS, E]
                if part == 0:
                    step(nc.vector.tensor_tensor(slot_ge, iota_s[:, :].unsqueeze(2).broadcast_to(by_expert),
                                                 cum_f[:, :].unsqueeze(1).broadcast_to(by_expert), ALU.is_ge))
                elif part == 1:
                    step(nc.vector.tensor_tensor(slot_nt, slot_ge, tiles_f[:, :].unsqueeze(1).broadcast_to(by_expert),
                                                 ALU.mult))
                elif part == 2:
                    step(nc.vector.tensor_reduce(slot_f[:, 0, :], slot_ge, AX, ALU.add))
                    step(nc.vector.tensor_copy(slot_i[:, 0, :], slot_f[:, 0, :]), wait=False)
                else:
                    step(nc.vector.tensor_reduce(slot_f[:, 1, :], slot_nt, AX, ALU.add))
                    step(nc.vector.scalar_tensor_tensor(slot_f[:, 1, :], slot_f[:, 0, :], float(KMAX), slot_f[:, 1, :],
                                                        ALU.mult, ALU.subtract))
                    step(nc.vector.tensor_tensor(slot_i[:, 1, :], slot_f[:, 1, :], iota_s[:, :], ALU.add))

            def lists():
                v.wait_ge(list_ready, E)
                ps = rt_ps[:, 0:E * KMAX]
                step(nc.vector.tensor_scalar(tok0, ps, 0.0, None, ALU.is_equal))
                step(nc.vector.scalar_tensor_tensor(tokf, tok0, dump_row[:, 0:1], ps, ALU.mult, ALU.add))
                step(nc.vector.tensor_scalar(tok[:, 0:E * KMAX], tokf, -1.0, None, ALU.add))
                step(nc.vector.tensor_scalar(tok[:, E * KMAX:], dump_row[:, :], -1.0, None, ALU.add))
                nc.vector.memset(tick[:, 0:1], 0.0).then_inc(route_ready, 1)

            PARTS = HC
            COLS = IC * H // PARTS
            G_STEPS, D_STEPS = 7, 5
            N_STEPS = 1 + PARTS * (G_STEPS + D_STEPS)

            def end_of(n):
                return (n + 1) * N_STEPS + (0 if isinstance(n, int) and n == E else 1)

            def dequant(n, buf, g, d, fill=None, free=None):
                if d is None:
                    done = n * N_STEPS + 1
                elif g is None:
                    done = end_of(n) - D_STEPS
                else:
                    done = n * N_STEPS + 1 + G_STEPS + d * (G_STEPS + D_STEPS)
                at = [0]

                def link(ins, wait=True):
                    at[0] += 1
                    ins.then_inc(dqs, 1)
                    if wait:
                        v.wait_ge(dqs, done + at[0])
                v.wait_ge(dqs, done)
                if g is not None:
                    c = HC - 1 - g
                    link(nc.vector.tensor_scalar(dq_sign[:, :], gu_half[:, :], 0x8000, None, ALU.bitwise_and), wait=False)
                    link(nc.vector.tensor_scalar(dq_mag[:, :], gu_half[:, :], 3, 0x0E00, ALU.logical_shift_right,
                                                 ALU.bitwise_and), wait=d is None)
                if fill:
                    fill()
                if d is not None:
                    cols = slice(d * COLS, (d + 1) * COLS) if isinstance(d, int) else bass.ds(d * COLS, COLS)
                    raw = dn_raw[:, buf].rearrange("p t n -> p (t n)")[:, cols]
                    link(nc.vector.tensor_scalar(dn_bits[:, 0:COLS], raw, dn_shift[:, 0:1], None,
                                                 ALU.logical_shift_left))
                if g is not None:
                    link(nc.vector.tensor_tensor(dq_mag[:, :], dq_mag[:, :], dq_sign[:, :], ALU.bitwise_or),
                         wait=d is None)
                if d is not None:
                    link(nc.vector.tensor_scalar(dn_bits[:, 0:COLS], dn_bits[:, 0:COLS], 3, 0x8E000000 - (1 << 32),
                                                 ALU.arith_shift_right, ALU.bitwise_and))
                if g is not None:
                    link(nc.vector.tensor_scalar(dq_code[:, :], dq_mag[:, :].bitcast(F16), CODE_SCALE, None, ALU.mult),
                         wait=d is None)
                if d is not None:
                    link(nc.vector.tensor_scalar(dn_code[:, 0:COLS],
                                                 dn_bits[:, 0:COLS].bitcast(F16).rearrange("p (n f) -> p n f", f=2)[:, :, 1],
                                                 CODE_SCALE, None, ALU.mult))
                if g is not None:
                    link(nc.vector.tensor_scalar(gu_half[:, :], gu_half[:, :], 4, None, ALU.logical_shift_left), wait=False)
                    for hl in range(2):
                        link(nc.vector.tensor_tensor(wgu[:, buf, hl, c, :], dq_code[:, :], gu_sc[:, buf, hl, :], ALU.mult),
                             wait=False)
                if d is not None:
                    if free is not None:
                        v.wait_ge(y_done, free)
                    for hl in range(2):
                        link(nc.vector.tensor_tensor(wdn[:, buf, hl].rearrange("p t n -> p (t n)")[:, cols],
                                                     dn_code[:, 0:COLS],
                                                     dn_sc[:, buf, hl].rearrange("p t n -> p (t n)")[:, cols], ALU.mult),
                             wait=False)
                assert at[0] == (g is not None) * G_STEPS + (d is not None) * D_STEPS

            def take_words(n, buf):
                if not isinstance(n, int) or n:
                    v.wait_ge(dqs, n * N_STEPS + 1 - D_STEPS - 1)
                v.wait_ge(ld_w[buf], loaded(n))
                words = gu_raw[:, buf, :].bitcast(U16).rearrange("p (n f) -> p n f", f=2)
                nc.vector.tensor_copy(gu_half[:, :], words[:, :, 0]).then_inc(dqs, 1)

            def end_gate_up(n, buf):
                v.wait_ge(dqs, n * N_STEPS + 1 + G_STEPS + (PARTS - 1) * (G_STEPS + D_STEPS))
                nc.vector.memset(tick[:, 0:1], 0.0).then_inc(dqg_ready, 1)
                if not isinstance(n, int) or n < E:
                    take_words(n + 1, 1 - buf)

            def end_dequant(n):
                v.wait_ge(dqs, end_of(n))
                nc.vector.memset(tick[:, 0:1], 0.0).then_inc(dq_ready, 1)

            def first_stats(b):
                v.wait_ge(ld_x[b], 16)
                norm_stats(stats, mv, 0, b)

            first_stats(0)
            first_stats(1)
            v.wait_ge(si_ps_ready, 1)
            nc.vector.tensor_scalar(si[:, :], si_ps[:, 0:NT], bias[:, 0:1], None, ALU.add).then_inc(si_ready, 1)
            x_factors(0)
            first_stats(2)
            attend(0)
            x_factors(1)
            first_stats(3)
            attend(1)
            x_factors(2)
            x_factors(3)
            take_words(0, 0)
            for k in range(PARTS):
                if k == 2:
                    attend(2)
                dequant(0, 0, k, k - 1 if k else None, fill=lambda: low_x(2 * k))
                low_x(2 * k + 1)
            end_gate_up(0, 0)
            attend(3)
            low_halves_x(2)
            low_halves_x(B - 1)
            dequant(0, 0, None, PARTS - 1)
            end_dequant(0)

            def activations(s, b, weight):
                if not isinstance(s, int) or s >= 2:
                    v.wait_ge(at_done, s - 1)
                v.wait_ge(sg_done, s + 1)
                nc.vector.scalar_tensor_tensor(act[:, b, :], gu_ps[:, 2 + b, 0:I], weight, sg[:, b, :], ALU.mult,
                                               ALU.mult).then_inc(act_done, 1)

            def low_halves(s, b):
                v.wait_ge(ah_done, s + 1)
                nc.vector.tensor_tensor(tile_order_i(acth[:, b, 1, :]), natural_i(act[:, b, :]),
                                        tile_order_i(acth[:, b, 0, :]), ALU.subtract).then_inc(al_done, 1)

            def add_y(i):
                v.wait_ge(y_done, i + 1)
                nc.vector.scalar_tensor_tensor(X[:, i, :], y_ps[i % 2][:, :], 1.0 / W_SCALE, X[:, i, :], ALU.mult,
                                               ALU.add).then_inc(acc_done, 1)

            def first_weights(k):
                if k == 0:
                    dequant(1, 1, 0, None)
                elif k < PARTS:
                    dequant(1, 1, k, k - 1)
                else:
                    end_gate_up(1, 1)
                    dequant(1, 1, None, PARTS - 1)
                    end_dequant(1)
                    dequant(2, 0, 0, None)

            def mark(e):
                if e >= 2:
                    v.wait_ge(list_ready, e - 1)
                else:
                    v.wait_ge(place_ready, 1)
                    for k in range(ROWS_AHEAD):
                        v.wait_ge(st_rows[k], 16 * (NT // ROWS_AHEAD))
                nc.vector.tensor_tensor(onehot[:, e % 2], rank_q[:, e, :].unsqueeze(1).broadcast_to([P, P, NT]), place,
                                        ALU.is_equal).then_inc(onehot_ready, 1)

            def after_shared_slot(i):
                if i == 2:
                    ranks()
                    tables()
                if i == 3:
                    token_values()
                if 4 <= i < 4 + E // 2:
                    mark(2 * (i - 4))
                    mark(2 * (i - 4) + 1)
                if 4 <= i < 8:
                    slot_tables(i - 4)
                if i == 8:
                    first_weights(0)
                if i == 10:
                    first_weights(1)
                if i == NT - 4:
                    lists()
                if i >= NT - 3:
                    first_weights(i - (NT - 3) + 2)

            for i in range(2):
                activations(i, i, shared_w[:, 0:1])
            for i in range(2):
                low_halves(i, i)
            route()
            add_y(0)
            for i in range(2, NT):
                activations(i, i % 2, shared_w[:, 0:1])
                low_halves(i, i % 2)
                add_y(i - 1)
                after_shared_slot(i)

            def head(r, e):
                b = r % 2
                v.wait_ge(wslot_done, r + 1)
                activations(r + NT, b, wslot[:, b, bass.ds(e, 1)])

            def routed_slot(r, e):
                head(r, e)
                low_halves(r + NT, r % 2)

            def expert(e, buf_next, add_last=False):
                at_e = bass.ds(e, 1)
                both = v.value_load(first_tiles_i[0:1, at_e], min_val=1, max_val=(SLOTS + 1) * TILES_ROOM - 1)
                first, tiles = both // TILES_ROOM, both % TILES_ROOM
                n = e + 2
                if buf_next is None:
                    routed_slot(first, e)
                    with v.If(tiles > 1):
                        with v.Fori(1, tiles) as k:
                            routed_slot(first + k, e)
                    return
                head(first, e)
                dequant(n, buf_next, 1, 0, fill=lambda: low_halves(first + NT, first % 2), free=first + NT)
                if add_last:
                    add_y(NT - 1)
                for k in range(1, PARTS - 1):
                    with v.If(tiles > k):
                        head(first + k, e)
                        dequant(n, buf_next, k + 1, k, fill=lambda: low_halves(first + k + NT, (first + k) % 2))
                    with v.Else():
                        dequant(n, buf_next, k + 1, k)
                end_gate_up(n, buf_next)
                with v.If(tiles > PARTS - 1):
                    routed_slot(first + PARTS - 1, e)
                dequant(n, buf_next, None, PARTS - 1)
                end_dequant(n)
                with v.If(tiles > PARTS):
                    with v.Fori(PARTS, tiles) as k:
                        routed_slot(first + k, e)
                if not isinstance(e, int) or e < E - 2:
                    dequant(n + 1, 1 - buf_next, 0, None)

            v.wait_ge(route_ready, 1)
            expert(0, 0, add_last=True)
            expert(1, 1)
            with v.Fori(1, E // 2 - 1) as h:
                expert(2 * h, 0)
                expert(2 * h + 1, 1)
            expert(E - 2, 0)
            expert(E - 1, None)

        @block.tensor
        def _(pe):
            pe.wait_ge(pool_const, POOL_CONST)
            for b in range(B):
                pe.wait_ge(ld_ctx[b], 16)
                if b >= 2:
                    pe.wait_ge(ctxT_ready, b - 1)
                for t in range(TB):
                    mm = nc.tensor.transpose(tp_ps[b % 2][:, t * P:(t + 1) * P], ctxs[:, b * TB + t, :], id32[:, :])
                mm.then_inc(ctxT_ps_ready, 1)
            pe.wait_ge(wj_ready, 1)
            pe.wait_ge(ld_const, 16 * 6)
            for b in range(B):
                pe.wait_ge(ctxT_ready, b + 1)
                nc.tensor.matmul(sj_ps[b][:, :], wj_all[:, :], ctxT[:, b, :], start=True, stop=True).then_inc(sj_ready, 1)
                for t in range(TB):
                    i = b * TB + t
                    mm = nc.tensor.matmul(si_ps[:, i:i + 1], ctxT[:, b, t * P:(t + 1) * P], wij[:, 0:1], start=True,
                                          stop=True)
            mm.then_inc(si_ps_ready, 1)
            pe.wait_ge(gw_ready, 1)
            for hl in range(2):
                dst = tp_ps[hl][:, 0:HC * E // 2].bitcast(F16)
                for c in range(HC):
                    mm = nc.tensor.transpose(dst[:, c * E:(c + 1) * E], gw_hl[:, hl, c * P:(c + 1) * P], id16[0:E, 0:E])
                mm.then_inc(gwT_ps_ready, 1)
            pe.wait_ge(gwT_ready, 2)

            def transpose_x(i):
                pe.wait_ge(xl_ready, i + 1)
                if i >= 2:
                    pe.wait_ge(xT_ready, i - 1)
                dst = tp_ps[i % 2][:, :].bitcast(F16)
                for k in range(2 * HC):
                    mm = nc.tensor.transpose(dst[:, k * P:(k + 1) * P], xhl[:, i % ROWS_AHEAD].rearrange("p a h -> p (a h)")[:, k * P:(k + 1) * P],
                                             id16[:, :])
                mm.then_inc(xT_ps_ready, 1)

            def route(i):
                pe.wait_ge(xT_ready, i + 1)
                for k in range(2 * HC):
                    mm = nc.tensor.matmul(lg_ps[:, i * 2 * E:(i + 1) * 2 * E], xT[:, i, k // HC, k % HC, :], gwT[:, k % HC, :],
                                          start=(k == 0), stop=(k == 2 * HC - 1))
                mm.then_inc(lg_ps_ready, 1)
            def gate_up(s, b, x, w, half):
                if half == 0 and (not isinstance(s, int) or s >= 2):
                    pe.wait_ge(act_done, s - 1)
                for c in range(half * HC // 2, (half + 1) * HC // 2):
                    for xp, wp in ((0, 0), (0, 1), (1, 0)):
                        for ps, col in ((g_ps, 0), (u_ps, I)):
                            mm = nc.tensor.matmul(ps[b][:, 0:I], x(xp * HC + c), wgu[:, w, wp, c, col:col + I],
                                                  start=(c == 0 and xp == 0 and wp == 0),
                                                  stop=(c == HC - 1 and xp == 1), skip_group_check=True)
                if half == 1:
                    mm.then_inc(gu_done, 1)

            def transpose_act(s, b):
                pe.wait_ge(ah_done, s + 1)
                pe.wait_ge(al_done, s + 1)
                if not isinstance(s, int) or s >= 1:
                    pe.wait_ge(aT_done, s)
                for hl in range(2):
                    for t in range(IC):
                        k = hl * IC + t
                        mm = nc.tensor.transpose(at_ps[:, k * P:(k + 1) * P], acth[:, b, hl, t * P:(t + 1) * P], id16[:, :])
                mm.then_inc(at_done, 1)

            def down(s, b, w):
                pe.wait_ge(aT_done, s + 1)
                if isinstance(s, int) and 2 <= s < NT + 2:
                    pe.wait_ge(acc_done, s - 1)
                elif not isinstance(s, int) or s >= 2:
                    pe.wait_ge(yev_done, s - 1 - NT)
                n = 0
                for t in range(IC):
                    for ap, wp in ((0, 0), (0, 1), (1, 0)):
                        mm = nc.tensor.matmul(y_ps[b][:, :], aT[:, b, ap, t, :], wdn[:, w, wp, t, :],
                                              start=(n == 0), stop=(n == 3 * IC - 1))
                        n += 1
                mm.then_inc(y_done, 1)

            def transpose_rows(r, b):
                pe.wait_ge(xg_ld[b], 8 * (r - b) + 16)
                if not isinstance(r, int) or r >= 1:
                    pe.wait_ge(xTs_done, r)
                halves = xg[:, b, 0:H].bitcast(F16)
                for k in range(2 * HC):
                    mm = nc.tensor.transpose(xT_ps[:, k * P:(k + 1) * P], halves[:, k * P:(k + 1) * P], id16[:, :])
                mm.then_inc(tx_done, 1)

            def count():
                pe.wait_ge(sel_ready, 1)
                nc.tensor.matmul(rt_ps[:, 0:NT * E], tri[:, :], sel16[:, :], start=True, stop=True)
                nc.tensor.matmul(rt_ps[:, NT * E:2 * NT * E], ones16[:, :], sel16[:, :], start=True,
                                 stop=True).then_inc(count_ready, 1)

            def list_tokens(e):
                pe.wait_ge(onehot_ready, e + 1)
                for i in range(NT):
                    mm = nc.tensor.matmul(rt_ps[:, e * KMAX:(e + 1) * KMAX], onehot[:, e % 2, :, i], values[:, :, e, i],
                                          start=(i == 0), stop=(i == NT - 1))
                mm.then_inc(list_ready, 1)

            def shared_gate_up(i, half):
                gate_up(i, i % 2, lambda k: xT[:, i, k // HC, k % HC, :], 0, half)

            for i in range(NT):
                transpose_x(i)
                if i == 2 * TB - 1:
                    pe.wait_ge(dqg_ready, 1)
                    for k in range(2):
                        pe.wait_ge(sig_ready, (k + 3) * TB)
                        for half in range(2):
                            shared_gate_up(k, half)
                if i:
                    route(i - 1)
            route(NT - 1)
            transpose_act(0, 0)
            pe.wait_ge(dq_ready, 1)

            for i in range(2, NT):
                b = i % 2
                shared_gate_up(i, 0)
                if i == 2:
                    down(0, 0, 0)
                transpose_act(i - 1, 1 - b)
                if i == 2:
                    count()
                if i == NT - 1:
                    pe.wait_ge(route_ready, 1)
                    transpose_rows(0, 0)
                shared_gate_up(i, 1)
                down(i - 1, 1 - b, 0)
                if 5 <= i < 5 + E // 2:
                    list_tokens(2 * (i - 5))
                    list_tokens(2 * (i - 5) + 1)

            inner = pe.value_load(pairs_i[0:1, 0:1], min_val=E // 2 - 2, max_val=SLOTS // 2 - 2)

            def slot(r, b, rows=True):
                s = NT + r
                e = pe.value_load(slot_i[0:1, 0, bass.ds(r, 1)], min_val=0, max_val=E - 1)
                w = (e + 1) % 2

                def x(k):
                    return xTs[:, b, k * P:(k + 1) * P]
                pe.wait_ge(dqg_ready, e + 2)
                pe.wait_ge(xTs_done, r + 1)
                gate_up(s, b, x, w, 0)
                transpose_act(s - 1, 1 - b)
                if rows:
                    transpose_rows(r + 1, 1 - b)
                gate_up(s, b, x, w, 1)
                if isinstance(r, int) and r == 0:
                    w_prev = 0
                else:
                    e_prev = pe.value_load(slot_i[0:1, 0, bass.ds(r - 1, 1)], min_val=0, max_val=E - 1)
                    w_prev = (e_prev + 1) % 2
                    pe.wait_ge(dq_ready, e_prev + 2)
                down(s - 1, 1 - b, w_prev)
            slot(0, 0)
            slot(1, 1)
            with pe.Fori(1, inner + 1) as j:
                slot(2 * j, 0)
                slot(2 * j + 1, 1)
            slot(2 * inner + 2, 0)
            slot(2 * inner + 3, 1, rows=False)
            transpose_act(2 * inner + 3 + NT, 1)
            e_last = pe.value_load(slot_i[0:1, 0, bass.ds(2 * inner + 3, 1)], min_val=0, max_val=E - 1)
            down(2 * inner + 3 + NT, 1, (e_last + 1) % 2)


_NAMES = ["x", "ctx_512", "g_xattn", "g_ffn", "L0_xattn_W", "L0_xattn_b", "L0_ffn_gate_w", "L0_ffn_gate_up_packed",
          "L0_ffn_gate_up_scales", "L0_ffn_down_packed", "L0_ffn_down_scales", "L0_ffn_shared_gate_up_packed",
          "L0_ffn_shared_gate_up_scales", "L0_ffn_shared_down_packed", "L0_ffn_shared_down_scales"]


def kernel(**inputs):
    import numpy as np
    import concourse.bacc as bacc
    from concourse.bass_utils import run_bass_kernel_spmd

    nc = bacc.Bacc("TRN2", target_bir_lowering=False, num_devices=1)
    arrays, args = {}, []
    for name in _NAMES:
        a = np.ascontiguousarray(inputs[name])
        arrays[f"in_{name}"] = a
        args.append(nc.dram_tensor(f"in_{name}", a.shape, mybir.dt.from_np(a.dtype), kind="ExternalInput").ap())
    b, n, h = inputs["x"].shape
    out = nc.dram_tensor("out", (b * n + P, h), F32, kind="ExternalOutput").ap()
    gated_xattn_moe(nc, *args, out)
    r = run_bass_kernel_spmd(nc, [arrays], core_ids=[0])
    return r.results[0]["out"][:b * n].reshape(b, n, h)
```
